# Optimizing a Trainium2 kernel written in Bass

```python
import numpy as np
import jax
import jax.numpy as jnp

def _softmax(x, axis=-1):
    return jax.nn.softmax(x, axis=axis)

def _gelu(x):
    return jax.nn.gelu(x, approximate=True)

def _silu(x):
    return jax.nn.silu(x)

def _sigmoid(x):
    return jax.nn.sigmoid(x)

def _layernorm(x, axis=-1, eps=1e-05):
    m = jnp.mean(x, axis=axis, keepdims=True)
    v = jnp.var(x, axis=axis, keepdims=True)
    return (x - m) / jnp.sqrt(v + eps)

def _scatter_add(tgt, idx, src, axis=0):
    return tgt.at[idx].add(src)

def _segment_sum(src, seg, n):
    return jax.ops.segment_sum(src, seg, n)
kernel_name = 'mk_perceiver_d2_seqx_r8_745933'

def setup_inputs(seed: int=0):
    np.random.seed(seed)
    _w = jnp.asarray

    def _rec_inputs():
        import jax
        import jax.numpy as jnp
        _rk = jax.random.key(seed)
        x = 7.22e-05 + 1 * jax.random.normal(jax.random.fold_in(_rk, 1), (4, 128, 128), jnp.float32)
        _lenS = 128 - jax.random.randint(jax.random.fold_in(_rk, 7), (4,), 0, max(1, 128 // 4) + 1, jnp.int32)
        _lenS2 = 2048 - jax.random.randint(jax.random.fold_in(_rk, 8), (4,), 0, max(1, 2048 // 4) + 1, jnp.int32)
        _ctx_1024P = jax.random.normal(jax.random.fold_in(_rk, 11), (4, 16, 128), jnp.float32)
        _ctx_1024c = jax.random.dirichlet(jax.random.fold_in(_rk, 511), 0.3 * jnp.ones((16,), jnp.float32), (4, 2048))
        _ctx_1024t = jnp.einsum('bsk,bkd->bsd', _ctx_1024c, _ctx_1024P)
        _ctx_1024t = _ctx_1024t * jax.lax.rsqrt(jnp.mean(jnp.square(_ctx_1024t)) + 1e-12) * 0.953939
        ctx_1024 = 4.13588e-05 + 0.999923 * (_ctx_1024t + 0.3 * jax.random.normal(jax.random.fold_in(_rk, 611), (4, 2048, 128), jnp.float32))
        _validS = jnp.arange(128)[None, :] < _lenS[:, None]
        _validS2 = jnp.arange(2048)[None, :] < _lenS2[:, None]
        _causal = jnp.tril(jnp.ones((128, 128), dtype=bool))
        mask_1xSxS2_ff0 = jnp.where(jnp.ones((1, 128, 2048), dtype=bool), 0.0, -1000000000.0).astype(jnp.float32)
        mask_Bx1x1xS2_fk0 = jnp.where(jnp.broadcast_to(_validS2[:, None, None, :], (4, 1, 1, 2048)), 0.0, 1.0).astype(jnp.float32)
        return (x, ctx_1024, mask_1xSxS2_ff0, mask_Bx1x1xS2_fk0)
    x, ctx_1024, mask_1xSxS2_ff0, mask_Bx1x1xS2_fk0 = _rec_inputs()

    def _L0_xattn_setup():
        import jax, jax.numpy as jnp
        import numpy as np
        INP_SIZE = 128
        D_MODEL = 128
        B, S = (4, 256)
        key = jax.random.key(seed)
        ks = jax.random.split(key, 9)
        q = jax.random.normal(ks[0], (B, S, INP_SIZE), dtype=jnp.float32)
        k = jax.random.normal(ks[1], (B, S, INP_SIZE), dtype=jnp.float32)
        v = jax.random.normal(ks[2], (B, S, INP_SIZE), dtype=jnp.float32)
        mask = jnp.zeros((1, S, S), dtype=jnp.float32)
        kernel_q = jax.random.normal(ks[3], (INP_SIZE, D_MODEL), dtype=jnp.float32) * 0.05
        kernel_k = jax.random.normal(ks[4], (INP_SIZE, D_MODEL), dtype=jnp.float32) * 0.05
        kernel_v = jax.random.normal(ks[5], (INP_SIZE, D_MODEL), dtype=jnp.float32) * 0.05
        bias_q = jax.random.normal(ks[6], (D_MODEL,), dtype=jnp.float32) * 0.05
        bias_k = jax.random.normal(ks[7], (D_MODEL,), dtype=jnp.float32) * 0.05
        bias_v = jax.random.normal(ks[8], (D_MODEL,), dtype=jnp.float32) * 0.05
        return {'q': q, 'k': k, 'v': v, 'mask': mask, 'kernel_q': kernel_q, 'bias_q': bias_q, 'kernel_k': kernel_k, 'bias_k': bias_k, 'kernel_v': kernel_v, 'bias_v': bias_v}
    _L0_xattn_all = _L0_xattn_setup()
    _L0_xattn_in = {k: v for k, v in _L0_xattn_all.items() if k in ('kernel_q', 'bias_q', 'kernel_k', 'bias_k', 'kernel_v', 'bias_v')}
    del _L0_xattn_all

    def _L0_attn_setup():
        import jax, jax.numpy as jnp
        import numpy as np
        EPS = 0.0001

        def mp_normalize(x, axis):
            red = int(np.prod([x.shape[a] for a in axis])) if isinstance(axis, (list, tuple)) else x.shape[axis]
            w = jnp.sqrt(jnp.sum(jnp.square(x.astype(jnp.float32)), axis=axis, keepdims=True))
            w = EPS + w / np.sqrt(red)
            return x / w.astype(x.dtype)

        def mp_linear(x, w, gain):
            fan_in = w.shape[1]
            wn = mp_normalize(w.astype(jnp.float32), axis=(1,)) * (gain / np.sqrt(fan_in))
            return jnp.einsum('bse,oe->bso', x, wn.astype(x.dtype))

        def attention(query, gain, w_q, w_k, w_v, w_o, num_heads=16, attn_balance=0.5):
            B, S, E = query.shape
            hd = E // num_heads
            res = query
            q = mp_linear(query, w_q, gain).reshape(B, S, num_heads, hd).transpose(0, 2, 1, 3)
            k = mp_linear(query, w_k, gain).reshape(B, S, num_heads, hd).transpose(0, 2, 1, 3)
            v = mp_linear(query, w_v, gain).reshape(B, S, num_heads, hd).transpose(0, 2, 1, 3)
            q = mp_normalize(q, axis=(3,))
            k = mp_normalize(k, axis=(3,))
            scores = jnp.einsum('bnsh,bnsk->bnhk', q, k / np.sqrt(S))
            attn = jax.nn.softmax(scores, axis=3)
            o = jnp.einsum('bnhk,bnsk->bnsh', attn, v)
            o = o.transpose(0, 2, 1, 3).reshape(B, S, E)
            out = mp_linear(o, w_o, gain)
            t = attn_balance
            return (res * (1.0 - t) + out * t) / np.sqrt((1 - t) ** 2 + t ** 2)
        key = jax.random.key(seed)
        ks = jax.random.split(key, 5)
        B, S, E = (4, 512, 128)
        return {'query': jax.random.normal(ks[0], (B, S, E), dtype=jnp.float32), 'gain': jnp.float32(1.0), 'w_q': jax.random.normal(ks[1], (E, E), dtype=jnp.float32), 'w_k': jax.random.normal(ks[2], (E, E), dtype=jnp.float32), 'w_v': jax.random.normal(ks[3], (E, E), dtype=jnp.float32), 'w_o': jax.random.normal(ks[4], (E, E), dtype=jnp.float32)}
    _L0_attn_all = _L0_attn_setup()
    _L0_attn_in = {k: v for k, v in _L0_attn_all.items() if k in ('gain', 'w_q', 'w_k', 'w_v', 'w_o')}
    del _L0_attn_all

    def _L0_ffn_setup():
        import jax, jax.numpy as jnp
        import numpy as np
        DIM = 128

        def _reference_tuple_inner(x, W_r, W_k, W_v, mu_r, mu_k):
            B, T, C = x.shape
            x_prev = jnp.concatenate([jnp.zeros((B, 1, C), x.dtype), x[:, :-1, :]], axis=1)
            xr = mu_r * x + (1.0 - mu_r) * x_prev
            xk = mu_k * x + (1.0 - mu_k) * x_prev
            r = jax.nn.sigmoid(jnp.einsum('btc,dc->btd', xr, W_r))
            k = jnp.einsum('btc,dc->btd', xk, W_k)
            k_act = jnp.square(jax.nn.relu(k))
            out = r * jnp.einsum('btc,dc->btd', k_act, W_v)
            new_state = x[:, -1, :]
            return (out, new_state)
        key = jax.random.key(seed)
        ks = jax.random.split(key, 6)
        B, T, C = (8, 256, DIM)
        x = jax.random.normal(ks[0], (B, T, C), dtype=jnp.float32)
        s = 1.0 / np.sqrt(C)
        W_r = jax.random.uniform(ks[1], (C, C), jnp.float32, -s, s)
        W_k = jax.random.uniform(ks[2], (C, C), jnp.float32, -s, s)
        W_v = jax.random.uniform(ks[3], (C, C), jnp.float32, -s, s)
        mu_r = jax.random.uniform(ks[4], (C,), jnp.float32)
        mu_k = jax.random.uniform(ks[5], (C,), jnp.float32)
        return {'x': x, 'W_r': W_r, 'W_k': W_k, 'W_v': W_v, 'mu_r': mu_r, 'mu_k': mu_k}
    _L0_ffn_all = _L0_ffn_setup()
    _L0_ffn_in = {k: v for k, v in _L0_ffn_all.items() if k in ('W_r', 'W_k', 'W_v', 'mu_r', 'mu_k')}
    del _L0_ffn_all

    def _L1_xattn_setup():
        import jax, jax.numpy as jnp
        import numpy as np
        B, S, D, H = (2, 256, 128, 16)
        DH = D // H

        def _split_heads(x):
            b, s, _ = x.shape
            return x.reshape(b, s, H, DH).transpose(0, 2, 1, 3)
        key = jax.random.key(seed)
        ks = jax.random.split(key, 8)
        scale = 0.02
        return {'query': jax.random.normal(ks[0], (B, S, D), jnp.float32), 'key': jax.random.normal(ks[1], (B, S, D), jnp.float32), 'value': jax.random.normal(ks[2], (B, S, D), jnp.float32), 'mask': jax.random.randint(ks[3], (B, 1, 1, S), 0, 2).astype(jnp.float32), 'Wq': jax.random.normal(ks[4], (D, D), jnp.float32) * scale, 'bq': jnp.zeros((D,), jnp.float32), 'Wk': jax.random.normal(ks[5], (D, D), jnp.float32) * scale, 'bk': jnp.zeros((D,), jnp.float32), 'Wv': jax.random.normal(ks[6], (D, D), jnp.float32) * scale, 'bv': jnp.zeros((D,), jnp.float32), 'Wo': jax.random.normal(ks[7], (D, D), jnp.float32) * scale, 'bo': jnp.zeros((D,), jnp.float32)}
    _L1_xattn_all = _L1_xattn_setup()
    _L1_xattn_in = {k: v for k, v in _L1_xattn_all.items() if k in ('Wq', 'bq', 'Wk', 'bk', 'Wv', 'bv', 'Wo', 'bo')}
    del _L1_xattn_all

    def _L1_attn_setup():
        import jax, jax.numpy as jnp
        import numpy as np
        import math
        B, S, D, H = (1, 256, 128, 16)
        HD = D // H
        SCALE = 1.0 / math.sqrt(HD)
        ENT = 0.5
        DECAY = 0.1
        SUP = 0.3
        EPS = 1e-05

        def _heads(x):
            b, s, _ = x.shape
            return x.reshape(b, s, H, HD).transpose(0, 2, 1, 3)
        key = jax.random.key(seed)
        ks = jax.random.split(key, 24)

        def w(k, shape, s=0.02):
            return jax.random.normal(k, shape, dtype=jnp.float32) * s
        return {'hidden_states': jax.random.normal(ks[0], (B, S, D), dtype=jnp.float32), 'Wq': w(ks[1], (D, D)), 'bq': jnp.zeros((D,), jnp.float32), 'Wk': w(ks[2], (D, D)), 'bk': jnp.zeros((D,), jnp.float32), 'Wv': w(ks[3], (D, D)), 'bv': jnp.zeros((D,), jnp.float32), 'Wo': w(ks[4], (D, D)), 'bo': jnp.zeros((D,), jnp.float32), 'Weq': w(ks[5], (D, D), 0.002), 'beq': jnp.zeros((D,), jnp.float32), 'Wek': w(ks[6], (D, D), 0.002), 'bek': jnp.zeros((D,), jnp.float32), 'amp_w': w(ks[7], (H, D)), 'amp_b': jnp.zeros((H,), jnp.float32), 'ph_w': w(ks[8], (H, D)), 'ph_b': jnp.zeros((H,), jnp.float32), 'mix_w': w(ks[9], (H, HD, HD)), 'mix_b': jnp.zeros((H, HD), jnp.float32), 'ln_g': jnp.ones((D,), jnp.float32), 'ln_b': jnp.zeros((D,), jnp.float32)}
    _L1_attn_all = _L1_attn_setup()
    _L1_attn_in = {k: v for k, v in _L1_attn_all.items() if k in ('Wq', 'bq', 'Wk', 'bk', 'Wv', 'bv', 'Wo', 'bo', 'Weq', 'beq', 'Wek', 'bek', 'amp_w', 'amp_b', 'ph_w', 'ph_b', 'mix_w', 'mix_b', 'ln_g', 'ln_b')}
    del _L1_attn_all

    def _L1_ffn_setup():
        import jax, jax.numpy as jnp
        import numpy as np
        B, S, D, F, E = (8, 128, 128, 512, 8)
        EPS = 1e-05
        key = jax.random.key(seed)
        ks = jax.random.split(key, 4)
        s = 0.02
        return {'input_features': jax.random.normal(ks[0], (B, S, D), jnp.float32), 'centroids': jax.random.normal(ks[1], (E, D), jnp.float32) * 0.1, 'ln_g': jnp.ones((E, D), jnp.float32), 'ln_b': jnp.zeros((E, D), jnp.float32), 'w1': jax.random.normal(ks[2], (E, D, F), jnp.float32) * s, 'b1': jnp.zeros((E, F), jnp.float32), 'w2': jax.random.normal(ks[3], (E, F, D), jnp.float32) * s, 'b2': jnp.zeros((E, D), jnp.float32)}
    _L1_ffn_all = _L1_ffn_setup()
    _L1_ffn_in = {k: v for k, v in _L1_ffn_all.items() if k in ('centroids', 'ln_g', 'ln_b', 'w1', 'b1', 'w2', 'b2')}
    del _L1_ffn_all
    return {'x': x, 'ctx_1024': ctx_1024, 'mask_1xSxS2_ff0': mask_1xSxS2_ff0, 'mask_Bx1x1xS2_fk0': mask_Bx1x1xS2_fk0, 'L0_xattn_kernel_q': _L0_xattn_in['kernel_q'], 'L0_xattn_bias_q': _L0_xattn_in['bias_q'], 'L0_xattn_kernel_k': _L0_xattn_in['kernel_k'], 'L0_xattn_bias_k': _L0_xattn_in['bias_k'], 'L0_xattn_kernel_v': _L0_xattn_in['kernel_v'], 'L0_xattn_bias_v': _L0_xattn_in['bias_v'], 'L0_attn_gain': _L0_attn_in['gain'], 'L0_attn_w_q': _L0_attn_in['w_q'], 'L0_attn_w_k': _L0_attn_in['w_k'], 'L0_attn_w_v': _L0_attn_in['w_v'], 'L0_attn_w_o': _L0_attn_in['w_o'], 'L0_ffn_W_r': _L0_ffn_in['W_r'], 'L0_ffn_W_k': _L0_ffn_in['W_k'], 'L0_ffn_W_v': _L0_ffn_in['W_v'], 'L0_ffn_mu_r': _L0_ffn_in['mu_r'], 'L0_ffn_mu_k': _L0_ffn_in['mu_k'], 'L1_xattn_Wq': _L1_xattn_in['Wq'], 'L1_xattn_bq': _L1_xattn_in['bq'], 'L1_xattn_Wk': _L1_xattn_in['Wk'], 'L1_xattn_bk': _L1_xattn_in['bk'], 'L1_xattn_Wv': _L1_xattn_in['Wv'], 'L1_xattn_bv': _L1_xattn_in['bv'], 'L1_xattn_Wo': _L1_xattn_in['Wo'], 'L1_xattn_bo': _L1_xattn_in['bo'], 'L1_attn_Wq': _L1_attn_in['Wq'], 'L1_attn_bq': _L1_attn_in['bq'], 'L1_attn_Wk': _L1_attn_in['Wk'], 'L1_attn_bk': _L1_attn_in['bk'], 'L1_attn_Wv': _L1_attn_in['Wv'], 'L1_attn_bv': _L1_attn_in['bv'], 'L1_attn_Wo': _L1_attn_in['Wo'], 'L1_attn_bo': _L1_attn_in['bo'], 'L1_attn_Weq': _L1_attn_in['Weq'], 'L1_attn_beq': _L1_attn_in['beq'], 'L1_attn_Wek': _L1_attn_in['Wek'], 'L1_attn_bek': _L1_attn_in['bek'], 'L1_attn_amp_w': _L1_attn_in['amp_w'], 'L1_attn_amp_b': _L1_attn_in['amp_b'], 'L1_attn_ph_w': _L1_attn_in['ph_w'], 'L1_attn_ph_b': _L1_attn_in['ph_b'], 'L1_attn_mix_w': _L1_attn_in['mix_w'], 'L1_attn_mix_b': _L1_attn_in['mix_b'], 'L1_attn_ln_g': _L1_attn_in['ln_g'], 'L1_attn_ln_b': _L1_attn_in['ln_b'], 'L1_ffn_centroids': _L1_ffn_in['centroids'], 'L1_ffn_ln_g': _L1_ffn_in['ln_g'], 'L1_ffn_ln_b': _L1_ffn_in['ln_b'], 'L1_ffn_w1': _L1_ffn_in['w1'], 'L1_ffn_b1': _L1_ffn_in['b1'], 'L1_ffn_w2': _L1_ffn_in['w2'], 'L1_ffn_b2': _L1_ffn_in['b2']}

def reference(x, ctx_1024, mask_1xSxS2_ff0, mask_Bx1x1xS2_fk0, L0_xattn_kernel_q, L0_xattn_bias_q, L0_xattn_kernel_k, L0_xattn_bias_k, L0_xattn_kernel_v, L0_xattn_bias_v, L0_attn_gain, L0_attn_w_q, L0_attn_w_k, L0_attn_w_v, L0_attn_w_o, L0_ffn_W_r, L0_ffn_W_k, L0_ffn_W_v, L0_ffn_mu_r, L0_ffn_mu_k, L1_xattn_Wq, L1_xattn_bq, L1_xattn_Wk, L1_xattn_bk, L1_xattn_Wv, L1_xattn_bv, L1_xattn_Wo, L1_xattn_bo, L1_attn_Wq, L1_attn_bq, L1_attn_Wk, L1_attn_bk, L1_attn_Wv, L1_attn_bv, L1_attn_Wo, L1_attn_bo, L1_attn_Weq, L1_attn_beq, L1_attn_Wek, L1_attn_bek, L1_attn_amp_w, L1_attn_amp_b, L1_attn_ph_w, L1_attn_ph_b, L1_attn_mix_w, L1_attn_mix_b, L1_attn_ln_g, L1_attn_ln_b, L1_ffn_centroids, L1_ffn_ln_g, L1_ffn_ln_b, L1_ffn_w1, L1_ffn_b1, L1_ffn_w2, L1_ffn_b2):
    import jax
    import jax.numpy as jnp

    def _L0_xattn_ref(q, k, v, mask, kernel_q, bias_q, kernel_k, bias_k, kernel_v, bias_v):
        import jax, jax.numpy as jnp
        import numpy as np
        INP_SIZE = 128
        D_MODEL = 128
        B, S = (4, 256)
        qp = jnp.einsum('bsi,id->bsd', q, kernel_q) + bias_q
        kp = jnp.einsum('bsi,id->bsd', k, kernel_k) + bias_k
        vp = jnp.einsum('bsi,id->bsd', v, kernel_v) + bias_v
        dk = jnp.asarray(kp.shape[-1], dtype=jnp.float32)
        logits = jnp.einsum('bqd,bkd->bqk', qp, kp) / jnp.sqrt(dk)
        logits = logits + mask
        attn = jax.nn.softmax(logits, axis=-1)
        out = jnp.einsum('bqk,bkd->bqd', attn, vp)
        return out

    def _L0_attn_ref(query, gain, w_q, w_k, w_v, w_o):
        import jax, jax.numpy as jnp
        import numpy as np
        EPS = 0.0001

        def mp_normalize(x, axis):
            red = int(np.prod([x.shape[a] for a in axis])) if isinstance(axis, (list, tuple)) else x.shape[axis]
            w = jnp.sqrt(jnp.sum(jnp.square(x.astype(jnp.float32)), axis=axis, keepdims=True))
            w = EPS + w / np.sqrt(red)
            return x / w.astype(x.dtype)

        def mp_linear(x, w, gain):
            fan_in = w.shape[1]
            wn = mp_normalize(w.astype(jnp.float32), axis=(1,)) * (gain / np.sqrt(fan_in))
            return jnp.einsum('bse,oe->bso', x, wn.astype(x.dtype))

        def attention(query, gain, w_q, w_k, w_v, w_o, num_heads=16, attn_balance=0.5):
            B, S, E = query.shape
            hd = E // num_heads
            res = query
            q = mp_linear(query, w_q, gain).reshape(B, S, num_heads, hd).transpose(0, 2, 1, 3)
            k = mp_linear(query, w_k, gain).reshape(B, S, num_heads, hd).transpose(0, 2, 1, 3)
            v = mp_linear(query, w_v, gain).reshape(B, S, num_heads, hd).transpose(0, 2, 1, 3)
            q = mp_normalize(q, axis=(3,))
            k = mp_normalize(k, axis=(3,))
            scores = jnp.einsum('bnsh,bnsk->bnhk', q, k / np.sqrt(S))
            attn = jax.nn.softmax(scores, axis=3)
            o = jnp.einsum('bnhk,bnsk->bnsh', attn, v)
            o = o.transpose(0, 2, 1, 3).reshape(B, S, E)
            out = mp_linear(o, w_o, gain)
            t = attn_balance
            return (res * (1.0 - t) + out * t) / np.sqrt((1 - t) ** 2 + t ** 2)
        return attention(query, gain, w_q, w_k, w_v, w_o)

    def _L0_ffn_ref(x, W_r, W_k, W_v, mu_r, mu_k):
        import jax, jax.numpy as jnp
        import numpy as np
        DIM = 128

        def _reference_tuple_inner(x, W_r, W_k, W_v, mu_r, mu_k):
            B, T, C = x.shape
            x_prev = jnp.concatenate([jnp.zeros((B, 1, C), x.dtype), x[:, :-1, :]], axis=1)
            xr = mu_r * x + (1.0 - mu_r) * x_prev
            xk = mu_k * x + (1.0 - mu_k) * x_prev
            r = jax.nn.sigmoid(jnp.einsum('btc,dc->btd', xr, W_r))
            k = jnp.einsum('btc,dc->btd', xk, W_k)
            k_act = jnp.square(jax.nn.relu(k))
            out = r * jnp.einsum('btc,dc->btd', k_act, W_v)
            new_state = x[:, -1, :]
            return (out, new_state)
        return _reference_tuple_inner(x, W_r, W_k, W_v, mu_r, mu_k)[0]

    def _L1_xattn_ref(query, key, value, mask, Wq, bq, Wk, bk, Wv, bv, Wo, bo):
        import jax, jax.numpy as jnp
        import numpy as np
        B, S, D, H = (2, 256, 128, 16)
        DH = D // H

        def _split_heads(x):
            b, s, _ = x.shape
            return x.reshape(b, s, H, DH).transpose(0, 2, 1, 3)
        q = _split_heads(query @ Wq + bq)
        k = _split_heads(key @ Wk + bk)
        v = _split_heads(value @ Wv + bv)
        logits = jnp.einsum('bhqd,bhkd->bhqk', q, k) / jnp.sqrt(jnp.float32(DH))
        logits = logits + mask * -1000000000.0
        attn = jax.nn.softmax(logits, axis=-1)
        out = jnp.einsum('bhqk,bhkd->bhqd', attn, v)
        out = out.transpose(0, 2, 1, 3).reshape(query.shape[0], -1, D)
        return out @ Wo + bo

    def _L1_attn_ref(hidden_states, Wq, bq, Wk, bk, Wv, bv, Wo, bo, Weq, beq, Wek, bek, amp_w, amp_b, ph_w, ph_b, mix_w, mix_b, ln_g, ln_b):
        import jax, jax.numpy as jnp
        import numpy as np
        import math
        B, S, D, H = (1, 256, 128, 16)
        HD = D // H
        SCALE = 1.0 / math.sqrt(HD)
        ENT = 0.5
        DECAY = 0.1
        SUP = 0.3
        EPS = 1e-05

        def _heads(x):
            b, s, _ = x.shape
            return x.reshape(b, s, H, HD).transpose(0, 2, 1, 3)
        hs = hidden_states
        b, s, _ = hs.shape
        q = _heads(hs @ Wq.T + bq)
        k = _heads(hs @ Wk.T + bk)
        v = _heads(hs @ Wv.T + bv)
        scores = jnp.einsum('bhqd,bhkd->bhqk', q, k) * SCALE
        eq = _heads(hs @ Weq.T + beq)
        ek = _heads(hs @ Wek.T + bek)
        pos = jnp.arange(s)
        decay = jnp.exp(-DECAY * jnp.abs(pos[:, None] - pos[None, :]).astype(jnp.float32))
        esc = jnp.einsum('bhqd,bhkd->bhqk', eq, ek) * (1.0 / math.sqrt(HD)) * decay
        attn = jax.nn.softmax(scores + ENT * esc, axis=-1)
        amps = jax.nn.sigmoid(hs @ amp_w.T + amp_b)
        phases = jnp.tanh(hs @ ph_w.T + ph_b) * math.pi
        a = amps.transpose(0, 2, 1)[..., None]
        p = phases.transpose(0, 2, 1)[..., None]
        sup = jnp.einsum('bhsd,hod->bhso', v, mix_w) + mix_b[None, :, None, :]
        mixed = v + SUP * a * jnp.cos(p) * sup + SUP * a * jnp.sin(p) * jnp.roll(sup, 1, axis=-1)
        ctx = jnp.einsum('bhqk,bhkd->bhqd', attn, mixed)
        ctx = ctx.transpose(0, 2, 1, 3).reshape(b, s, D)
        out = ctx @ Wo.T + bo
        res = hs + out
        mu = jnp.mean(res, axis=-1, keepdims=True)
        var = jnp.mean((res - mu) ** 2, axis=-1, keepdims=True)
        return (res - mu) * jax.lax.rsqrt(var + EPS) * ln_g + ln_b

    def _L1_ffn_ref(input_features, centroids, ln_g, ln_b, w1, b1, w2, b2):
        import jax, jax.numpy as jnp
        import numpy as np
        B, S, D, F, E = (8, 128, 128, 512, 8)
        EPS = 1e-05
        x = input_features.reshape(-1, D)
        aff = jax.lax.stop_gradient(x @ centroids.T)
        eid = jnp.argmax(aff, axis=-1)
        alpha = jax.nn.sigmoid(jnp.sum(x * centroids[eid], axis=-1, keepdims=True))
        mu = jnp.mean(x, axis=-1, keepdims=True)
        var = jnp.mean((x - mu) ** 2, axis=-1, keepdims=True)
        xn = (x - mu) * jax.lax.rsqrt(var + EPS)
        xln = xn * ln_g[eid] + ln_b[eid]
        onehot = jax.nn.one_hot(eid, E, dtype=x.dtype)
        ffn = jnp.zeros_like(x)
        for e in range(E):
            h = jax.nn.relu(xln @ w1[e] + b1[e])
            ffn = ffn + onehot[:, e:e + 1] * (h @ w2[e] + b2[e])
        out = x + alpha * ffn
        return out.reshape(input_features.shape)
    x = x + _L0_xattn_ref(_layernorm(x, axis=-1), ctx_1024, ctx_1024, mask_1xSxS2_ff0, L0_xattn_kernel_q, L0_xattn_bias_q, L0_xattn_kernel_k, L0_xattn_bias_k, L0_xattn_kernel_v, L0_xattn_bias_v)
    x = x + _L0_attn_ref(_layernorm(x, axis=-1), L0_attn_gain, L0_attn_w_q, L0_attn_w_k, L0_attn_w_v, L0_attn_w_o)
    x = x + _L0_ffn_ref(_layernorm(x, axis=-1), L0_ffn_W_r, L0_ffn_W_k, L0_ffn_W_v, L0_ffn_mu_r, L0_ffn_mu_k)
    x = x + _L1_xattn_ref(_layernorm(x, axis=-1), ctx_1024, ctx_1024, mask_Bx1x1xS2_fk0, L1_xattn_Wq, L1_xattn_bq, L1_xattn_Wk, L1_xattn_bk, L1_xattn_Wv, L1_xattn_bv, L1_xattn_Wo, L1_xattn_bo)
    x = x + _L1_attn_ref(_layernorm(x, axis=-1), L1_attn_Wq, L1_attn_bq, L1_attn_Wk, L1_attn_bk, L1_attn_Wv, L1_attn_bv, L1_attn_Wo, L1_attn_bo, L1_attn_Weq, L1_attn_beq, L1_attn_Wek, L1_attn_bek, L1_attn_amp_w, L1_attn_amp_b, L1_attn_ph_w, L1_attn_ph_b, L1_attn_mix_w, L1_attn_mix_b, L1_attn_ln_g, L1_attn_ln_b)
    x = x + _L1_ffn_ref(_layernorm(x, axis=-1), L1_ffn_centroids, L1_ffn_ln_g, L1_ffn_ln_b, L1_ffn_w1, L1_ffn_b1, L1_ffn_w2, L1_ffn_b2)
    return x

_drawn_inputs = setup_inputs


def setup_inputs(seed=0):
    import zlib

    import numpy as np

    out = dict(_drawn_inputs(seed))
    spreads = {'L1_xattn_bq': (0.0, 0.8),
     'L1_xattn_bk': (0.0, 2.0),
     'L1_xattn_bv': (0.0, 0.648),
     'L1_xattn_bo': (0.0, 0.1),
     'L1_attn_bq': (0.0, 0.8),
     'L1_attn_bk': (0.0, 2.0),
     'L1_attn_bv': (0.0, 0.8),
     'L1_attn_bo': (0.0, 0.1),
     'L1_attn_beq': (0.0, 2.0),
     'L1_attn_bek': (0.0, 2.0),
     'L1_attn_amp_b': (0.0, 2.0),
     'L1_attn_ph_b': (0.0, 0.8),
     'L1_attn_mix_b': (0.0, 0.8),
     'L1_attn_ln_g': (1.0, 0.2),
     'L1_attn_ln_b': (0.0, 0.1),
     'L1_ffn_ln_g': (1.0, 0.6),
     'L1_ffn_ln_b': (0.0, 0.8),
     'L1_ffn_b1': (0.0, 0.8),
     'L1_ffn_b2': (0.0, 0.357)}
    factors = {'L0_xattn_bias_q': 8.0,
     'L0_xattn_bias_k': 64.0,
     'L0_ffn_W_r': 5.389,
     'L0_ffn_mu_r': 8.0,
     'L1_xattn_Wq': 8.0,
     'L1_xattn_Wk': 8.0,
     'L1_xattn_Wv': 3.936,
     'L1_xattn_Wo': 3.029,
     'L1_attn_Wq': 8.0,
     'L1_attn_Wk': 8.0,
     'L1_attn_Wv': 8.0,
     'L1_attn_Wo': 5.165,
     'L1_attn_Weq': 64.0,
     'L1_attn_Wek': 28.462,
     'L1_attn_amp_w': 8.0,
     'L1_attn_ph_w': 8.0,
     'L1_attn_mix_w': 8.0,
     'L1_ffn_w1': 4.061,
     'L1_ffn_w2': 3.21}
    for name, (base, spread) in spreads.items():
        noise = np.random.default_rng([zlib.crc32(name.encode()), seed]).standard_normal(out[name].shape)
        drawn = base * np.exp(spread * noise) if base else spread * noise
        out[name] = jnp.asarray(drawn.astype(out[name].dtype))
    for name, factor in factors.items():
        out[name] = (out[name] * factor).astype(out[name].dtype)
    return out
```

```python
from contextlib import ExitStack
import math

import concourse.bass as bass
from concourse import mybir

F32 = mybir.dt.float32
BF16 = mybir.dt.bfloat16
ALU = mybir.AluOpType
ACT = mybir.ActivationFunctionType
AX = mybir.AxisListType

B, S, D = 4, 128, 128
KEYS = 2048
KT = KEYS // 128
H, HD = 16, 8
BANK = 512
NE, FF = 8, 512
FT = FF // 128
HQ = 4
UNITS = H // HQ
COMBOS = [(0, 0), (1, 0), (2, 0), (0, 1), (1, 1), (0, 2)]
ROWS = len(COMBOS) * HD
MASK_ROW = 2 * ROWS
MAX_ROW = MASK_ROW + 3
PAIR_ROWS = MAX_ROW + 6
MATS = ["L0x_q", "L0x_kT", "L0x_v", "L0a_q", "L0a_k", "L0a_v", "L0a_o", "L0f_rT", "L0f_kT", "L0f_vT",
        "L1x_q", "L1x_k", "L1x_v", "L1x_o", "L1a_qT", "L1a_kT", "L1a_vT", "L1a_oT", "L1a_eqT", "L1a_ekT",
        "mix", "mix_rolled", "amp_ph"]
COLS = ["L0x_bq", "L0x_bk", "gain", "mu_r", "mu_k", "L1x_bq", "L1x_bk",
        "L1a_bq", "L1a_bk", "L1a_bv", "L1a_beq", "L1a_bek"]
ROWV = ["L0x_bv", "L1x_bv", "L1x_bo", "L1a_bv", "L1a_bo", "L1a_ln_g", "L1a_ln_b", "mix_b", "mix_b_rolled",
        "amp_ph_b"]
CONSTS = ["identity", "off_block", "head_mask", "decay", "first_weight"]


def build(nc, x, ctx, ctx_t, mask0, mask1, mats, cols, expert_cols, rows, centroids_t, b2, w1, w2,
          consts, out):
    with ExitStack() as stack:
        def sb(name, shape, dt=F32):
            return stack.enter_context(nc.sbuf_tensor(name, shape, dt))

        made = {}

        def sem(name):
            if name not in made:
                made[name] = stack.enter_context(nc.semaphore(name))
            return made[name]

        LINES = {
            "attn0_dve": [("a_wsq", 4), ("a_rw", 2), ("a_wn", 4), ("a_res", 1), ("a_headsq", 1), ("a_headw", 1),
                ("a_headr", 1), ("a_qkn", 1), ("a_masked", 1), ("a_max", 1), ("a_shifted", 1), ("a_sum", 1),
                ("a_rsum", 1), ("a_probs", 1)],
            "attn0_pe": [("a_wnt", 1), ("a_qk", 1), ("a_v", 1), ("a_scores", 1), ("a_mo", 1), ("a_out", 1)],
            "attn0_act": [("a_wnT", 1), ("a_sq", 1), ("a_vT", 1), ("a_headn", 1), ("a_exp", 1), ("a_mo_sb", 1)],
            "attn0_pool": [("a_half", 1), ("a_wroot", 1), ("a_w", 1)],
            "ffn0_dve": [("f_shift", 2), ("f_mix", 2), ("f_clamped", 1), ("f_ksq", 1), ("f_gate", 2), ("f_out", 1)],
            "ffn0_pe": [("f_r", 1), ("f_k", 1), ("f_v", 1)],
            "ffn0_act": [("f_relu", 1), ("f_exp", 1)],
            "ffn0_pool": [("f_zero", 1), ("f_om", 1)],
            "attn1_dve": [("b_q", 2), ("b_z", 2), ("b_vb", 1), ("b_arg", 1), ("b_amp1", 3), ("b_s1", 1), ("b_s2", 1),
                ("b_coef", 2), ("b_t1", 1), ("b_t2", 1), ("b_t3", 1), ("b_mixed", 1), ("b_zero", 1), ("c_bo",
                1), ("c_res", 1), ("c_gain", 1), ("c_shiftb", 1)],
            "attn1_pe": [("b_proj", 5), ("b_amp", 1), ("b_vn", 1), ("b_sup", 2), ("c_all_t", 1), ("c_out", 1)],
            "attn1_act": [("b_vT", 1), ("b_k", 2), ("b_eamp", 1), ("b_tanh", 1), ("b_abs", 1), ("b_sin", 2), ("c_oT", 1)],
            "ffn1_dve": [("d_res", 1), ("d_top", 2), ("d_clamp", 1), ("d_sel", 4), ("d_al", 2), ("d_gate", 1)],
            "ffn1_pe": [("d_aff", 1), ("d_gate_t", 1), ("d_b2", 1)],
            "ffn1_act": [("d_exp", 1), ("d_gate_T", 1)],
        }
        LINE_OF = {name: line for line, steps in LINES.items() for name, _ in steps}

        def sem_of(name):
            return sem(LINE_OF[name])

        def step(name, count):
            steps = [n for n, _ in LINES[LINE_OF[name]]]
            return sem_of(name), sum(c for _, c in LINES[LINE_OF[name]][:steps.index(name)]) + count

        k_stack = nc.dram_tensor("k_stack", (B, H, ROWS, KEYS), BF16, kind="Internal").ap()
        q_stack = nc.dram_tensor("q_stack", (H, ROWS, B * S), BF16, kind="Internal").ap()
        mask_parts_d = nc.dram_tensor("mask_parts_d", (3, B, KEYS), BF16, kind="Internal").ap()
        v_units = nc.dram_tensor("v_units", (B, UNITS, 128, KT * HQ * (HD + 1)), F32, kind="Internal").ap()

        W = sb("W", [128, len(MATS), 128])
        C = sb("C", [128, len(COLS)])
        EC = sb("EC", [128, NE * (2 + FT)])
        R = sb("R", [128, len(ROWV), 128])
        K = sb("K", [128, len(CONSTS), 128])
        CT = sb("CT", [128, NE])
        B2 = sb("B2", [NE, D])
        ident_bf = sb("ident_bf", [128, 128], BF16)

        def mat(n):
            return W[:, MATS.index(n), :]

        def col(n):
            i = COLS.index(n)
            return C[:, i:i + 1]

        def row(n):
            return R[:, ROWV.index(n), :]

        def const(n):
            return K[:, CONSTS.index(n), :]

        ident = const("identity")

        xN = sb("xN", [128, B, D])
        xhN = sb("xhN", [128, B, D])
        xhT = sb("xhT", [128, B * S])
        stats = sb("stats", [128, B, 6])
        mv = sb("mv", [128, B, 2])
        var_eps = sb("var_eps", [128, B])
        rstd = sb("rstd", [128, B])
        neg_half = sb("neg_half", [128, B])
        tA = sb("tA", [128, 1024])
        tB = sb("tB", [128, 1024])
        tC = sb("tC", [128, 1024])
        tD = sb("tD", [128, 1024])
        tE = sb("tE", [128, 1024])
        tF = sb("tF", [128, 1024])
        small = sb("small", [128, 256])
        ARENA = 38400
        arena = sb("arena", [128, ARENA])

        def carve(sizes):
            at, got = 0, []
            for words in sizes:
                got.append(arena[:, at:at + words])
                at += words
            assert at <= ARENA
            return got

        ps = stack.enter_context(nc.psum_tensor("ps", [128, 8 * BANK], F32))

        def bank(i, n=BANK, off=0):
            return ps[:, i * BANK + off:i * BANK + off + n]

        def b3(ap, inner=128):
            return ap.rearrange("p (b d) -> p b d", d=inner)

        def bc_mid(ap, n):
            return ap.rearrange("p (o m) -> p o m", o=1).broadcast_to([128, n, ap.shape[1]])

        def bc_in(ap, n):
            return ap.rearrange("p (m o) -> p m o", o=1).broadcast_to([128, ap.shape[1], n])

        def ln_dve(v, i, ready, src=None, dst=None):
            src = b3(xN_flat) if src is None else src
            dst = xhN if dst is None else dst
            for b in range(B):
                if b == 0:
                    v.wait_ge(*ready)
                v.bn_stats(stats[:, b, :], src[:, b, :]).then_inc(sem("ln_stats"), 1)
            for b in range(B):
                v.wait_ge(sem("ln_stats"), i * B + b + 1)
                v.bn_aggr(mv[:, b, :], stats[:, b, :]).then_inc(sem("ln_mv"), 1)
            v.wait_ge(sem("ln_rstd"), i + 1)
            for b in range(B):
                v.tensor_scalar(dst[:, b, :], src[:, b, :], mv[:, b, 0:1], rstd[:, b:b + 1],
                                ALU.subtract, ALU.mult).then_inc(sem("ln_xh"), 1)

        def ln_pool(g, i, eps=1e-5):
            g.wait_ge(sem("ln_mv"), i * B + B)
            g.tensor_scalar(var_eps[:, :], mv[:, :, 1], eps, None, ALU.add).then_inc(sem("ln_ve"), 1)
            g.wait_ge(sem("ln_ve"), i + 1)
            g.tensor_tensor(rstd[:, :], var_eps[:, :], neg_half[:, :], ALU.pow).then_inc(sem("ln_rstd"), 1)

        def transpose4_pe(pe, src, bk, ready, done):
            pe.wait_ge(*ready)
            for b in range(B):
                t = pe.transpose(bank(bk, 128, 128 * b), src[:, b, :], ident)
            t.then_inc(done, 1)

        START_AT_ONE = ["o0_done", "s_masked", "pt_copied", "k_rest_done", "v_added", "x0_new", "scores0",
                        "k_out0", "k_out1", "v_out0", "v_out1", "p_t", "exp0", "nbias0", "k3_done"]

        xN_flat = xN[:, :, :].rearrange("p b d -> p (b d)")
        SQ_D = 1.0 / math.sqrt(D)

        (ctxN0, ctxN1, ctxT0, ctxT1, mask_sb, s_mask, p_nat, p_t, kp0, kp1, vb0, vb1, kr0, kr1, x_bv,
         mask1_f, mask1_r, mask1_p) = carve([
             2048, 2048, 2048, 2048, 2048, 2048, 2048, 2048, 3072, 3072, KT * H * 9, KT * H * 9, 512, 512, 512,
             64, 64, 96])
        ctxN = [b3(ctxN0), b3(ctxN1)]
        ctxT = [ctxT0, ctxT1]
        k_parts = [kp.bitcast(BF16).rearrange("p (j n) -> p j n", j=3) for kp in (kp0, kp1)]
        vbuf = [vb.rearrange("p (u t g e) -> p u t g e", u=UNITS, t=KT, g=HQ) for vb in (vb0, vb1)]
        k_rest = [kr0, kr1]
        mparts = mask1_p.bitcast(BF16).rearrange("p (j n) -> p j n", j=3)
        qT, qk_T, kwork = tA[:, 0:512], tB[:, 0:512], tA[:, 512:1024]
        qk_b = [tC[:, 0:128], tC[:, 128:256]]
        oT0 = [tD[:, 0:128], tD[:, 128:256]]
        c_q, mx, mc, nbias, rsum, rinv, cb = (small[:, 8 * i:8 * i + 8] for i in range(7))

        def l0x_sync(sp):
            for name in START_AT_ONE:
                sp.sem_inc(sem(name), 1)
            for name, value in START.items():
                sp.sem_inc(sem(name), value)
            sp.dma_start(xN[:, :, :], x.rearrange("b s d -> s b d")).then_inc(sem("in_x"), 16)
            sp.dma_start(K[:, :, :], consts).then_inc(sem("in_consts"), 16)
            sp.dma_start(W[:, :, :], mats).then_inc(sem("in_mats"), 16)
            sp.dma_start(C[:, :], cols).then_inc(sem("in_small"), 16)
            sp.dma_start(R[:, :, :], rows.partition_broadcast(128)).then_inc(sem("in_rows"), 16)
            sp.dma_start(mask1_f, mask1).then_inc(sem("in_mask1"), 16)
            sp.dma_start(mask_sb, mask0).then_inc(sem("in_mask0"), 16)
            sp.dma_start(EC[:, :], expert_cols).then_inc(sem("in_experts"), 16)
            sp.dma_start(CT[:, :], centroids_t).then_inc(sem("in_experts"), 16)
            sp.dma_start(B2[:, :], b2).then_inc(sem("in_experts"), 16)
            with sp.Fori(0, B // 2) as it:
                for s in range(2):
                    sp.wait_ge(sem("o0_done"), it * 2 + 1)
                    sp.dma_start(ctxT[s], ctx_t[bass.ds(it * 2 + s, 1), :, :].rearrange("o d n -> (o d) n")
                                 ).then_inc(sem(f"in_ctx{s}"), 16)
                    for half in range(2):
                        t = slice(half * KT // 2, (half + 1) * KT // 2)
                        sp.dma_start(ctxN[s][:, t, :],
                                     ctx[bass.ds(it * 2 + s, 1), half * KEYS // 2:(half + 1) * KEYS // 2, :]
                                     .rearrange("o (t p) d -> p (o t) d", p=128)).then_inc(sem(f"in_ctx{s}"), 16)

        def l0x_store(g, s, it):
            n = it * 2 + s
            g.wait_ge(sem("k1_done"), n * 4 + 4)
            g.wait_ge(sem("k3_done"), n * 4 + 4 + 1)
            for c, (_, j) in enumerate(COMBOS):
                g.dma_start(k_stack[bass.ds(n, 1), :, c * HD:(c + 1) * HD, :].rearrange("o h d n -> (o h) d n"),
                            k_parts[s][:, j, :]).then_inc(sem(f"k_out{s}"), 16)
            g.wait_ge(sem("v_added"), n * KT + KT + 1)
            g.dma_start(v_units[bass.ds(n, 1), :, :, :].rearrange("o u k n -> k (o u) n"),
                        vbuf[s].rearrange("p u t g e -> p u (t g e)")).then_inc(sem(f"v_out{s}"), 16)

        def l0x_pe(pe):
            pe.wait_ge(sem("in_consts"), 16)
            transpose4_pe(pe, xhN, 0, (sem("ln_xh"), 0 * B + B), sem("ln_t"))
            pe.wait_ge(sem("in_mats"), 16)
            pe.wait_ge(sem("ln_T"), 1)
            pe.matmul(bank(1), mat("L0x_q"), xhT[:, :], start=True, stop=True).then_inc(sem("q0"), 1)
            pe.wait_ge(sem("q0_sb"), 1)
            pe.matmul(bank(2), mat("L0x_kT"), qT, start=True, stop=True).then_inc(sem("qk0"), 1)
            for b in range(B):
                m = pe.matmul(bank(3, 1, b), qT[:, b * S:(b + 1) * S], col("L0x_bk"), start=True, stop=True)
            m.then_inc(sem("c0"), 1)
            pe.wait_ge(sem("c0_sb"), 1)
            with pe.Fori(0, B // 2) as it:
                for s in range(2):
                    n = it * 2 + s
                    pe.wait_ge(sem(f"in_ctx{s}"), it * 48 + 48)
                    pe.wait_ge(sem("qk_b"), n + 1)
                    pe.wait_ge(sem("s_masked"), n + 1)
                    for c in range(4):
                        m = pe.matmul(bank(c), qk_b[s], ctxT[s][:, c * BANK:(c + 1) * BANK], start=True, stop=True)
                    m.then_inc(sem("scores0"), 1)
                    for c in range(4):
                        if c == 0:
                            pe.wait_ge(sem("pt_copied"), n * 4 + 1)
                        pe.wait_ge(sem("k_rest_done"), n * 4 + c + 1)
                        pe.matmul(bank(4), mat("L1x_k"), ctxT[s][:, c * BANK:(c + 1) * BANK], start=True, stop=True
                                  ).then_inc(sem("k_proj"), 1)
                        pe.wait_ge(sem("v_added"), n * KT + 4 * c + 1)
                        for t in range(4 * c, 4 * c + 4):
                            m = pe.matmul(bank(5, 128, 128 * (t % 4)), ctxT[s][:, t * 128:(t + 1) * 128],
                                          mat("L1x_v"), start=True, stop=True)
                        m.then_inc(sem("v_proj"), 1)
                    pe.wait_ge(sem("exp0"), n + 1 + 1)
                    for gr in range(4):
                        if gr == 1:
                            pe.wait_ge(sem("k_rest_done"), n * 4 + 4 + 1)
                        if gr == 2:
                            pe.wait_ge(sem("v_added"), n * KT + KT + 1)
                        if gr == 3:
                            pe.wait_ge(sem("pt_copied"), n * 4 + 1 + 1)
                        for t in range(4 * gr, 4 * gr + 4):
                            m = pe.transpose(bank((6, 4, 5, 6)[gr], 128, 128 * (t % 4)),
                                             p_nat[:, t * 128:(t + 1) * 128], ident)
                        m.then_inc(sem("p_t"), 1)
                    pe.wait_ge(sem("x0_new"), n + 1)
                    for gr in range(4):
                        pe.wait_ge(sem("pt_copied"), n * 4 + gr + 1 + 1)
                        for t in range(4 * gr, 4 * gr + 4):
                            m = pe.matmul(bank(7, 128), ctxN[s][:, t, :], p_t[:, t * 128:(t + 1) * 128],
                                          start=t == 0, stop=t == KT - 1)
                    m.then_inc(sem("o0_done"), 1)
                    pe.wait_ge(sem("oT0_sb"), n + 1)
                    pe.matmul(bank(7, 128, 128), oT0[s], mat("L0x_v"), start=True, stop=True).then_inc(sem("y0"), 1)

        def l0x_act(act):
            act.wait_ge(sem("ln_t"), 1)
            act.activation(xhT[:, :], bank(0), ACT.Copy).then_inc(sem("ln_T"), 1)
            act.wait_ge(sem("in_small"), 16)
            act.wait_ge(sem("q0"), 1)
            act.activation(qT, bank(1), ACT.Identity, bias=col("L0x_bq")).then_inc(sem("q0_sb"), 1)
            act.wait_ge(sem("qk0"), 1)
            act.activation(qk_T, bank(2), ACT.Copy, scale=SQ_D).then_inc(sem("qk0_sb"), 1)
            act.wait_ge(sem("qk0_sb"), 1)
            with act.Fori(0, B // 2) as it:
                for s in range(2):
                    n = it * 2 + s
                    act.wait_ge(sem("scores0"), it * 2 + 1)
                    act.activation(qk_b[s], qk_T[:, bass.ds(n * 128, 128)], ACT.Copy).then_inc(sem("qk_b"), 1)
                    for c in range(4):
                        act.wait_ge(sem("k_proj"), n * 4 + c + 1)
                        if c == 0:
                            act.wait_ge(sem(f"k_out{s}"), it * 16 * len(COMBOS) + 1)
                        act.activation(k_parts[s][:, 0, c * BANK:(c + 1) * BANK], bank(4), ACT.Identity,
                                       bias=col("L1x_bk")).then_inc(sem("k1_done"), 1)
                        if c == 0:
                            act.wait_ge(sem("nbias0"), n + 1 + 1)
                            act.wait_ge(sem("p_t"), n * 4 + 1)
                            act.activation(p_nat, s_mask, ACT.Exp, bias=nbias[:, s:s + 1],
                                           accum_out=rsum[:, s:s + 1]).then_inc(sem("exp0"), 1)
                    act.wait_ge(sem("o0_done"), n + 1)
                    for gr in range(4):
                        act.wait_ge(sem("p_t"), n * 4 + gr + 1 + 1)
                        act.activation(p_t[:, gr * BANK:(gr + 1) * BANK], bank((6, 4, 5, 6)[gr]), ACT.Copy
                                       ).then_inc(sem("pt_copied"), 1)
                    act.wait_ge(sem("o0_done"), n + 1 + 1)
                    act.activation(oT0[s], bank(7, 128), ACT.Copy).then_inc(sem("oT0_sb"), 1)
                    l0x_store(act, s, it)

        def l0x_dve(v):
            ln_dve(v, 0, (sem("in_x"), 16))
            for s in range(2):
                v.memset(vbuf[s][:, :, :, :, HD], 1.0).then_inc(sem("v_ones"), 1)
            v.wait_ge(sem("in_rows"), 16)
            v.tensor_tensor(b3(x_bv), xN[:, :, :], bc_mid(row("L0x_bv"), B), ALU.add).then_inc(sem("x_bv"), 1)
            l0a_prepare_dve(v)
            x1_early_dve(v)
            v.wait_ge(sem("c0"), 1)
            v.tensor_scalar(c_q[:, 0:B], bank(3, B), SQ_D, None, ALU.mult).then_inc(sem("c0_sb"), 1)
            v.wait_ge(sem("c0_sb"), 1)
            v.wait_ge(sem("in_mask0"), 16)
            v.wait_ge(sem("in_small"), 16)
            v.wait_ge(sem("x_bv"), 1)
            with v.Fori(0, B // 2) as it:
                for s in range(2):
                    n = it * 2 + s
                    v.wait_ge(sem("scores0"), n + 1 + 1)
                    v.wait_ge(sem("exp0"), n + 1)
                    v.wait_ge(sem("nbias0"), n + 1)
                    v.tensor_copy(cb[:, s:s + 1], c_q[:, bass.ds(n, 1)]).then_inc(sem("c_b"), 1)
                    v.tensor_tensor_reduce(s_mask, ps[:, 0:KEYS], mask_sb, 1.0, -3.0e38, ALU.add, ALU.max,
                                           mx[:, s:s + 1]).then_inc(sem("s_masked"), 1)
                    v.wait_ge(sem("s_masked"), n + 1 + 1)
                    v.wait_ge(sem("c_b"), n + 1)
                    v.tensor_tensor(mc[:, s:s + 1], mx[:, s:s + 1], cb[:, s:s + 1], ALU.add
                                    ).then_inc(sem("mc0"), 1)
                    v.wait_ge(sem("mc0"), n + 1)
                    v.tensor_tensor(nbias[:, s:s + 1], cb[:, s:s + 1], mc[:, s:s + 1], ALU.subtract
                                    ).then_inc(sem("nbias0"), 1)
                    for c in range(4):
                        v.wait_ge(sem("k1_done"), n * 4 + c + 1)
                        v.wait_ge(sem("k3_done"), it * 8 + (s * 4 + c - 1 if s * 4 + c > 1 else 0) + 1)
                        v.scalar_tensor_tensor(out=k_rest[c % 2], in0=bank(4), scalar=col("L1x_bk"),
                                               in1=k_parts[s][:, 0, c * BANK:(c + 1) * BANK],
                                               op0=ALU.add, op1=ALU.subtract).then_inc(sem("k_rest_done"), 1)
                        if c == 0:
                            v.wait_ge(sem(f"k_out{s}"), it * 16 * len(COMBOS) + 1)
                        v.wait_ge(sem("k_rest_done"), n * 4 + c + 1 + 1)
                        v.tensor_copy(k_parts[s][:, 1, c * BANK:(c + 1) * BANK], k_rest[c % 2]
                                      ).then_inc(sem("k2_done"), 1)
                        v.wait_ge(sem("v_proj"), n * 4 + c + 1)
                        if c == 0:
                            v.wait_ge(sem(f"v_out{s}"), it * 16 + 1)
                        for t in range(4 * c, 4 * c + 4):
                            v.tensor_tensor(vbuf[s][:, :, t, :, 0:HD],
                                            bank(5, 128, 128 * (t % 4)).rearrange("p (u g d) -> p u g d", u=UNITS, g=HQ),
                                            row("L1x_bv").rearrange("p (u g d) -> p u g d", u=UNITS, g=HQ),
                                            ALU.add).then_inc(sem("v_added"), 1)
                    v.wait_ge(sem("exp0"), n + 1 + 1)
                    v.reciprocal(rinv[:, s:s + 1], rsum[:, s:s + 1]).then_inc(sem("rinv0"), 1)
                    v.wait_ge(sem("rinv0"), n + 1)
                    v.wait_ge(sem("y0"), n + 1)
                    xb = xN_flat[:, bass.ds(n * 128, 128)]
                    v.scalar_tensor_tensor(out=xb, in0=bank(7, 128, 128), scalar=rinv[:, s:s + 1],
                                           in1=x_bv[:, bass.ds(n * 128, 128)], op0=ALU.mult, op1=ALU.add
                                           ).then_inc(sem("x0_new"), 1)

        def l0x_pool(g):
            g.memset(neg_half[:, :], -0.5).then_inc(sem("pool_const"), 1)
            g.wait_ge(sem("pool_const"), 1)
            ln_pool(g, 0)
            l0a_prepare_pool(g)
            x1_early_pool(g)
            g.wait_ge(sem("in_mask1"), 16)
            g.tensor_scalar(mask1_r, mask1_f, -1.0e9, None, ALU.mult).then_inc(sem("mask1_c"), 1)
            for j in range(3):
                g.wait_ge(sem("mask1_c"), 2 * j + 1)
                g.tensor_copy(mparts[:, j, :], mask1_r).then_inc(sem("mask1_c"), 1)
                if j < 2:
                    g.wait_ge(sem("mask1_c"), 2 * j + 2)
                    g.tensor_tensor(mask1_r, mask1_r, mparts[:, j, :], ALU.subtract).then_inc(sem("mask1_c"), 1)
            g.wait_ge(sem("mask1_c"), 6)
            for j in range(3):
                g.dma_start(mask_parts_d[j].rearrange("b (p n) -> (b p) n", n=64), mparts[:, j, :]
                            ).then_inc(sem("mask1_out"), 16)
            g.wait_ge(sem("v_ones"), 2)
            with g.Fori(0, B // 2) as it:
                for s in range(2):
                    n = it * 2 + s
                    for c in range(4):
                        at = slice(c * BANK, (c + 1) * BANK)
                        g.wait_ge(sem("k2_done"), n * 4 + c + 1)
                        g.tensor_tensor(k_parts[s][:, 2, at], k_rest[c % 2], k_parts[s][:, 1, at], ALU.subtract
                                        ).then_inc(sem("k3_done"), 1)

        w_norm, r_scale, om = small[:, 64:68], small[:, 72:76], small[:, 80:82]
        half = small[:, 84:88]
        a_mx, a_sum, a_r = small[:, 88:92], small[:, 92:96], small[:, 96:100]
        wn, wnT, vT_a = tE[:, 0:512], tF[:, 0:512], tE[:, 512:1024]
        head_sq, head_n, head_w, head_r = (tB[:, 128 * i_:128 * i_ + 128] for i_ in range(4))
        RES = 0.5 / math.sqrt(0.5)
        EPS_W = 1e-4

        def l0a_prepare_dve(v):
            v.wait_ge(sem("in_mats"), 16)
            for i_, n_ in enumerate(["L0a_q", "L0a_k", "L0a_v", "L0a_o"]):
                v.tensor_tensor_reduce(tF[:, 512 + 128 * i_:640 + 128 * i_], mat(n_), mat(n_), 1.0, 0.0,
                                       ALU.mult, ALU.add, w_norm[:, i_:i_ + 1]).then_inc(sem_of("a_wsq"), 1)

        def l0a_prepare_pool(g):
            g.memset(half, 0.5).then_inc(sem_of("a_half"), 1)
            g.wait_ge(*step("a_half", 1))
            g.wait_ge(*step("a_wsq", 4))
            g.tensor_tensor(w_norm, w_norm, half, ALU.pow).then_inc(sem_of("a_wroot"), 1)
            g.wait_ge(*step("a_wroot", 1))
            g.tensor_scalar(w_norm, w_norm, SQ_D, EPS_W, ALU.mult, ALU.add).then_inc(sem_of("a_w"), 1)

        def l0a_dve(v):
            v.wait_ge(*step("a_w", 1))
            v.reciprocal(r_scale, w_norm).then_inc(sem_of("a_rw"), 1)
            v.wait_ge(*step("a_rw", 1))
            v.tensor_scalar(r_scale, r_scale, col("gain"), SQ_D, ALU.mult, ALU.mult).then_inc(sem_of("a_rw"), 1)
            v.wait_ge(*step("a_rw", 2))
            for i_, n_ in enumerate(["L0a_q", "L0a_k", "L0a_v", "L0a_o"]):
                v.tensor_scalar(wn[:, 128 * i_:128 * i_ + 128], mat(n_), r_scale[:, i_:i_ + 1], None, ALU.mult
                                ).then_inc(sem_of("a_wn"), 1)
            ln_dve(v, 1, (sem("x0_new"), B + 1))
            v.wait_ge(sem("ln_xh"), 1 * B + B)
            v.scalar_tensor_tensor(out=xN_flat, in0=xhN[:, :, :].rearrange("p b d -> p (b d)"), scalar=RES,
                                   in1=xN_flat, op0=ALU.mult, op1=ALU.add).then_inc(sem_of("a_res"), 1)
            v.wait_ge(*step("a_sq", 1))
            v.tensor_reduce(head_sq, tA[:, :].rearrange("p (g d) -> p g d", d=HD), AX.X, ALU.add
                            ).then_inc(sem_of("a_headsq"), 1)
            v.wait_ge(*step("a_headn", 1))
            v.tensor_scalar(head_w, head_n, EPS_W, None, ALU.add).then_inc(sem_of("a_headw"), 1)
            v.wait_ge(*step("a_headw", 1))
            v.reciprocal(head_r, head_w).then_inc(sem_of("a_headr"), 1)
            v.wait_ge(*step("a_headr", 1))
            v.tensor_tensor(tC[:, :].rearrange("p (g d) -> p g d", d=HD),
                            ps[:, 2 * BANK:4 * BANK].rearrange("p (g d) -> p g d", d=HD), bc_in(head_r, HD),
                            ALU.mult).then_inc(sem_of("a_qkn"), 1)
            v.wait_ge(*step("a_scores", 1))
            v.tensor_tensor(b3(tD[:, 0:512]), b3(bank(5)), bc_mid(const("off_block"), B), ALU.add
                            ).then_inc(sem_of("a_masked"), 1)
            v.wait_ge(*step("a_masked", 1))
            v.tensor_reduce(a_mx, b3(tD[:, 0:512]), AX.X, ALU.max).then_inc(sem_of("a_max"), 1)
            v.wait_ge(*step("a_max", 1))
            v.tensor_tensor(b3(tD[:, 0:512]), b3(tD[:, 0:512]), bc_in(a_mx, 128), ALU.subtract
                            ).then_inc(sem_of("a_shifted"), 1)
            v.wait_ge(*step("a_exp", 1))
            v.tensor_reduce(a_sum, b3(tD[:, 512:1024]), AX.X, ALU.add).then_inc(sem_of("a_sum"), 1)
            v.wait_ge(*step("a_sum", 1))
            v.reciprocal(a_r, a_sum).then_inc(sem_of("a_rsum"), 1)
            v.wait_ge(*step("a_rsum", 1))
            v.tensor_tensor(b3(tD[:, 0:512]), b3(tD[:, 512:1024]), bc_in(a_r, 128), ALU.mult
                            ).then_inc(sem_of("a_probs"), 1)
            v.wait_ge(*step("a_out", 1))
            v.wait_ge(*step("a_res", 1))
            v.scalar_tensor_tensor(out=xN_flat, in0=bank(7), scalar=RES, in1=xN_flat, op0=ALU.mult, op1=ALU.add
                                   ).then_inc(sem("x1_new"), 1)

        def l0a_pe(pe):
            pe.wait_ge(*step("a_wn", 4))
            transpose4_pe(pe, b3(wn), 0, step("a_wn", 4), sem_of("a_wnt"))
            transpose4_pe(pe, xhN, 1, (sem("ln_xh"), 1 * B + B), sem("ln_t"))
            pe.wait_ge(*step("a_wnT", 1))
            pe.wait_ge(sem("ln_T"), 2)
            for b in range(B):
                m = pe.matmul(bank(2 + b // 2, 256, 256 * (b % 2)), xhT[:, b * S:(b + 1) * S], wnT[:, 0:256],
                              start=True, stop=True)
            m.then_inc(sem_of("a_qk"), 1)
            pe.matmul(bank(4), wnT[:, 256:384], xhT[:, :], start=True, stop=True).then_inc(sem_of("a_v"), 1)
            pe.wait_ge(*step("a_qkn", 1))
            for b in range(B):
                m = pe.matmul(bank(5, 128, 128 * b), tC[:, 256 * b:256 * b + 128], tC[:, 256 * b + 128:256 * b + 256],
                              start=True, stop=True)
            m.then_inc(sem_of("a_scores"), 1)
            pe.wait_ge(*step("a_probs", 1))
            for b in range(B):
                m = pe.matmul(bank(6, 128, 128 * b), tD[:, 128 * b:128 * b + 128], wnT[:, 384:512],
                              start=True, stop=True)
            m.then_inc(sem_of("a_mo"), 1)
            pe.wait_ge(*step("a_vT", 1))
            pe.wait_ge(*step("a_mo_sb", 1))
            for b in range(B):
                m = pe.matmul(bank(7, 128, 128 * b), vT_a[:, b * S:(b + 1) * S], tA[:, 128 * b:128 * b + 128],
                              start=True, stop=True)
            m.then_inc(sem_of("a_out"), 1)

        def l0a_act(act):
            act.wait_ge(*step("a_wnt", 1))
            act.activation(wnT, bank(0), ACT.Copy).then_inc(sem_of("a_wnT"), 1)
            act.wait_ge(sem("ln_t"), 2)
            act.activation(xhT[:, :], bank(1), ACT.Copy).then_inc(sem("ln_T"), 1)
            act.wait_ge(*step("a_qk", 1))
            act.activation(tA[:, :], ps[:, 2 * BANK:4 * BANK], ACT.Square).then_inc(sem_of("a_sq"), 1)
            act.wait_ge(*step("a_v", 1))
            act.activation(vT_a, bank(4), ACT.Copy).then_inc(sem_of("a_vT"), 1)
            act.wait_ge(*step("a_headsq", 1))
            act.activation(head_n, head_sq, ACT.Sqrt, scale=1.0 / HD).then_inc(sem_of("a_headn"), 1)
            act.wait_ge(*step("a_shifted", 1))
            act.activation(tD[:, 512:1024], tD[:, 0:512], ACT.Exp, scale=1.0 / math.sqrt(S)).then_inc(sem_of("a_exp"), 1)
            act.wait_ge(*step("a_mo", 1))
            act.activation(tA[:, 0:512], bank(6), ACT.Copy).then_inc(sem_of("a_mo_sb"), 1)

        x_pad = mask_sb[:, 0:B * (S + 1)].rearrange("p (b s) -> p b s", s=S + 1)
        x_r, x_k = tB[:, 0:512], tB[:, 512:1024]

        def l0f_pool(g):
            g.wait_ge(sem("x0_new"), B + 1)
            g.memset(x_pad[:, :, 0:1], 0.0).then_inc(sem_of("f_zero"), 1)
            g.tensor_scalar(om, C[:, 3:5], -1.0, 1.0, ALU.mult, ALU.add).then_inc(sem_of("f_om"), 1)

        def l0f_dve(v):
            ln_dve(v, 2, (sem("x1_new"), 1))
            v.wait_ge(*step("f_om", 1))
            v.wait_ge(*step("f_zero", 1))
            v.wait_ge(sem("ln_T"), 3)
            for i_, dst in enumerate((x_r, x_k)):
                v.tensor_scalar(b3(tC[:, 512 * i_:512 * i_ + 512]), x_pad[:, :, 0:S], om[:, i_:i_ + 1], None, ALU.mult
                                ).then_inc(sem_of("f_shift"), 1)
            for i_, dst in enumerate((x_r, x_k)):
                v.wait_ge(*step("f_shift", i_ + 1))
                v.scalar_tensor_tensor(out=b3(dst), in0=x_pad[:, :, 1:S + 1], scalar=C[:, 3 + i_:4 + i_],
                                       in1=b3(tC[:, 512 * i_:512 * i_ + 512]), op0=ALU.mult, op1=ALU.add
                                       ).then_inc(sem_of("f_mix"), 1)
            v.wait_ge(*step("f_r", 1))
            v.tensor_scalar(tE[:, 0:512], bank(1), -87.0, None, ALU.max).then_inc(sem_of("f_clamped"), 1)
            v.wait_ge(*step("f_relu", 1))
            v.tensor_tensor(tD[:, 512:1024], tD[:, 0:512], tD[:, 0:512], ALU.mult).then_inc(sem_of("f_ksq"), 1)
            v.wait_ge(*step("f_exp", 1))
            v.tensor_scalar(tE[:, 0:512], tE[:, 0:512], 1.0, None, ALU.add).then_inc(sem_of("f_gate"), 1)
            v.wait_ge(*step("f_gate", 1))
            v.reciprocal(tE[:, 512:1024], tE[:, 0:512]).then_inc(sem_of("f_gate"), 1)
            v.wait_ge(*step("f_gate", 2))
            v.wait_ge(*step("f_v", 1))
            v.tensor_tensor(tC[:, 0:512], bank(3), tE[:, 512:1024], ALU.mult).then_inc(sem_of("f_out"), 1)
            v.wait_ge(*step("f_out", 1))
            v.tensor_tensor(xN_flat, xN_flat, tC[:, 0:512], ALU.add).then_inc(sem("x2_new"), 1)

        def l0f_pe(pe):
            transpose4_pe(pe, xhN, 0, (sem("ln_xh"), 2 * B + B), sem("ln_t"))
            pe.wait_ge(*step("f_mix", 2))
            for b in range(B):
                m = pe.matmul(bank(1, 128, 128 * b), x_r[:, b * S:(b + 1) * S], mat("L0f_rT"), start=True, stop=True)
            m.then_inc(sem_of("f_r"), 1)
            pe.matmul(bank(2), mat("L0f_kT"), x_k, start=True, stop=True).then_inc(sem_of("f_k"), 1)
            pe.wait_ge(*step("f_ksq", 1))
            for b in range(B):
                m = pe.matmul(bank(3, 128, 128 * b), tD[:, 512 + b * S:512 + (b + 1) * S], mat("L0f_vT"),
                              start=True, stop=True)
            m.then_inc(sem_of("f_v"), 1)

        def l0f_act(act):
            act.wait_ge(sem("ln_t"), 3)
            act.wait_ge(*step("f_zero", 1))
            act.activation(x_pad[:, :, 1:S + 1], b3(bank(0)), ACT.Copy).then_inc(sem("ln_T"), 1)
            act.wait_ge(*step("f_k", 1))
            act.activation(tD[:, 0:512], bank(2), ACT.Relu).then_inc(sem_of("f_relu"), 1)
            act.wait_ge(*step("f_clamped", 1))
            act.activation(tE[:, 0:512], tE[:, 0:512], ACT.Exp, scale=-1.0).then_inc(sem_of("f_exp"), 1)

        PV_COLS = HD + 1
        GROUPS = KT // 2
        STEPS = UNITS * GROUPS
        at = 0
        k_slot, p_ring, v_slot, q_slot = [], [], [], []
        for i_ in range(UNITS):
            k_slot.append(arena[:, at:at + KEYS].bitcast(BF16).rearrange("p (g n) -> p g n", g=2))
            at += KEYS
        at = 10240
        for i_ in range(4):
            p_ring.append(arena[:, at:at + 1024])
            at += 1024
        for i_ in range(UNITS):
            v_slot.append(arena[:, at:at + KT * HQ * PV_COLS])
            at += KT * HQ * PV_COLS
        at = 33600
        for i_ in range(UNITS):
            q_slot.append(arena[:, at:at + 256].bitcast(BF16).rearrange("p (g a q) -> p g a q", g=2, a=2))
            at += 256
        q_f, q_rest = tA[:, 0:512], tA[:, 512:1024]
        q_part = tB[:, 0:768].bitcast(BF16).rearrange("p (j n) -> p j n", j=3)
        chunk_max = [tC[:, 16 * i_:16 * i_ + 16] for i_ in range(2)]
        neg_max = [tC[:, 32 + 4 * i_:36 + 4 * i_] for i_ in range(2)]
        m_rest = [tC[:, 40 + 4 * i_:44 + 4 * i_] for i_ in range(2)]
        m_part = [tC[:, 64 + 8 * i_:70 + 8 * i_].bitcast(BF16).rearrange("p (j h) -> p j h", j=3) for i_ in range(2)]
        m_cols = [tC[:, 96 + 32 * i_:114 + 32 * i_].bitcast(BF16).rearrange("p (h c) -> p h c", c=9) for i_ in range(2)]
        o_rcp = tC[:, 180:184]
        m_none = tC[:, 184:188]
        m_none3 = tC[:, 188:194].rearrange("p (g j) -> p g j", j=3)
        o_raw = tC[:, 256:384]
        zeros = tC[:, 384:512]
        o_all = tD[:, 0:512]
        o_T = tE[:, 0:512]
        ONES_PAIR = 1.0019378662109375
        START = {"exp1": 2, "pv_chunk": 4, "pv_copied": 1, "o1_t": 1, "o1_norm": 1}

        def x1_init_pool(g, slots):
            for i_ in slots:
                g.memset(arena[:, i_ * KEYS:(i_ + 1) * KEYS], ONES_PAIR).then_inc(sem("k_ones"), 1)

        def x1_early_pool(g):
            for i_ in range(UNITS):
                g.memset(arena[:, 33600 + 256 * i_:33856 + 256 * i_], 0.0).then_inc(sem("q_zero"), 1)

        def x1_early_dve(v):
            v.wait_ge(sem("q_zero"), UNITS)
            for i_ in range(UNITS):
                v.memset(arena[MASK_ROW:MAX_ROW, 33600 + 256 * i_:33856 + 256 * i_], ONES_PAIR
                         ).then_inc(sem("q_ones"), 1)

        def x1_load(sp, b, u):
            sp.dma_start(k_slot[u][0:MASK_ROW, :, :],
                         k_stack[bass.ds(b, 1), HQ * u:HQ * u + HQ, :, :]
                         .rearrange("o (g a) r n -> (o a r) g n", a=2)).then_inc(sem(f"unit_in{u}"), 16)
            for g_ in range(2):
                sp.dma_start(k_slot[u][MASK_ROW:MAX_ROW, g_, :],
                             mask_parts_d[:, bass.ds(b, 1), :].rearrange("j o n -> j (o n)")
                             ).then_inc(sem(f"unit_in{u}"), 16)
            for a_ in range(2):
                sp.dma_start(q_slot[u][ROWS * a_:ROWS * a_ + ROWS, :, a_, :],
                             q_stack[HQ * u + a_:HQ * u + a_ + 3:2, :, bass.ds(b * S, S)]
                             .rearrange("g r q -> r g q")).then_inc(sem(f"unit_in{u}"), 16)
            sp.dma_start(v_slot[u], v_units[bass.ds(b, 1), u, :, :].rearrange("o k n -> (o k) n")
                         ).then_inc(sem(f"unit_in{u}"), 16)

        def x1_sync(sp):
            for s_ in range(2):
                sp.wait_ge(sem(f"k_out{s_}"), B // 2 * 16 * len(COMBOS) + 1)
                sp.wait_ge(sem(f"v_out{s_}"), B // 2 * 16 + 1)
            sp.wait_ge(sem("mask1_out"), 48)
            sp.wait_ge(sem("k_ones"), UNITS)
            sp.wait_ge(sem("q_ones"), UNITS)
            sp.wait_ge(sem("q_out"), 16 * len(COMBOS))
            for u in range(UNITS):
                x1_load(sp, 0, u)
            with sp.Fori(1, B) as b:
                for u in range(UNITS):
                    sp.wait_ge(sem("pv_chunk"), (b * UNITS - UNITS + u + 1) * GROUPS + START["pv_chunk"])
                    x1_load(sp, b, u)

        def x1_q_store(act):
            act.wait_ge(sem("q1_part"), 3)
            for c, (i_, _) in enumerate(COMBOS):
                act.dma_start(q_stack[:, c * HD:(c + 1) * HD, :], q_part[:, i_, :]
                              ).then_inc(sem("q_out"), 16)

        def rows_chunk(pe, u, i_, m):
            g_, a_, c = i_ // 8, i_ // 4 % 2, i_ % 4
            if not (isinstance(m, int) and m < 2):
                pe.wait_ge(sem("max_done"), m - 1)
            pe.matmul(bank(4 + i_ % 2), q_slot[u][0:MAX_ROW, g_, a_, :], k_slot[u][0:MAX_ROW, g_, c * BANK:(c + 1) * BANK],
                      start=True, stop=True).then_inc(sem("rows_done"), 1)

        def max_rows_pe(pe, u, n):
            pe.wait_ge(sem("m_cols"), 2 * n + 2)
            out_bf = bank(7).bitcast(BF16)
            for h_ in range(HQ):
                t = pe.transpose(out_bf[MASK_ROW:PAIR_ROWS, 128 * h_:128 * h_ + 128], m_cols[u % 2][:, h_, :],
                                 ident_bf[:, :])
            t.then_inc(sem("m_t"), 1)

        def cols_chunk(pe, u, k2, n, N):
            if k2 == 0:
                pe.wait_ge(sem("m_rows"), n + 1)
            pe.wait_ge(sem("exp1"), N - 1 + START["exp1"])
            for kk in range(2):
                kt = 2 * k2 + kk
                for g_ in range(2):
                    m = pe.matmul(ps[:, (N_slot(k2) * 2 + kk) * BANK + 256 * g_:(N_slot(k2) * 2 + kk) * BANK + 256 * g_ + 256],
                                  k_slot[u][0:PAIR_ROWS, g_, kt * 128:kt * 128 + 128],
                                  q_slot[u][0:PAIR_ROWS, g_, :, :].rearrange("p a q -> p (a q)"),
                                  start=True, stop=True)
            m.then_inc(sem("cols_done"), 1)

        def N_slot(k2):
            return k2 % 2

        def values_chunk(pe, u, k2, n, N):
            if k2 == 0:
                pe.wait_ge(sem("pv_copied"), n + START["pv_copied"])
            pe.wait_ge(sem("exp1"), N + 1 + START["exp1"])
            for kk in range(2):
                kt = 2 * k2 + kk
                for h_ in range(HQ):
                    m = pe.matmul(ps[32 * h_:32 * h_ + PV_COLS, 6 * BANK:6 * BANK + 128],
                                  v_slot[u][:, kt * HQ * PV_COLS + h_ * PV_COLS:kt * HQ * PV_COLS + (h_ + 1) * PV_COLS],
                                  p_ring[k2 % 4][:, kk * BANK + 128 * h_:kk * BANK + 128 * h_ + 128],
                                  start=kt == 0, stop=kt == KT - 1)
            m.then_inc(sem("pv_chunk"), 1)

        def out_turn_pe(pe, n):
            pe.wait_ge(sem("pv_copied"), n + 1 + START["pv_copied"])
            pe.wait_ge(sem("o1_norm"), n + START["o1_norm"])
            pe.transpose(bank(7, 128, 256), o_raw, ident).then_inc(sem("o1_t"), 1)

        def x1_pe_batch(pe, b, last):
            for g in range(STEPS):
                u, k2 = g // GROUPS, g % GROUPS
                n, N = b * UNITS + u, b * STEPS + g
                cols_chunk(pe, u, k2, n, N)
                if g > 0:
                    pu, pk = (g - 1) // GROUPS, (g - 1) % GROUPS
                    values_chunk(pe, pu, pk, b * UNITS + pu, N - 1)
                if not last or u < 2:
                    if k2 == 0:
                        ahead = b if u < 2 else b + 1
                        pe.wait_ge(sem(f"unit_in{(u + 2) % UNITS}"), ahead * 96 + 96)
                    for j in range(2):
                        rows_chunk(pe, (u + 2) % UNITS, 2 * k2 + j, b * 64 + 32 + 2 * g + j)
                if k2 == 3 and not (last and u == UNITS - 1):
                    pe.wait_ge(sem("o1_norm"), n - 1 + START["o1_norm"] if u else n + START["o1_norm"])
                    max_rows_pe(pe, (u + 1) % UNITS, n + 1)
                if k2 == 5 and u > 0:
                    if not (last and u == UNITS - 1):
                        pe.wait_ge(sem("m_rows"), n + 2)
                    out_turn_pe(pe, n - 1)
            values_chunk(pe, UNITS - 1, GROUPS - 1, b * UNITS + UNITS - 1, b * STEPS + STEPS - 1)
            out_turn_pe(pe, b * UNITS + UNITS - 1)

        def x1_pe(pe):
            transpose4_pe(pe, xhN, 0, (sem("ln_xh"), 3 * B + B), sem("ln_t"))
            pe.wait_ge(sem("ln_T"), 4)
            pe.matmul(bank(1), mat("L1x_q"), xhT[:, :], start=True, stop=True).then_inc(sem("q1"), 1)
            pe.wait_ge(sem("x1_zeros"), 1)
            pe.matmul(bank(6, 128), zeros, zeros, start=True, stop=True)
            for n in range(2):
                pe.wait_ge(sem(f"unit_in{n}"), 96)
                for i_ in range(16):
                    rows_chunk(pe, n, i_, 16 * n + i_)
            max_rows_pe(pe, 0, 0)
            with pe.Fori(0, B - 1) as b:
                x1_pe_batch(pe, b, False)
            x1_pe_batch(pe, B - 1, True)
            transpose4_pe(pe, b3(o_all), 0, (sem("o1_norm"), B * UNITS + 1), sem("o1_all_t"))
            pe.wait_ge(sem("o1_T"), 1)
            for b in range(B):
                m = pe.matmul(bank(1, 128, 128 * b), o_T[:, 128 * b:128 * b + 128], mat("L1x_o"), start=True, stop=True)
            m.then_inc(sem("y1"), 1)

        def copy_out_act(act, n):
            act.wait_ge(sem("o1_t"), n + START["o1_t"])
            act.wait_ge(sem("pv_chunk"), n * GROUPS + GROUPS + START["pv_chunk"])
            act.activation(o_raw, bank(6, 128), ACT.Copy).then_inc(sem("pv_copied"), 1)

        def x1_act_batch(act, b):
            for g in range(STEPS):
                u, k2 = g // GROUPS, g % GROUPS
                N = b * STEPS + g
                act.wait_ge(sem("cols_done"), N + 1)
                act.wait_ge(sem("pv_chunk"), N - 3 + START["pv_chunk"])
                act.activation(p_ring[k2 % 4], ps[:, 2 * BANK * (k2 % 2):2 * BANK * (k2 % 2) + 2 * BANK], ACT.Exp
                               ).then_inc(sem("exp1"), 1)
                if k2 == 0 and u > 0:
                    copy_out_act(act, b * UNITS + u - 1)
            copy_out_act(act, b * UNITS + UNITS - 1)

        def x1_act(act):
            act.wait_ge(sem("ln_t"), 4)
            act.activation(xhT[:, :], bank(0), ACT.Copy).then_inc(sem("ln_T"), 1)
            x1_q_store(act)
            with act.Fori(0, B - 1) as b:
                x1_act_batch(act, b)
            x1_act_batch(act, B - 1)
            act.wait_ge(sem("o1_all_t"), 1)
            act.activation(o_T, bank(0), ACT.Copy).then_inc(sem("o1_T"), 1)

        def max_chunk(v, u, i_, m):
            v.wait_ge(sem("rows_done"), m + 1)
            v.tensor_reduce(chunk_max[u % 2][:, i_:i_ + 1], bank(4 + i_ % 2), AX.X, ALU.max, negate=True
                            ).then_inc(sem("max_done"), 1)
            if i_ == 15:
                v.wait_ge(sem("max_done"), m + 1)
                v.tensor_reduce(neg_max[u % 2], chunk_max[u % 2].rearrange("p (h c) -> p h c", c=4), AX.X, ALU.min
                                ).then_inc(sem("neg_max"), 1)

        def max_rows_dve(v, u, n):
            v.wait_ge(sem("m_t"), n + 1)
            v.tensor_copy(q_slot[u][MASK_ROW:PAIR_ROWS, :, :, :].rearrange("p g a q -> p (g a q)"),
                          bank(7).bitcast(BF16)[MASK_ROW:PAIR_ROWS, 0:512]).then_inc(sem("m_rows"), 1)

        def norm_out_dve(v, b, u):
            n = b * UNITS + u
            t = bank(7, 128, 256).rearrange("p (h c) -> p h c", c=32)
            v.wait_ge(sem("o1_t"), n + 1 + START["o1_t"])
            v.reciprocal(o_rcp, t[:, :, HD]).then_inc(sem("o1_rcp"), 1)
            v.wait_ge(sem("o1_rcp"), n + 1)
            v.tensor_tensor(o_all[:, bass.ds(b * 128 + u * 32, 32)].rearrange("p (h d) -> p h d", d=HD),
                            t[:, :, 0:HD], bc_in(o_rcp, HD), ALU.mult).then_inc(sem("o1_norm"), 1)

        def x1_dve_batch(v, b, last):
            for g in range(STEPS):
                u, k2 = g // GROUPS, g % GROUPS
                n = b * UNITS + u
                if not last or u < 2:
                    for j in range(2):
                        max_chunk(v, (u + 2) % UNITS, 2 * k2 + j, b * 64 + 32 + 2 * g + j)
                if k2 == 4 and not (last and u == UNITS - 1):
                    max_rows_dve(v, (u + 1) % UNITS, n + 1)
                if k2 == 6 and u > 0:
                    norm_out_dve(v, b, u - 1)
            norm_out_dve(v, b, UNITS - 1)

        def x1_dve(v):
            ln_dve(v, 3, (sem("x2_new"), 1))
            v.wait_ge(sem("q1"), 1)
            v.tensor_scalar(q_f, bank(1), col("L1x_bq"), 1.0 / math.sqrt(HD), ALU.add, ALU.mult
                            ).then_inc(sem("q1_f"), 1)
            for j in range(3):
                v.wait_ge(sem("q1_f"), j + 1)
                v.tensor_copy(q_part[:, j, :], q_f).then_inc(sem("q1_part"), 1)
                if j < 2:
                    v.wait_ge(sem("q1_part"), j + 1)
                    v.tensor_tensor(q_f, q_f, q_part[:, j, :], ALU.subtract).then_inc(sem("q1_f"), 1)
            v.memset(zeros, 0.0).then_inc(sem("x1_zeros"), 1)
            v.wait_ge(sem("in_consts"), 16)
            v.tensor_copy(ident_bf[:, :], ident).then_inc(sem("ident_bf"), 1)
            v.tensor_tensor(xN[:, :, :], xN[:, :, :], bc_mid(row("L1x_bo"), B), ALU.add).then_inc(sem("x1_bo"), 1)
            for n in range(2):
                for i_ in range(16):
                    max_chunk(v, n, i_, 16 * n + i_)
            max_rows_dve(v, 0, 0)
            with v.Fori(0, B - 1) as b:
                x1_dve_batch(v, b, False)
            x1_dve_batch(v, B - 1, True)
            v.wait_ge(sem("y1"), 1)
            v.tensor_tensor(xN_flat, bank(1), xN_flat, ALU.add).then_inc(sem("x3_new"), 1)

        def x1_pool(g):
            g.wait_ge(sem("x2_new"), 1)
            for i_ in range(2):
                g.memset(tC[:, 96 + 32 * i_:114 + 32 * i_], 0.0).then_inc(sem("m_zero"), 1)
            g.memset(tC[:, 184:194], 0.0).then_inc(sem("m_zero"), 1)
            g.wait_ge(sem("m_zero"), 3)
            for i_ in range(2):
                g.memset(m_cols[i_][:, :, 0:3], 1.0).then_inc(sem("m_zero"), 1)
            g.wait_ge(sem("m_zero"), 5)
            with g.Fori(0, B * UNITS // 2) as it:
                for i_ in range(2):
                    n = it * 2 + i_
                    g.wait_ge(sem("neg_max"), n + 1)
                    g.tensor_tensor(m_part[i_][:, 0, :], neg_max[i_], m_none, ALU.add).then_inc(sem("m_split"), 1)
                    g.wait_ge(sem("m_split"), n * 4 + 1)
                    g.tensor_tensor(m_rest[i_], neg_max[i_], m_part[i_][:, 0, :], ALU.subtract).then_inc(sem("m_split"), 1)
                    g.wait_ge(sem("m_split"), n * 4 + 2)
                    g.tensor_tensor(m_part[i_][:, 1, :], m_rest[i_], m_none, ALU.add).then_inc(sem("m_split"), 1)
                    g.wait_ge(sem("m_split"), n * 4 + 3)
                    g.tensor_tensor(m_part[i_][:, 2, :], m_rest[i_], m_part[i_][:, 1, :], ALU.subtract
                                    ).then_inc(sem("m_split"), 1)
                    g.wait_ge(sem("m_split"), n * 4 + 4)
                    for a_ in range(2):
                        g.tensor_tensor(m_cols[i_][:, a_:a_ + 3:2, 3 + 3 * a_:6 + 3 * a_],
                                        m_part[i_][:, :, a_:a_ + 3:2].rearrange("p j g -> p g j"),
                                        m_none3, ALU.add).then_inc(sem("m_cols"), 1)

        (q2T, eq2T, k2T, ek2T, v2T, k_bd, ek_bd, s_sum, p2, p2T, e_dec, mix9, q_b2, eq_b2, m_b2, raw2, amp_w, o2_all,
         o2_T) = carve([512, 512, 512, 512, 512, 2048, 2048, 2048, 2048, 1024, 1024, B * H * 9, 128, 128, H * 9, 512,
                        1024, 512, 512])
        z_all = amp_w[:, 0:128].rearrange("p (b c) -> p b c", c=32)
        e_amp, th, p_abs, s_arg, sin_p, cos_p, c_sin, c_cos = (
            amp_w[:, 128 + 64 * i_:192 + 64 * i_].rearrange("p (b h) -> p b h", h=H) for i_ in range(8))
        mix_v = mix9.rearrange("p (b h e) -> p b h e", b=B, h=H)
        o2_rcp = amp_w[:, 640:656]
        o2_zero = tF[:, 0:512]
        SQ_HD = 1.0 / math.sqrt(HD)
        START.update({"c_scores": 1, "c_sum": 2, "c_exp": 4, "c_pt": 4, "c_ptc": 2, "c_pv": 2, "c_raw": 1, "c_ot": 1,
                      "c_norm": 1})

        def l1a_pe(pe):
            transpose4_pe(pe, xhN, 0, (sem("ln_xh"), 4 * B + B), sem("ln_t"))
            pe.wait_ge(sem("ln_T"), 5)
            for i_, n_ in enumerate(["L1a_vT", "L1a_qT", "L1a_eqT", "L1a_kT", "L1a_ekT"]):
                pe.matmul(bank(1 + i_), mat(n_), xhT[:, :], start=True, stop=True).then_inc(sem_of("b_proj"), 1)
            for b in range(B):
                m = pe.matmul(bank(7, 32, 32 * b), xhT[:, b * S:(b + 1) * S], mat("amp_ph")[:, 0:32],
                              start=True, stop=True)
            m.then_inc(sem_of("b_amp"), 1)
            for b in range(B):
                m = pe.matmul(bank(6, 128, 128 * b), xhT[:, b * S:(b + 1) * S], mat("L1a_vT"), start=True, stop=True)
            m.then_inc(sem_of("b_vn"), 1)
            pe.wait_ge(*step("b_vT", 1))
            pe.wait_ge(*step("b_q", 2))
            for i_, n_ in enumerate(("mix", "mix_rolled")):
                for b in range(B):
                    m = pe.matmul(bank((1, 2)[i_], 128, 128 * b), v2T[:, b * S:(b + 1) * S], mat(n_),
                                  start=True, stop=True)
                m.then_inc(sem_of("b_sup"), 1)
            pe.wait_ge(*step("b_mixed", 1))
            pe.wait_ge(*step("b_k", 2))
            pe.wait_ge(*step("b_zero", 1))
            pe.matmul(bank(6), o2_zero[:, 0:128], o2_zero, start=True, stop=True)

            def scores(b, j):
                n = b * 4 + j
                pe.wait_ge(sem("c_sum"), n - 1 + START["c_sum"])
                pe.matmul(bank(j % 2), eq_b2, ek_bd[:, j * BANK:(j + 1) * BANK], start=True, stop=True)
                pe.matmul(bank(2 + j % 2), q_b2, k_bd[:, j * BANK:(j + 1) * BANK], start=True, stop=True
                          ).then_inc(sem("c_scores"), 1)

            def values(b, j):
                n = b * 4 + j
                pe.wait_ge(sem("c_ptc"), n + 1 + START["c_ptc"])
                for h_ in range(4):
                    m = pe.matmul(ps[32 * h_:32 * h_ + 9, 6 * BANK + 128 * j:6 * BANK + 128 * j + 128],
                                  m_b2[:, (4 * j + h_) * 9:(4 * j + h_) * 9 + 9],
                                  p2T[:, (j % 2) * BANK + 128 * h_:(j % 2) * BANK + 128 * h_ + 128],
                                  start=True, stop=True)
                m.then_inc(sem("c_pv"), 1)

            with pe.Fori(0, B) as b:
                pe.wait_ge(sem("c_qb"), b * 3 + 3)
                pe.wait_ge(sem("c_kbd"), b + 1)
                pe.wait_ge(sem("c_ekbd"), b + 1)
                scores(b, 0)
                scores(b, 1)
                for j in range(4):
                    n = b * 4 + j
                    pe.wait_ge(sem("c_exp"), n + 1 + START["c_exp"])
                    pe.wait_ge(sem("c_ptc"), n - 1 + START["c_ptc"])
                    for h_ in range(4):
                        t = pe.transpose(bank(4 + j % 2, 128, 128 * h_),
                                         p2[:, j * BANK + 128 * h_:j * BANK + 128 * h_ + 128], ident)
                    t.then_inc(sem("c_pt"), 1)
                    if j + 2 < 4:
                        scores(b, j + 2)
                    if j == 0:
                        pe.wait_ge(sem("c_raw"), b + START["c_raw"])
                    else:
                        values(b, j - 1)
                values(b, 3)
                pe.wait_ge(sem("c_raw"), b + 1 + START["c_raw"])
                pe.wait_ge(sem("c_norm"), b + START["c_norm"])
                for j in range(4):
                    t = pe.transpose(bank(7, 128, 128 * j), raw2[:, 128 * j:128 * j + 128], ident)
                t.then_inc(sem("c_ot"), 1)
            transpose4_pe(pe, b3(o2_all), 0, (sem("c_norm"), B + 1), sem_of("c_all_t"))
            pe.wait_ge(*step("c_oT", 1))
            for b in range(B):
                m = pe.matmul(bank(1, 128, 128 * b), o2_T[:, 128 * b:128 * b + 128], mat("L1a_oT"),
                              start=True, stop=True)
            m.then_inc(sem_of("c_out"), 1)

        def l1a_act(act):
            act.wait_ge(sem("ln_t"), 5)
            act.activation(xhT[:, :], bank(0), ACT.Copy).then_inc(sem("ln_T"), 1)
            act.wait_ge(*step("b_proj", 1))
            act.activation(v2T, bank(1), ACT.Identity, bias=col("L1a_bv")).then_inc(sem_of("b_vT"), 1)
            act.wait_ge(*step("b_proj", 5))
            act.activation(k2T, bank(4), ACT.Identity, bias=col("L1a_bk")).then_inc(sem_of("b_k"), 1)
            act.activation(ek2T, bank(5), ACT.Identity, bias=col("L1a_bek")).then_inc(sem_of("b_k"), 1)
            act.wait_ge(*step("b_z", 2))
            act.activation(e_amp, e_amp, ACT.Exp, scale=-1.0).then_inc(sem_of("b_eamp"), 1)
            act.activation(th, z_all[:, :, H:2 * H], ACT.Tanh).then_inc(sem_of("b_tanh"), 1)
            act.wait_ge(*step("b_tanh", 1))
            act.activation(p_abs, th, ACT.Abs, scale=math.pi).then_inc(sem_of("b_abs"), 1)
            act.wait_ge(*step("b_arg", 1))
            act.activation(sin_p, th, ACT.Sin, scale=math.pi).then_inc(sem_of("b_sin"), 1)
            act.activation(cos_p, s_arg, ACT.Sin).then_inc(sem_of("b_sin"), 1)
            act.wait_ge(*step("b_q", 2))
            act.wait_ge(*step("b_mixed", 1))

            def turned(b, j):
                n = b * 4 + j
                act.wait_ge(sem("c_pt"), n + 1 + START["c_pt"])
                act.wait_ge(sem("c_pv"), n - 1 + START["c_pv"])
                act.activation(p2T[:, (j % 2) * BANK:(j % 2) * BANK + BANK], bank(4 + j % 2), ACT.Copy
                               ).then_inc(sem("c_ptc"), 1)

            with act.Fori(0, B) as b:
                act.wait_ge(sem("c_scores"), b * 4 + START["c_scores"])
                act.wait_ge(sem("c_pv"), b * 4 + START["c_pv"])
                act.activation(eq_b2, eq2T[:, bass.ds(b * 128, 128)], ACT.Copy).then_inc(sem("c_qb"), 1)
                act.activation(q_b2, q2T[:, bass.ds(b * 128, 128)], ACT.Copy).then_inc(sem("c_qb"), 1)
                act.activation(m_b2, mix9[:, bass.ds(b * H * 9, H * 9)], ACT.Copy).then_inc(sem("c_qb"), 1)
                for j in range(4):
                    n = b * 4 + j
                    act.wait_ge(sem("c_shift"), n + 1)
                    act.wait_ge(sem("c_pt"), n - 3 + START["c_pt"])
                    act.activation(p2[:, j * BANK:(j + 1) * BANK], s_sum[:, j * BANK:(j + 1) * BANK], ACT.Exp
                                   ).then_inc(sem("c_exp"), 1)
                    if j > 0:
                        turned(b, j - 1)
                turned(b, 3)
                act.wait_ge(sem("c_pv"), b * 4 + 4 + START["c_pv"])
                act.wait_ge(sem("c_ot"), b + START["c_ot"])
                act.activation(raw2, bank(6), ACT.Copy).then_inc(sem("c_raw"), 1)
            act.wait_ge(*step("c_all_t", 1))
            act.activation(o2_T, bank(0), ACT.Copy).then_inc(sem_of("c_oT"), 1)

        def l1a_dve(v):
            ln_dve(v, 4, (sem("x3_new"), 1))
            v.wait_ge(*step("b_proj", 3))
            v.tensor_scalar(q2T, bank(2), col("L1a_bq"), SQ_HD, ALU.add, ALU.mult).then_inc(sem_of("b_q"), 1)
            v.tensor_scalar(eq2T, bank(3), col("L1a_beq"), SQ_HD, ALU.add, ALU.mult).then_inc(sem_of("b_q"), 1)
            v.wait_ge(*step("b_amp", 1))
            v.tensor_tensor(z_all, bank(7, 128).rearrange("p (b c) -> p b c", c=32),
                            bc_mid(row("amp_ph_b")[:, 0:32], B), ALU.add).then_inc(sem_of("b_z"), 1)
            v.wait_ge(*step("b_z", 1))
            v.tensor_scalar(e_amp, z_all[:, :, 0:H], -87.0, None, ALU.max).then_inc(sem_of("b_z"), 1)
            v.wait_ge(*step("b_vn", 1))
            v.tensor_tensor(b3(tE[:, 0:512]), b3(bank(6)), bc_mid(row("L1a_bv"), B), ALU.add).then_inc(sem_of("b_vb"), 1)
            v.wait_ge(*step("b_abs", 1))
            v.tensor_scalar(s_arg, p_abs, -1.0, math.pi / 2, ALU.mult, ALU.add).then_inc(sem_of("b_arg"), 1)
            v.wait_ge(*step("b_eamp", 1))
            v.tensor_scalar(e_amp, e_amp, 1.0, None, ALU.add).then_inc(sem_of("b_amp1"), 1)
            v.wait_ge(*step("b_amp1", 1))
            v.reciprocal(e_amp, e_amp).then_inc(sem_of("b_amp1"), 1)
            v.wait_ge(*step("b_amp1", 2))
            v.tensor_scalar(e_amp, e_amp, 0.3, None, ALU.mult).then_inc(sem_of("b_amp1"), 1)
            v.wait_ge(*step("b_sup", 2))
            v.tensor_tensor(b3(tC[:, 0:512]), b3(bank(1)), bc_mid(row("mix_b"), B), ALU.add).then_inc(sem_of("b_s1"), 1)
            v.tensor_tensor(b3(tD[:, 0:512]), b3(bank(2)), bc_mid(row("mix_b_rolled"), B), ALU.add
                            ).then_inc(sem_of("b_s2"), 1)
            v.wait_ge(*step("b_amp1", 3))
            v.wait_ge(*step("b_sin", 2))
            v.tensor_tensor(c_cos, e_amp, cos_p, ALU.mult).then_inc(sem_of("b_coef"), 1)
            v.tensor_tensor(c_sin, e_amp, sin_p, ALU.mult).then_inc(sem_of("b_coef"), 1)
            v.wait_ge(*step("b_s2", 1))
            v.wait_ge(*step("b_coef", 2))

            def by_head(ap):
                return ap.rearrange("p (g d) -> p g d", d=HD)

            v.tensor_tensor(by_head(tC[:, 0:512]), by_head(tC[:, 0:512]),
                            bc_in(c_cos.rearrange("p b h -> p (b h)"), HD), ALU.mult).then_inc(sem_of("b_t1"), 1)
            v.tensor_tensor(by_head(tD[:, 0:512]), by_head(tD[:, 0:512]),
                            bc_in(c_sin.rearrange("p b h -> p (b h)"), HD), ALU.mult).then_inc(sem_of("b_t2"), 1)
            v.wait_ge(*step("b_t1", 1))
            v.tensor_tensor(tE[:, 0:512], tE[:, 0:512], tC[:, 0:512], ALU.add).then_inc(sem_of("b_t3"), 1)
            v.wait_ge(*step("b_t2", 1))
            v.wait_ge(*step("b_t3", 1))
            v.wait_ge(sem("b_mix_one"), 1)
            v.tensor_tensor(mix9.rearrange("p (g e) -> p g e", e=9)[:, :, 0:HD], by_head(tE[:, 0:512]),
                            by_head(tD[:, 0:512]), ALU.add).then_inc(sem_of("b_mixed"), 1)
            v.memset(o2_zero, 0.0).then_inc(sem_of("b_zero"), 1)
            v.wait_ge(*step("b_k", 2))
            head_cols = const("head_mask")[:, 0:H]
            with v.Fori(0, B) as b:
                v.wait_ge(sem("c_scores"), b * 4 + START["c_scores"])
                v.tensor_tensor(b3(k_bd), bc_mid(k2T[:, bass.ds(b * 128, 128)], H), bc_in(head_cols, 128), ALU.mult
                                ).then_inc(sem("c_kbd"), 1)
                for j in range(4):
                    n = b * 4 + j
                    ss = s_sum[:, j * BANK:(j + 1) * BANK]
                    dec = e_dec[:, (j % 2) * BANK:(j % 2) * BANK + BANK]
                    v.wait_ge(sem("c_scores"), n + 1 + START["c_scores"])
                    v.tensor_tensor(b3(dec), b3(bank(j % 2)), bc_mid(const("decay"), 4), ALU.mult
                                    ).then_inc(sem("c_dec"), 1)
                    v.wait_ge(sem("c_dec"), n + 1)
                    v.wait_ge(sem("c_exp"), n - 3 + START["c_exp"])
                    v.tensor_tensor(ss, bank(2 + j % 2), dec, ALU.add).then_inc(sem("c_sum"), 1)
                    v.wait_ge(sem("c_sum"), n + 1 + START["c_sum"])
                    v.tensor_reduce(amp_w[:, 656 + 4 * j:660 + 4 * j], b3(ss), AX.X, ALU.max).then_inc(sem("c_max"), 1)
                    v.wait_ge(sem("c_max"), n + 1)
                    v.tensor_tensor(b3(ss), b3(ss), bc_in(amp_w[:, 656 + 4 * j:660 + 4 * j], 128), ALU.subtract
                                    ).then_inc(sem("c_shift"), 1)
                v.wait_ge(sem("c_ot"), b + 1 + START["c_ot"])
                t = bank(7).rearrange("p (h c) -> p h c", c=32)
                v.reciprocal(o2_rcp, t[:, :, HD]).then_inc(sem("c_rcp"), 1)
                v.wait_ge(sem("c_rcp"), b + 1)
                v.tensor_tensor(o2_all[:, bass.ds(b * 128, 128)].rearrange("p (h d) -> p h d", d=HD), t[:, :, 0:HD],
                                bc_in(o2_rcp, HD), ALU.mult).then_inc(sem("c_norm"), 1)
            v.tensor_tensor(xhN[:, :, :], xhN[:, :, :], bc_mid(row("L1a_bo"), B), ALU.add).then_inc(sem_of("c_bo"), 1)
            v.wait_ge(*step("c_bo", 1))
            v.wait_ge(*step("c_out", 1))
            v.tensor_tensor(tA[:, 0:512], bank(1), xhN[:, :, :].rearrange("p b d -> p (b d)"), ALU.add
                            ).then_inc(sem_of("c_res"), 1)
            ln_dve(v, 5, step("c_res", 1), src=b3(tA[:, 0:512]), dst=b3(tB[:, 0:512]))
            v.wait_ge(sem("ln_xh"), 5 * B + B)
            v.tensor_tensor(b3(tB[:, 0:512]), b3(tB[:, 0:512]), bc_mid(row("L1a_ln_g"), B), ALU.mult
                            ).then_inc(sem_of("c_gain"), 1)
            v.tensor_tensor(xN[:, :, :], xN[:, :, :], bc_mid(row("L1a_ln_b"), B), ALU.add).then_inc(sem_of("c_shiftb"), 1)
            v.wait_ge(*step("c_gain", 1))
            v.wait_ge(*step("c_shiftb", 1))
            v.tensor_tensor(xN_flat, xN_flat, tB[:, 0:512], ALU.add).then_inc(sem("x4_new"), 1)

        def l1a_pool(g):
            ln_pool(g, 4)
            g.memset(mix_v[:, :, :, HD], 1.0).then_inc(sem("b_mix_one"), 1)
            g.wait_ge(*step("b_k", 2))
            with g.Fori(0, B) as b:
                g.wait_ge(sem("c_scores"), b * 4 + START["c_scores"])
                g.tensor_tensor(b3(ek_bd), bc_mid(ek2T[:, bass.ds(b * 128, 128)], H),
                                bc_in(const("head_mask")[:, 0:H], 128), ALU.mult).then_inc(sem("c_ekbd"), 1)
            ln_pool(g, 5)

        w_slot = [arena[:, 34700 + 1024 * i_:35724 + 1024 * i_] for i_ in range(2)]
        (xn2N, xn2T, xe0, xe1, h0, h1, oh_T) = carve([512, 512, 512, 512, 2048, 2048, 512])
        x_e, h_e = [xe0, xe1], [h0, h1]
        aff = small[:, 104:136].rearrange("p (b e) -> p b e", e=NE)
        score = small[:, 136:168].rearrange("p (b e) -> p b e", e=NE)
        gate = small[:, 168:200].rearrange("p (b e) -> p b e", e=NE)
        top, s_top, alpha = small[:, 200:204], small[:, 204:208], small[:, 208:212]
        START.update({"e_relu": 4, "e_y": 2, "e_acc": 1, "e_h": 1, "e_x": 1})

        def l1f_sync(sp):
            sp.wait_ge(sem("x3_new"), 1)
            with sp.Fori(0, NE // 2) as it:
                for s in range(2):
                    sp.wait_ge(sem("e_y"), it * 2 + s - 1 + START["e_y"])
                    sp.dma_start(w_slot[s][:, 0:512], w1[bass.ds(it * 2 + s, 1), :, :].rearrange("o d f -> (o d) f")
                                 ).then_inc(sem(f"in_w{s}"), 16)
                    sp.dma_start(w_slot[s][:, 512:1024].rearrange("p (t d) -> p t d", d=D),
                                 w2[bass.ds(it * 2 + s, 1), :, :].rearrange("o (t p) d -> p (o t) d", p=128)
                                 ).then_inc(sem(f"in_w{s}"), 16)

        def l1f_pe(pe):
            transpose4_pe(pe, xhN, 0, (sem("ln_xh"), 6 * B + B), sem("ln_t"))
            pe.wait_ge(sem("ln_T"), 6)
            pe.wait_ge(sem("in_experts"), 48)
            for b in range(B):
                m = pe.matmul(bank(1, NE, NE * b), xhT[:, b * S:(b + 1) * S], CT[:, :], start=True, stop=True)
            m.then_inc(sem_of("d_aff"), 1)
            transpose4_pe(pe, b3(xn2N), 2, (sem("ln_xh"), 7 * B + B), sem("ln_t"))
            pe.wait_ge(*step("d_gate", 1))
            for b in range(B):
                t = pe.transpose(ps[0:NE, 3 * BANK + 128 * b:3 * BANK + 128 * b + 128], gate[:, b, :], ident)
            t.then_inc(sem_of("d_gate_t"), 1)
            pe.wait_ge(*step("d_gate_T", 1))
            for b in range(B):
                m = pe.matmul(bank(7, 128, 128 * b), oh_T[0:NE, 128 * b:128 * b + 128], B2[:, :], start=True, stop=True)
            m.then_inc(sem_of("d_b2"), 1)
            pe.wait_ge(sem("ln_T"), 7)
            with pe.Fori(0, NE // 2) as it:
                for s in range(2):
                    e = it * 2 + s
                    pe.wait_ge(sem(f"in_w{s}"), it * 32 + 32)
                    pe.wait_ge(sem("e_x"), e + 1 + START["e_x"])
                    for t in range(FT):
                        pe.wait_ge(sem("e_relu"), e * FT + t - 3 + START["e_relu"])
                        pe.matmul(bank(t), w_slot[s][:, 128 * t:128 * t + 128], x_e[s], start=True, stop=True
                                  ).then_inc(sem("e_h"), 1)
                    pe.wait_ge(sem("e_relu"), e * FT + FT + START["e_relu"])
                    pe.wait_ge(sem("e_acc"), e * B + START["e_acc"])
                    for b in range(B):
                        for t in range(FT):
                            m = pe.matmul(bank(4 + s, 128, 128 * b), h_e[s][:, BANK * t + 128 * b:BANK * t + 128 * b + 128],
                                          w_slot[s][:, 512 + 128 * t:640 + 128 * t], start=t == 0, stop=t == FT - 1)
                    m.then_inc(sem("e_y"), 1)

        def l1f_act(act):
            act.wait_ge(sem("ln_t"), 6)
            act.activation(xhT[:, :], bank(0), ACT.Copy).then_inc(sem("ln_T"), 1)
            act.wait_ge(sem("ln_t"), 7)
            act.activation(xn2T, bank(2), ACT.Copy).then_inc(sem("ln_T"), 1)
            act.wait_ge(*step("d_clamp", 1))
            act.activation(alpha, alpha, ACT.Exp, scale=-1.0).then_inc(sem_of("d_exp"), 1)
            act.wait_ge(*step("d_gate_t", 1))
            act.activation(oh_T[0:NE, :], ps[0:NE, 3 * BANK:4 * BANK], ACT.Copy).then_inc(sem_of("d_gate_T"), 1)
            with act.Fori(0, NE // 2) as it:
                for s in range(2):
                    e = it * 2 + s
                    act.wait_ge(sem("e_y"), e - 1 + START["e_y"])
                    for t in range(FT):
                        act.wait_ge(sem("e_h"), e * FT + t + 1 + START["e_h"])
                        act.activation(h_e[s][:, BANK * t:BANK * t + BANK], bank(t), ACT.Relu,
                                       bias=EC[:, bass.ds(2 * NE + e * FT + t, 1)]).then_inc(sem("e_relu"), 1)

        def l1f_dve(v):
            ln_dve(v, 6, (sem("x4_new"), 1))
            v.wait_ge(sem("ln_xh"), 6 * B + B)
            v.tensor_tensor(xN[:, :, :], xN[:, :, :], xhN[:, :, :], ALU.add).then_inc(sem_of("d_res"), 1)
            ln_dve(v, 7, step("d_res", 1), src=xhN[:, :, :], dst=b3(xn2N))
            v.wait_ge(*step("d_aff", 1))
            v.tensor_copy(aff, bank(1, NE * B).rearrange("p (b e) -> p b e", e=NE)).then_inc(sem_of("d_top"), 1)
            v.wait_ge(*step("d_top", 1))
            v.tensor_reduce(top, aff, AX.X, ALU.max).then_inc(sem_of("d_top"), 1)
            v.wait_ge(*step("d_top", 2))
            v.tensor_scalar(alpha, top, -87.0, None, ALU.max).then_inc(sem_of("d_clamp"), 1)
            v.tensor_tensor(score, aff, bc_in(top, NE), ALU.is_equal).then_inc(sem_of("d_sel"), 1)
            v.wait_ge(*step("d_sel", 1))
            v.tensor_tensor(score, score, bc_mid(const("first_weight")[:, 0:NE], B), ALU.mult).then_inc(sem_of("d_sel"), 1)
            v.wait_ge(*step("d_sel", 2))
            v.tensor_reduce(s_top, score, AX.X, ALU.max).then_inc(sem_of("d_sel"), 1)
            v.wait_ge(*step("d_sel", 3))
            v.tensor_tensor(gate, score, bc_in(s_top, NE), ALU.is_equal).then_inc(sem_of("d_sel"), 1)
            v.wait_ge(*step("d_exp", 1))
            v.tensor_scalar(alpha, alpha, 1.0, None, ALU.add).then_inc(sem_of("d_al"), 1)
            v.wait_ge(*step("d_al", 1))
            v.reciprocal(alpha, alpha).then_inc(sem_of("d_al"), 1)
            v.wait_ge(*step("d_al", 2))
            v.wait_ge(*step("d_sel", 4))
            v.tensor_tensor(gate, gate, bc_in(alpha, NE), ALU.mult).then_inc(sem_of("d_gate"), 1)
            v.wait_ge(*step("d_b2", 1))
            v.wait_ge(*step("d_res", 1))
            v.tensor_tensor(xN_flat, xN_flat, bank(7), ALU.add).then_inc(sem("e_acc"), B)
            v.wait_ge(sem("ln_T"), 7)
            with v.Fori(0, NE // 2) as it:
                for s in range(2):
                    e = it * 2 + s
                    v.wait_ge(sem("e_h"), it * 2 * FT + START["e_h"])
                    v.tensor_scalar(x_e[s], xn2T, EC[:, bass.ds(e, 1)], EC[:, bass.ds(NE + e, 1)], ALU.mult, ALU.add
                                    ).then_inc(sem("e_x"), 1)
                for s in range(2):
                    e = it * 2 + s
                    v.wait_ge(sem("e_y"), e + 1 + START["e_y"])
                    for b in range(B):
                        v.wait_ge(sem("e_acc"), e * B + b + 1 + START["e_acc"])
                        v.scalar_tensor_tensor(out=xN[:, b, :], in0=bank(4 + s, 128, 128 * b),
                                               scalar=small[:, bass.ds(168 + b * NE + e, 1)], in1=xN[:, b, :],
                                               op0=ALU.mult, op1=ALU.add).then_inc(sem("e_acc"), 1)

        def l1f_pool(g):
            ln_pool(g, 6)
            ln_pool(g, 7)

        block = stack.enter_context(nc.Block())

        @block.sync
        def _(sp):
            l0x_sync(sp)
            x1_sync(sp)
            l1f_sync(sp)
            sp.wait_ge(sem("e_acc"), (NE + 1) * B + START["e_acc"])
            sp.wait_ge(sem("in_experts"), 48)
            sp.dma_start(out.rearrange("b s d -> s b d"), xN[:, :, :]).then_inc(sem("out"), 16)
            sp.wait_ge(sem("out"), 16)

        @block.tensor
        def _(pe):
            l0x_pe(pe)
            l0a_pe(pe)
            l0f_pe(pe)
            x1_pe(pe)
            l1a_pe(pe)
            l1f_pe(pe)

        @block.scalar
        def _(act):
            l0x_act(act)
            l0a_act(act)
            l0f_act(act)
            x1_act(act)
            l1a_act(act)
            l1f_act(act)

        @block.vector
        def _(v):
            l0x_dve(v)
            l0a_dve(v)
            l0f_dve(v)
            x1_dve(v)
            l1a_dve(v)
            l1f_dve(v)

        @block.gpsimd
        def _(g):
            l0x_pool(g)
            l0f_pool(g)
            ln_pool(g, 1)
            x1_init_pool(g, (0, 1))
            ln_pool(g, 2)
            x1_init_pool(g, (2, 3))
            ln_pool(g, 3)
            x1_pool(g)
            l1a_pool(g)
            l1f_pool(g)


def kernel(**inputs):
    import numpy as np
    import concourse.bacc as bacc
    from concourse.bass_utils import run_bass_kernel_spmd

    a = {n: np.asarray(v) for n, v in inputs.items()}

    def stacked(parts, axis):
        return np.ascontiguousarray(np.stack(parts, axis=axis))

    mix = np.zeros((H, HD, H, HD), np.float32)
    for h in range(H):
        mix[h, :, h, :] = a["L1_attn_mix_w"][h].T
    mats = {
        "L0x_q": a["L0_xattn_kernel_q"], "L0x_kT": a["L0_xattn_kernel_k"].T, "L0x_v": a["L0_xattn_kernel_v"],
        "L0a_q": a["L0_attn_w_q"], "L0a_k": a["L0_attn_w_k"], "L0a_v": a["L0_attn_w_v"], "L0a_o": a["L0_attn_w_o"],
        "L0f_rT": a["L0_ffn_W_r"].T, "L0f_kT": a["L0_ffn_W_k"].T, "L0f_vT": a["L0_ffn_W_v"].T,
        "L1x_q": a["L1_xattn_Wq"], "L1x_k": a["L1_xattn_Wk"], "L1x_v": a["L1_xattn_Wv"], "L1x_o": a["L1_xattn_Wo"],
        "L1a_qT": a["L1_attn_Wq"].T, "L1a_kT": a["L1_attn_Wk"].T, "L1a_vT": a["L1_attn_Wv"].T,
        "L1a_oT": a["L1_attn_Wo"].T, "L1a_eqT": a["L1_attn_Weq"].T, "L1a_ekT": a["L1_attn_Wek"].T,
        "mix": mix.reshape(D, D), "mix_rolled": np.roll(mix, 1, axis=3).reshape(D, D),
        "amp_ph": np.concatenate([a["L1_attn_amp_w"], a["L1_attn_ph_w"], np.zeros((96, D), np.float32)]).T,
    }
    cols = {
        "L0x_bq": a["L0_xattn_bias_q"], "L0x_bk": a["L0_xattn_bias_k"], "gain": np.broadcast_to(a["L0_attn_gain"], (D,)),
        "mu_r": a["L0_ffn_mu_r"], "mu_k": a["L0_ffn_mu_k"], "L1x_bq": a["L1_xattn_bq"], "L1x_bk": a["L1_xattn_bk"],
        "L1a_bq": a["L1_attn_bq"], "L1a_bk": a["L1_attn_bk"], "L1a_bv": a["L1_attn_bv"],
        "L1a_beq": a["L1_attn_beq"], "L1a_bek": a["L1_attn_bek"],
    }
    rows = {
        "L0x_bv": a["L0_xattn_bias_v"], "L1x_bv": a["L1_xattn_bv"], "L1x_bo": a["L1_xattn_bo"],
        "L1a_bv": a["L1_attn_bv"], "L1a_bo": a["L1_attn_bo"], "L1a_ln_g": a["L1_attn_ln_g"],
        "L1a_ln_b": a["L1_attn_ln_b"], "mix_b": a["L1_attn_mix_b"].reshape(D),
        "mix_b_rolled": np.roll(a["L1_attn_mix_b"], 1, axis=1).reshape(D),
        "amp_ph_b": np.concatenate([a["L1_attn_amp_b"], a["L1_attn_ph_b"], np.zeros(96, np.float32)]),
    }
    expert_cols = np.concatenate([a["L1_ffn_ln_g"].T, a["L1_ffn_ln_b"].T,
                                  a["L1_ffn_b1"].reshape(NE * FT, 128).T], axis=1)
    i = np.arange(128)
    first = np.zeros((128, 128))
    first[:, 0:NE] = NE - np.arange(NE)
    consts = {
        "identity": np.eye(128),
        "off_block": np.where(i[:, None] // HD == i[None, :] // HD, 0.0, -1.0e30),
        "head_mask": i[:, None] // HD == i[None, :],
        "decay": 0.5 * np.exp(-0.1 * np.abs(i[:, None] - i[None, :])),
        "first_weight": first,
    }
    arrays = {
        "x": a["x"], "ctx": a["ctx_1024"], "ctx_t": a["ctx_1024"].transpose(0, 2, 1),
        "mask0": a["mask_1xSxS2_ff0"].reshape(S, KEYS), "mask1": a["mask_Bx1x1xS2_fk0"].reshape(128, 64),
        "mats": stacked([mats[n] for n in MATS], 1), "cols": stacked([cols[n] for n in COLS], 1),
        "expert_cols": expert_cols, "rows": stacked([rows[n] for n in ROWV], 0),
        "centroids_t": a["L1_ffn_centroids"].T, "b2": a["L1_ffn_b2"], "w1": a["L1_ffn_w1"], "w2": a["L1_ffn_w2"],
        "consts": stacked([consts[n] for n in CONSTS], 1).astype(np.float32),
    }
    nc = bacc.Bacc("TRN2", target_bir_lowering=False, num_devices=1)
    given, args = {}, []
    for name, v in arrays.items():
        v = np.ascontiguousarray(v)
        given["in_" + name] = v
        args.append(nc.dram_tensor("in_" + name, v.shape, mybir.dt.from_np(v.dtype), kind="ExternalInput").ap())
    args.append(nc.dram_tensor("out_0", (B, S, D), F32, kind="ExternalOutput").ap())
    build(nc, *args)
    r = run_bass_kernel_spmd(nc, [given], core_ids=[0])
    return r.results[0]["out_0"]
```

```python
from contextlib import ExitStack
import math

import concourse.bass as bass
from concourse import mybir

F32 = mybir.dt.float32
BF16 = mybir.dt.bfloat16
ALU = mybir.AluOpType
ACT = mybir.ActivationFunctionType
AX = mybir.AxisListType

B, S, D = 4, 128, 128
KEYS = 2048
KT = KEYS // 128
H, HD = 16, 8
BANK = 512
NE, FF = 8, 512
FT = FF // 128
HQ = 4
UNITS = H // HQ
COMBOS = [(0, 0), (1, 0), (2, 0), (0, 1), (1, 1), (0, 2)]
ROWS = len(COMBOS) * HD
Q_STORES = [((0, 3), (0, 3)), ((0, 2), (3, 5)), ((0, 1), (5, 6))]
K_STORES = [(0, (0, 3)), (1, (3, 5)), (2, (5, 6))]
MASK_ROW = 2 * ROWS
MAX_ROW = MASK_ROW + 3
PAIR_ROWS = MAX_ROW + 6
MATS = ["L0x_q", "L0x_kT", "L0x_v", "L1x_k", "L1x_v",
        "L0a_q", "L0a_k", "L0a_v", "L0a_o", "L0f_rT", "L0f_kT", "L0f_vT", "L1x_q", "L1x_o", "L1a_qT", "L1a_kT", "L1a_vT", "L1a_oT", "L1a_eqT", "L1a_ekT",
        "mix", "mix_rolled", "amp_ph"]
COLS = ["L0x_bq", "L0x_bk", "gain", "mu_r", "mu_k", "L1x_bq", "L1x_bk",
        "L1a_bq", "L1a_bk", "L1a_bv", "L1a_beq", "L1a_bek"]
ROWV = ["L0x_bv", "L1x_bv", "L1x_bo", "L1a_bv", "L1a_bo", "L1a_ln_g", "L1a_ln_b", "mix_b", "mix_b_rolled",
        "amp_ph_b"]
CONSTS = ["identity", "off_block", "head_mask", "decay", "first_weight"]


def build(nc, x, ctx, ctx_t, mask0, mask1, mats, cols, expert_cols, rows, centroids_t, b2, w1, w2,
          consts, out):
    with ExitStack() as stack:
        def sb(name, shape, dt=F32):
            return stack.enter_context(nc.sbuf_tensor(name, shape, dt))

        made = {}

        def sem(name):
            if name not in made:
                made[name] = stack.enter_context(nc.semaphore(name))
            return made[name]

        LINES = {
            "attn0_dve": [("a_wsq", 4), ("a_rw", 2), ("a_wn", 4), ("a_res", 1), ("a_headsq", 1), ("a_headw", 1),
                ("a_headr", 1), ("a_qkn", 1), ("a_masked", 1), ("a_max", 1), ("a_shifted", 1), ("a_sum", 1),
                ("a_rsum", 1), ("a_probs", 1)],
            "attn0_pe": [("a_wnt", 1), ("a_qk", 1), ("a_v", 1), ("a_scores", 1), ("a_mo", 1), ("a_out", 1)],
            "attn0_act": [("a_wnT", 1), ("a_sq", 1), ("a_vT", 1), ("a_headn", 1), ("a_exp", 1), ("a_mo_sb", 1)],
            "attn0_pool": [("a_half", 1), ("a_wroot", 1), ("a_w", 1)],
            "ffn0_dve": [("f_mix", 4), ("f_clamped", 1), ("f_gate", 2), ("f_out", 1)],
            "ffn0_pe": [("f_r", 1), ("f_k", 1), ("f_v", 1)],
            "ffn0_act": [("f_exp", 1), ("f_relu", 1), ("f_ksq", 1)],
            "ffn0_pool": [("f_zero", 1), ("f_om", 1)],
            "attn1_dve": [("b_zero", 1), ("b_q", 2), ("b_z", 2), ("b_arg", 1), ("b_amp1", 3), ("b_vb", 1), ("b_s1", 1),
                          ("b_s2", 1), ("b_coef", 2), ("b_t1", 1), ("b_t2", 1), ("b_t3", 1), ("b_mixed", 1), ("c_bo", 1),
                          ("c_res", 1), ("c_gain", 1), ("c_shiftb", 1)],
            "attn1_pe": [("b_proj", 5), ("b_amp", 1), ("b_vn", 1), ("b_sup", 2), ("c_all_t", 1), ("c_out", 1)],
            "attn1_act": [("b_vT", 1), ("b_k", 2), ("b_eamp", 1), ("b_tanh", 1), ("b_abs", 1), ("b_sin", 2), ("c_oT", 1)],
            "ffn1_dve": [("d_res", 1), ("d_top", 2), ("d_clamp", 1), ("d_sel", 4), ("d_al", 2), ("d_gate", 1), ("d_gate_T", 1)],
            "ffn1_pe": [("d_aff", 1), ("d_gate_t", 1), ("d_b2", 1)],
            "ffn1_act": [("d_exp", 1)],
        }
        LINE_OF = {name: line for line, steps in LINES.items() for name, _ in steps}

        def sem_of(name):
            return sem(LINE_OF[name])

        def step(name, count):
            steps = [n for n, _ in LINES[LINE_OF[name]]]
            return sem_of(name), sum(c for _, c in LINES[LINE_OF[name]][:steps.index(name)]) + count

        k_stack = nc.dram_tensor("k_stack", (B, H, ROWS, KEYS), BF16, kind="Internal").ap()
        q_stack = nc.dram_tensor("q_stack", (H, ROWS, B * S), BF16, kind="Internal").ap()
        mask_parts_d = nc.dram_tensor("mask_parts_d", (3, B, KEYS), BF16, kind="Internal").ap()
        v_units = nc.dram_tensor("v_units", (B, UNITS, 128, KT * HQ * (HD + 1)), F32, kind="Internal").ap()

        W = sb("W", [128, len(MATS), 128])
        C = sb("C", [128, len(COLS)])
        EC = sb("EC", [128, NE * (2 + FT)])
        R = sb("R", [128, len(ROWV), 128])
        K = sb("K", [128, len(CONSTS), 128])
        CT = sb("CT", [128, NE])
        B2 = sb("B2", [NE, D])
        ident_bf = sb("ident_bf", [128, 128], BF16)

        def mat(n):
            return W[:, MATS.index(n), :]

        def col(n):
            i = COLS.index(n)
            return C[:, i:i + 1]

        def row(n):
            return R[:, ROWV.index(n), :]

        def const(n):
            return K[:, CONSTS.index(n), :]

        ident = const("identity")

        xN = sb("xN", [128, B, D])
        xhN = sb("xhN", [128, B, D])
        xhT = sb("xhT", [128, B * S])
        stats = sb("stats", [128, B, 6])
        mv = sb("mv", [128, B, 2])
        var_eps = sb("var_eps", [128, B])
        rstd = sb("rstd", [128, B])
        neg_half = sb("neg_half", [128, B])
        tA = sb("tA", [128, 1024])
        tB = sb("tB", [128, 1024])
        tC = sb("tC", [128, 1024])
        tD = sb("tD", [128, 1024])
        tE = sb("tE", [128, 1024])
        tF = sb("tF", [128, 1024])
        small = sb("small", [128, 256])
        ARENA = 38400
        arena = sb("arena", [128, ARENA])

        def carve(sizes):
            at, got = 0, []
            for words in sizes:
                got.append(arena[:, at:at + words])
                at += words
            assert at <= ARENA
            return got

        ps = stack.enter_context(nc.psum_tensor("ps", [128, 8 * BANK], F32))

        def bank(i, n=BANK, off=0):
            return ps[:, i * BANK + off:i * BANK + off + n]

        def b3(ap, inner=128):
            return ap.rearrange("p (b d) -> p b d", d=inner)

        def bc_mid(ap, n):
            return ap.rearrange("p (o m) -> p o m", o=1).broadcast_to([128, n, ap.shape[1]])

        def bc_in(ap, n):
            return ap.rearrange("p (m o) -> p m o", o=1).broadcast_to([128, ap.shape[1], n])

        def ln_dve(v, i, ready, src=None, dst=None):
            src = b3(xN_flat) if src is None else src
            dst = xhN if dst is None else dst
            for b in range(B):
                if b == 0:
                    v.wait_ge(*ready)
                v.bn_stats(stats[:, b, :], src[:, b, :]).then_inc(sem("ln_stats"), 1)
            for b in range(B):
                v.wait_ge(sem("ln_stats"), i * B + b + 1)
                v.bn_aggr(mv[:, b, :], stats[:, b, :]).then_inc(sem("ln_mv"), 1)
            v.wait_ge(sem("ln_rstd"), i + 1)
            for b in range(B):
                v.tensor_scalar(dst[:, b, :], src[:, b, :], mv[:, b, 0:1], rstd[:, b:b + 1],
                                ALU.subtract, ALU.mult).then_inc(sem("ln_xh"), 1)

        def ln_pool(g, i, eps=1e-5):
            g.wait_ge(sem("ln_mv"), i * B + B)
            g.tensor_scalar(var_eps[:, :], mv[:, :, 1], eps, None, ALU.add).then_inc(sem("ln_ve"), 1)
            g.wait_ge(sem("ln_ve"), i + 1)
            g.tensor_tensor(rstd[:, :], var_eps[:, :], neg_half[:, :], ALU.pow).then_inc(sem("ln_rstd"), 1)

        def transpose4_pe(pe, src, bk, ready, done, by_block=False):
            if not by_block:
                pe.wait_ge(*ready)
            for b in range(B):
                if by_block:
                    pe.wait_ge(ready[0], ready[1] - B + b + 1)
                t = pe.transpose(bank(bk, 128, 128 * b), src[:, b, :], ident)
            t.then_inc(done, 1)

        START_AT_ONE = ["s_masked", "pt_copied", "k_rest_done", "v_added", "x0_new", "scores0",
                        "k_out0", "k_out1", "v_out0", "v_out1", "p_t", "exp0", "nbias0", "k3_done"]

        xN_flat = xN[:, :, :].rearrange("p b d -> p (b d)")
        SQ_D = 1.0 / math.sqrt(D)

        (ctxN0, ctxN1, ctxT0, ctxT1, mask_sb, s_mask, p_nat, p_t, kp0, kp1, vb0, vb1, kr0, kr1, x_bv,
         mask1_f, mask1_r, mask1_p) = carve([
             2048, 2048, 2048, 2048, 2048, 2048, 2048, 2048, 3072, 3072, KT * H * 9, KT * H * 9, 512, 512, 512,
             64, 64, 96])
        ctxN = [b3(ctxN0), b3(ctxN1)]
        ctxT = [ctxT0, ctxT1]
        k_parts = [kp.bitcast(BF16).rearrange("p (j n) -> p j n", j=3) for kp in (kp0, kp1)]
        vbuf = [vb.rearrange("p (u t g e) -> p u t g e", u=UNITS, t=KT, g=HQ) for vb in (vb0, vb1)]
        k_rest = [kr0, kr1]
        mparts = mask1_p.bitcast(BF16).rearrange("p (j n) -> p j n", j=3)
        qT, qk_T, kwork = tA[:, 0:512], tB[:, 0:512], tA[:, 512:1024]
        qk_b = [tC[:, 0:128], tC[:, 128:256]]
        oT0 = [tD[:, 0:128], tD[:, 128:256]]
        c_q, mx, mc, nbias, rsum, rinv, cb = (small[:, 8 * i:8 * i + 8] for i in range(7))

        def l0x_sync(sp):
            for name in START_AT_ONE:
                sp.sem_inc(sem(name), 1)
            for name, value in START.items():
                sp.sem_inc(sem(name), value)
            sp.dma_start(xN[:, :, :], x.rearrange("b s d -> s b d")).then_inc(sem("in_x"), 16)
            sp.dma_start(K[:, :, :], consts).then_inc(sem("in_consts"), 16)
            sp.dma_start(W[:, 0:5, :], mats[:, 0:5, :]).then_inc(sem("in_mats_first"), 16)
            sp.dma_start(C[:, :], cols).then_inc(sem("in_small"), 16)
            with sp.Fori(0, B // 2) as it:
                for s in range(2):
                    sp.wait_ge(sem("o0_done"), it * 2 + s - 1 + START["o0_done"])
                    sp.dma_start(ctxT[s], ctx_t[bass.ds(it * 2 + s, 1), :, :].rearrange("o d n -> (o d) n")
                                 ).then_inc(sem(f"in_ctx{s}"), 16)
                    if s == 0:
                        sp.wait_ge(sem("in_mask0"), 16)
                    for half in range(2):
                        t = slice(half * KT // 2, (half + 1) * KT // 2)
                        sp.dma_start(ctxN[s][:, t, :],
                                     ctx[bass.ds(it * 2 + s, 1), half * KEYS // 2:(half + 1) * KEYS // 2, :]
                                     .rearrange("o (t p) d -> p (o t) d", p=128)).then_inc(sem(f"in_ctxN{s}"), 16)

        def l0x_store_k(act, s, n, i_):
            j, (c0, c1) = K_STORES[i_]
            if i_ == 0:
                act.wait_ge(sem("k1_done"), n * 4 + 4)
                act.wait_ge(sem("k3_done"), n * 4 + 4 + 1)
            act.dma_start(k_stack[bass.ds(n, 1), :, :, :].rearrange("o h (d c) n -> (o h d) c n", c=len(COMBOS))
                          [:, c0:c1, :],
                          k_parts[s][:, j:j + 1, :].broadcast_to([128, c1 - c0, KEYS])
                          ).then_inc(sem(f"k_out{s}"), 16)

        def l0x_store_v(act, s, n):
            act.wait_ge(sem("v_added"), n * 4 + 4 + 1)
            act.dma_start(v_units[bass.ds(n, 1), :, :, :].rearrange("o u k n -> k (o u) n"),
                          vbuf[s].rearrange("p u t g e -> p u (t g e)")).then_inc(sem(f"v_out{s}"), 16)

        T_BANK = (4, 6, 5, 4)

        def l0x_scores_pe(pe, s, n, it):
            pe.wait_ge(sem(f"in_ctx{s}"), it * 16 + 16)
            pe.wait_ge(sem("qk_b"), n + 1)
            pe.wait_ge(sem("s_masked"), n + 1)
            for c in range(4):
                m = pe.matmul(bank(c), qk_b[s], ctxT[s][:, c * BANK:(c + 1) * BANK], start=True, stop=True)
            m.then_inc(sem("scores0"), 1)

        def l0x_kv_pe(pe, s, n, c):
            if c == 0:
                pe.wait_ge(sem("pt_copied"), n * 4 + 1)
            if c >= 2:
                pe.wait_ge(sem("k_rest_done"), n * 4 + c)
            pe.matmul(bank(4 + 2 * (c % 2)), mat("L1x_k"), ctxT[s][:, c * BANK:(c + 1) * BANK],
                      start=True, stop=True).then_inc(sem("k_proj"), 1)
            if c >= 1:
                pe.wait_ge(sem("v_added"), n * 4 + c + 1)
            for t in range(4 * c, 4 * c + 4):
                m = pe.matmul(bank(5, 128, 128 * (t % 4)), ctxT[s][:, t * 128:(t + 1) * 128],
                              mat("L1x_v"), start=True, stop=True)
            m.then_inc(sem("v_proj"), 1)

        def l0x_probs_pe(pe, s, n, it):
            pe.wait_ge(sem("exp0"), n + 1 + 1)
            for gr in range(4):
                if gr == 0:
                    pe.wait_ge(sem("k_rest_done"), n * 4 + 4 + 1)
                if gr == 2:
                    pe.wait_ge(sem("v_added"), n * 4 + 4 + 1)
                if gr == 3:
                    pe.wait_ge(sem("pt_copied"), n * 4 + 1 + 1)
                for t in range(4 * gr, 4 * gr + 4):
                    m = pe.transpose(bank(T_BANK[gr], 128, 128 * (t % 4)), p_nat[:, t * 128:(t + 1) * 128], ident)
                m.then_inc(sem("p_t"), 1)
            pe.wait_ge(sem(f"in_ctxN{s}"), it * 32 + 32)
            pe.wait_ge(sem("x0_new"), n + 1)
            for gr in range(4):
                pe.wait_ge(sem("pt_copied"), n * 4 + gr + 1 + 1)
                for t in range(4 * gr, 4 * gr + 4):
                    m = pe.matmul(bank(7, 128), ctxN[s][:, t, :], p_t[:, t * 128:(t + 1) * 128],
                                  start=t == 0, stop=t == KT - 1)
            m.then_inc(sem("o0_done"), 1)

        def l0x_out_pe(pe, s, n):
            pe.wait_ge(sem("oT0_sb"), n + 1)
            pe.matmul(bank(7, 128, 128), oT0[s], mat("L0x_v"), start=True, stop=True).then_inc(sem("y0"), 1)

        def l0x_pe(pe):
            pe.wait_ge(sem("in_consts"), 16)
            transpose4_pe(pe, xhN, 0, (sem("ln_xh"), 0 * B + B), sem("ln_t"), by_block=True)
            pe.wait_ge(sem("in_mats_first"), 16)
            pe.wait_ge(sem("ln_T"), 1)
            pe.matmul(bank(1), mat("L0x_q"), xhT[:, :], start=True, stop=True).then_inc(sem("q0"), 1)
            pe.wait_ge(sem("q0_sb"), 1)
            pe.matmul(bank(2), mat("L0x_kT"), qT, start=True, stop=True).then_inc(sem("qk0"), 1)
            for b in range(B):
                m = pe.matmul(bank(3, 1, b), qT[:, b * S:(b + 1) * S], col("L0x_bk"), start=True, stop=True)
            m.then_inc(sem("c0"), 1)
            pe.wait_ge(sem("c0_sb"), 1)
            with pe.Fori(0, B // 2) as it:
                n = it * 2
                l0x_scores_pe(pe, 0, n, it)
                for c in range(4):
                    l0x_kv_pe(pe, 0, n, c)
                l0x_scores_pe(pe, 1, n + 1, it)
                l0x_probs_pe(pe, 0, n, it)
                for c in range(4):
                    l0x_kv_pe(pe, 1, n + 1, c)
                    if c == 0:
                        l0x_out_pe(pe, 0, n)
                l0x_probs_pe(pe, 1, n + 1, it)
                l0x_out_pe(pe, 1, n + 1)

        def l0x_act(act):
            act.wait_ge(sem("in_x"), 16)
            act.dma_start(R[:, :, :], rows.partition_broadcast(128)).then_inc(sem("in_rows"), 16)
            act.dma_start(mask1_f, mask1).then_inc(sem("in_mask1"), 16)
            act.dma_start(mask_sb, mask0).then_inc(sem("in_mask0"), 16)
            act.dma_start(W[:, 5:len(MATS), :], mats[:, 5:len(MATS), :]).then_inc(sem("in_mats"), 16)
            act.dma_start(EC[:, :], expert_cols).then_inc(sem("in_experts"), 16)
            act.dma_start(CT[:, :], centroids_t).then_inc(sem("in_experts"), 16)
            act.dma_start(B2[:, :], b2).then_inc(sem("in_experts"), 16)
            act.wait_ge(sem("ln_t"), 1)
            act.activation(xhT[:, :], bank(0), ACT.Copy).then_inc(sem("ln_T"), 1)
            act.wait_ge(sem("in_small"), 16)
            act.wait_ge(sem("q0"), 1)
            act.activation(qT, bank(1), ACT.Identity, bias=col("L0x_bq")).then_inc(sem("q0_sb"), 1)
            act.wait_ge(sem("qk0"), 1)
            act.activation(qk_T, bank(2), ACT.Copy, scale=SQ_D).then_inc(sem("qk0_sb"), 1)

            def exps(s, n):
                act.wait_ge(sem("nbias0"), n + 1 + 1)
                act.wait_ge(sem("p_t"), n * 4 + 1)
                act.activation(p_nat, s_mask, ACT.Exp, bias=nbias[:, s:s + 1],
                               accum_out=rsum[:, s:s + 1]).then_inc(sem("exp0"), 1)

            def second_parts(s, n, c):
                act.wait_ge(sem("k_rest_done"), n * 4 + c + 1 + 1)
                act.activation(k_parts[s][:, 1, c * BANK:(c + 1) * BANK], k_rest[c % 2], ACT.Copy
                               ).then_inc(sem("k2_done"), 1)

            with act.Fori(0, B // 2) as it:
                for s in range(2):
                    n = it * 2 + s
                    for c in range(4):
                        act.wait_ge(sem("k_proj"), n * 4 + c + 1)
                        if c == 0:
                            act.wait_ge(sem(f"k_out{s}"), it * 16 * len(K_STORES) + 1)
                        act.activation(k_parts[s][:, 0, c * BANK:(c + 1) * BANK], bank(4 + 2 * (c % 2)),
                                       ACT.Identity, bias=col("L1x_bk")).then_inc(sem("k1_done"), 1)
                        if c > 0:
                            second_parts(s, n, c - 1)
                        if s == 1 and c < 3:
                            l0x_store_k(act, 0, n - 1, c)
                    second_parts(s, n, 3)
                    if s == 0:
                        exps(0, n)
                    if s == 1:
                        l0x_store_v(act, 0, n - 1)
                    act.wait_ge(sem("o0_done"), n + START["o0_done"])
                    for gr in range(4):
                        act.wait_ge(sem("p_t"), n * 4 + gr + 1 + 1)
                        act.activation(p_t[:, gr * BANK:(gr + 1) * BANK], bank(T_BANK[gr]), ACT.Copy
                                       ).then_inc(sem("pt_copied"), 1)
                    if s == 0:
                        exps(1, n + 1)
                    act.wait_ge(sem("o0_done"), n + 1 + START["o0_done"])
                    act.activation(oT0[s], bank(7, 128), ACT.Copy).then_inc(sem("oT0_sb"), 1)
                    if s == 1:
                        for i_ in range(len(K_STORES)):
                            l0x_store_k(act, 1, n, i_)
                        l0x_store_v(act, 1, n)

        def l0x_dve(v):
            ln_dve(v, 0, (sem("in_x"), 16))
            for s in range(2):
                v.memset(vbuf[s][:, :, :, :, HD], 1.0).then_inc(sem("v_ones"), 1)
            v.wait_ge(sem("in_rows"), 16)
            v.tensor_tensor(b3(x_bv), xN[:, :, :], bc_mid(row("L0x_bv"), B), ALU.add).then_inc(sem("x_bv"), 1)
            x1_early_dve(v)
            v.wait_ge(sem("c0"), 1)
            v.tensor_scalar(c_q[:, 0:B], bank(3, B), SQ_D, None, ALU.mult).then_inc(sem("c0_sb"), 1)
            v.wait_ge(sem("c0_sb"), 1)
            v.wait_ge(sem("in_mask0"), 16)
            v.wait_ge(sem("in_small"), 16)
            v.wait_ge(sem("x_bv"), 1)
            v.wait_ge(sem("qk0_sb"), 1)

            def finish(s, n):
                v.wait_ge(sem("exp0"), n + 1 + 1)
                v.reciprocal(rinv[:, s:s + 1], rsum[:, s:s + 1]).then_inc(sem("rinv0"), 1)
                v.wait_ge(sem("rinv0"), n + 1)
                v.wait_ge(sem("y0"), n + 1)
                v.scalar_tensor_tensor(out=xN_flat[:, bass.ds(n * 128, 128)], in0=bank(7, 128, 128),
                                       scalar=rinv[:, s:s + 1], in1=x_bv[:, bass.ds(n * 128, 128)],
                                       op0=ALU.mult, op1=ALU.add).then_inc(sem("x0_new"), 1)

            v.memset(tB[:, 512:768], 0.0).then_inc(sem("qk_end"), 1)
            for s in range(2):
                v.tensor_copy(qk_b[s], qk_T[:, s * 128:s * 128 + 128]).then_inc(sem("qk_b"), 1)
            l0a_prepare_dve(v)
            l0a_weights_dve(v)
            v.wait_ge(sem("qk_end"), 1)
            with v.Fori(0, B // 2) as it:
                for s in range(2):
                    n = it * 2 + s
                    v.wait_ge(sem("scores0"), n + 1 + 1)
                    v.wait_ge(sem("exp0"), n + 1)
                    v.wait_ge(sem("nbias0"), n + 1)
                    v.tensor_copy(cb[:, s:s + 1], c_q[:, bass.ds(n, 1)]).then_inc(sem("c_b"), 1)
                    v.tensor_tensor_reduce(s_mask, ps[:, 0:KEYS], mask_sb, 1.0, -3.0e38, ALU.add, ALU.max,
                                           mx[:, s:s + 1]).then_inc(sem("s_masked"), 1)
                    v.wait_ge(sem("s_masked"), n + 1 + 1)
                    v.wait_ge(sem("c_b"), n + 1)
                    v.tensor_tensor(mc[:, s:s + 1], mx[:, s:s + 1], cb[:, s:s + 1], ALU.add
                                    ).then_inc(sem("mc0"), 1)
                    v.wait_ge(sem("mc0"), n + 1)
                    v.tensor_tensor(nbias[:, s:s + 1], cb[:, s:s + 1], mc[:, s:s + 1], ALU.subtract
                                    ).then_inc(sem("nbias0"), 1)
                    for c in range(4):
                        v.wait_ge(sem("v_proj"), n * 4 + c + 1)
                        if c == 0:
                            v.wait_ge(sem(f"v_out{s}"), it * 16 + 1)
                        v.tensor_tensor(vbuf[s][:, :, 4 * c:4 * c + 4, :, 0:HD],
                                        bank(5).rearrange("p (t u g d) -> p u t g d", t=4, u=UNITS, g=HQ),
                                        row("L1x_bv").rearrange("p (u o g d) -> p u o g d", u=UNITS, o=1, g=HQ)
                                        .broadcast_to([128, UNITS, 4, HQ, HD]),
                                        ALU.add).then_inc(sem("v_added"), 1)
                        v.wait_ge(sem("k1_done"), n * 4 + c + 1)
                        v.wait_ge(sem("k3_done"), it * 8 + (s * 4 + c - 1 if s * 4 + c > 1 else 0) + 1)
                        v.scalar_tensor_tensor(out=k_rest[c % 2], in0=bank(4 + 2 * (c % 2)), scalar=col("L1x_bk"),
                                               in1=k_parts[s][:, 0, c * BANK:(c + 1) * BANK],
                                               op0=ALU.add, op1=ALU.subtract).then_inc(sem("k_rest_done"), 1)
                        if s == 1 and c == 0:
                            finish(0, n - 1)
                for s in range(2):
                    v.wait_ge(sem("scores0"), it * 2 + 2 + 1)
                    v.tensor_copy(qk_b[s], tB[:, bass.ds(it * 256 + 256 + s * 128, 128)]).then_inc(sem("qk_b"), 1)
                finish(1, it * 2 + 1)

        def l0x_pool(g):
            g.memset(neg_half[:, :], -0.5).then_inc(sem("pool_const"), 1)
            g.wait_ge(sem("pool_const"), 1)
            ln_pool(g, 0)
            x1_early_pool(g)
            g.wait_ge(sem("in_mask1"), 16)
            g.tensor_scalar(mask1_r, mask1_f, -1.0e9, None, ALU.mult).then_inc(sem("mask1_c"), 1)
            for j in range(3):
                g.wait_ge(sem("mask1_c"), 2 * j + 1)
                g.tensor_copy(mparts[:, j, :], mask1_r).then_inc(sem("mask1_c"), 1)
                if j < 2:
                    g.wait_ge(sem("mask1_c"), 2 * j + 2)
                    g.tensor_tensor(mask1_r, mask1_r, mparts[:, j, :], ALU.subtract).then_inc(sem("mask1_c"), 1)
            g.wait_ge(sem("mask1_c"), 6)
            for j in range(3):
                g.dma_start(mask_parts_d[j].rearrange("b (p n) -> (b p) n", n=64), mparts[:, j, :]
                            ).then_inc(sem("mask1_out"), 16)
            g.wait_ge(sem("v_ones"), 2)
            l0a_prepare_pool(g)
            with g.Fori(0, B // 2) as it:
                for s in range(2):
                    n = it * 2 + s
                    for c in range(4):
                        at = slice(c * BANK, (c + 1) * BANK)
                        g.wait_ge(sem("k2_done"), n * 4 + c + 1)
                        g.tensor_tensor(k_parts[s][:, 2, at], k_rest[c % 2], k_parts[s][:, 1, at], ALU.subtract
                                        ).then_inc(sem("k3_done"), 1)

        w_norm, r_scale, om = small[:, 64:68], small[:, 72:76], small[:, 80:82]
        half = small[:, 84:88]
        a_mx, a_sum, a_r = small[:, 88:92], small[:, 92:96], small[:, 96:100]
        wn, wnT, vT_a = tE[:, 0:512], tF[:, 0:512], tE[:, 512:1024]
        head_sq, head_n, head_w, head_r = (tB[:, 128 * i_:128 * i_ + 128] for i_ in range(4))
        RES = 0.5 / math.sqrt(0.5)
        EPS_W = 1e-4

        def l0a_prepare_dve(v):
            v.wait_ge(sem("in_mats"), 16)
            for i_, n_ in enumerate(["L0a_q", "L0a_k", "L0a_v", "L0a_o"]):
                v.tensor_tensor_reduce(tF[:, 512 + 128 * i_:640 + 128 * i_], mat(n_), mat(n_), 1.0, 0.0,
                                       ALU.mult, ALU.add, w_norm[:, i_:i_ + 1]).then_inc(sem_of("a_wsq"), 1)

        def l0a_prepare_pool(g):
            g.memset(half, 0.5).then_inc(sem_of("a_half"), 1)
            g.wait_ge(*step("a_half", 1))
            g.wait_ge(*step("a_wsq", 4))
            g.tensor_tensor(w_norm, w_norm, half, ALU.pow).then_inc(sem_of("a_wroot"), 1)
            g.wait_ge(*step("a_wroot", 1))
            g.tensor_scalar(w_norm, w_norm, SQ_D, EPS_W, ALU.mult, ALU.add).then_inc(sem_of("a_w"), 1)

        def l0a_weights_dve(v):
            v.wait_ge(sem("in_small"), 16)
            v.wait_ge(*step("a_w", 1))
            v.reciprocal(r_scale, w_norm).then_inc(sem_of("a_rw"), 1)
            v.wait_ge(*step("a_rw", 1))
            v.tensor_scalar(r_scale, r_scale, col("gain"), SQ_D, ALU.mult, ALU.mult).then_inc(sem_of("a_rw"), 1)
            v.wait_ge(*step("a_rw", 2))
            for i_, n_ in enumerate(["L0a_q", "L0a_k", "L0a_v", "L0a_o"]):
                v.tensor_scalar(wn[:, 128 * i_:128 * i_ + 128], mat(n_), r_scale[:, i_:i_ + 1], None, ALU.mult
                                ).then_inc(sem_of("a_wn"), 1)

        def l0a_dve(v):
            ln_dve(v, 1, (sem("x0_new"), B + 1))
            v.wait_ge(sem("ln_xh"), 1 * B + B)
            v.scalar_tensor_tensor(out=xN_flat, in0=xhN[:, :, :].rearrange("p b d -> p (b d)"), scalar=RES,
                                   in1=xN_flat, op0=ALU.mult, op1=ALU.add).then_inc(sem_of("a_res"), 1)
            v.wait_ge(*step("a_sq", 1))
            v.tensor_reduce(head_sq, tA[:, :].rearrange("p (g d) -> p g d", d=HD), AX.X, ALU.add
                            ).then_inc(sem_of("a_headsq"), 1)
            v.wait_ge(*step("a_headn", 1))
            v.tensor_scalar(head_w, head_n, EPS_W, None, ALU.add).then_inc(sem_of("a_headw"), 1)
            v.wait_ge(*step("a_headw", 1))
            v.reciprocal(head_r, head_w).then_inc(sem_of("a_headr"), 1)
            v.wait_ge(*step("a_headr", 1))
            v.tensor_tensor(tC[:, :].rearrange("p (g d) -> p g d", d=HD),
                            ps[:, 2 * BANK:4 * BANK].rearrange("p (g d) -> p g d", d=HD), bc_in(head_r, HD),
                            ALU.mult).then_inc(sem_of("a_qkn"), 1)
            v.wait_ge(*step("a_scores", 1))
            v.tensor_tensor(b3(tD[:, 0:512]), b3(bank(5)), bc_mid(const("off_block"), B), ALU.add
                            ).then_inc(sem_of("a_masked"), 1)
            v.wait_ge(*step("a_masked", 1))
            v.tensor_reduce(a_mx, b3(tD[:, 0:512]), AX.X, ALU.max).then_inc(sem_of("a_max"), 1)
            v.wait_ge(*step("a_max", 1))
            v.tensor_tensor(b3(tD[:, 0:512]), b3(tD[:, 0:512]), bc_in(a_mx, 128), ALU.subtract
                            ).then_inc(sem_of("a_shifted"), 1)
            v.wait_ge(*step("a_exp", 1))
            v.tensor_reduce(a_sum, b3(tD[:, 512:1024]), AX.X, ALU.add).then_inc(sem_of("a_sum"), 1)
            v.wait_ge(*step("a_sum", 1))
            v.reciprocal(a_r, a_sum).then_inc(sem_of("a_rsum"), 1)
            v.wait_ge(*step("a_rsum", 1))
            v.tensor_tensor(b3(tD[:, 0:512]), b3(tD[:, 512:1024]), bc_in(a_r, 128), ALU.mult
                            ).then_inc(sem_of("a_probs"), 1)
            v.wait_ge(*step("a_out", 1))
            v.wait_ge(*step("a_res", 1))
            v.scalar_tensor_tensor(out=xN_flat, in0=bank(7), scalar=RES, in1=xN_flat, op0=ALU.mult, op1=ALU.add
                                   ).then_inc(sem("x1_new"), 1)

        def l0a_pe(pe):
            pe.wait_ge(*step("a_wn", 4))
            transpose4_pe(pe, b3(wn), 0, step("a_wn", 4), sem_of("a_wnt"))
            transpose4_pe(pe, xhN, 1, (sem("ln_xh"), 1 * B + B), sem("ln_t"), by_block=True)
            pe.wait_ge(*step("a_wnT", 1))
            pe.wait_ge(sem("ln_T"), 2)
            for b in range(B):
                m = pe.matmul(bank(2 + b // 2, 256, 256 * (b % 2)), xhT[:, b * S:(b + 1) * S], wnT[:, 0:256],
                              start=True, stop=True)
            m.then_inc(sem_of("a_qk"), 1)
            pe.matmul(bank(4), wnT[:, 256:384], xhT[:, :], start=True, stop=True).then_inc(sem_of("a_v"), 1)
            pe.wait_ge(*step("a_qkn", 1))
            for b in range(B):
                m = pe.matmul(bank(5, 128, 128 * b), tC[:, 256 * b:256 * b + 128], tC[:, 256 * b + 128:256 * b + 256],
                              start=True, stop=True)
            m.then_inc(sem_of("a_scores"), 1)
            pe.wait_ge(*step("a_probs", 1))
            for b in range(B):
                m = pe.matmul(bank(6, 128, 128 * b), tD[:, 128 * b:128 * b + 128], wnT[:, 384:512],
                              start=True, stop=True)
            m.then_inc(sem_of("a_mo"), 1)
            pe.wait_ge(*step("a_vT", 1))
            pe.wait_ge(*step("a_mo_sb", 1))
            for b in range(B):
                m = pe.matmul(bank(7, 128, 128 * b), vT_a[:, b * S:(b + 1) * S], tA[:, 128 * b:128 * b + 128],
                              start=True, stop=True)
            m.then_inc(sem_of("a_out"), 1)

        def l0a_act(act):
            act.wait_ge(*step("a_wnt", 1))
            act.activation(wnT, bank(0), ACT.Copy).then_inc(sem_of("a_wnT"), 1)
            act.wait_ge(sem("ln_t"), 2)
            act.activation(xhT[:, :], bank(1), ACT.Copy).then_inc(sem("ln_T"), 1)
            act.wait_ge(*step("a_qk", 1))
            act.activation(tA[:, :], ps[:, 2 * BANK:4 * BANK], ACT.Square).then_inc(sem_of("a_sq"), 1)
            act.wait_ge(*step("a_v", 1))
            act.activation(vT_a, bank(4), ACT.Copy).then_inc(sem_of("a_vT"), 1)
            act.wait_ge(*step("a_headsq", 1))
            act.activation(head_n, head_sq, ACT.Sqrt, scale=1.0 / HD).then_inc(sem_of("a_headn"), 1)
            act.wait_ge(*step("a_shifted", 1))
            act.activation(tD[:, 512:1024], tD[:, 0:512], ACT.Exp, scale=1.0 / math.sqrt(S)).then_inc(sem_of("a_exp"), 1)
            act.wait_ge(*step("a_mo", 1))
            act.activation(tA[:, 0:512], bank(6), ACT.Copy).then_inc(sem_of("a_mo_sb"), 1)

        x_pad = mask_sb[:, 0:B * (S + 1)].rearrange("p (b s) -> p b s", s=S + 1)
        x_r, x_k = tB[:, 0:512], tB[:, 512:1024]

        def l0f_pool(g):
            g.wait_ge(sem("x0_new"), B + 1)
            g.memset(x_pad[:, :, 0:1], 0.0).then_inc(sem_of("f_zero"), 1)
            g.tensor_scalar(om, C[:, 3:5], -1.0, 1.0, ALU.mult, ALU.add).then_inc(sem_of("f_om"), 1)

        def l0f_dve(v):
            ln_dve(v, 2, (sem("x1_new"), 1))
            v.wait_ge(*step("f_om", 1))
            v.wait_ge(*step("f_zero", 1))
            v.wait_ge(sem("ln_T"), 3)
            for i_, dst in enumerate((x_r, x_k)):
                before = b3(tC[:, 512 * i_:512 * i_ + 512])
                v.tensor_scalar(before, x_pad[:, :, 0:S], om[:, i_:i_ + 1], None, ALU.mult
                                ).then_inc(sem_of("f_mix"), 1)
                v.wait_ge(*step("f_mix", 2 * i_ + 1))
                v.scalar_tensor_tensor(out=b3(dst), in0=x_pad[:, :, 1:S + 1], scalar=C[:, 3 + i_:4 + i_], in1=before,
                                       op0=ALU.mult, op1=ALU.add).then_inc(sem_of("f_mix"), 1)
            v.wait_ge(*step("f_r", 1))
            v.tensor_scalar(tE[:, 0:512], bank(1), -87.0, None, ALU.max).then_inc(sem_of("f_clamped"), 1)
            v.wait_ge(*step("f_exp", 1))
            v.tensor_scalar(tE[:, 0:512], tE[:, 0:512], 1.0, None, ALU.add).then_inc(sem_of("f_gate"), 1)
            v.wait_ge(*step("f_gate", 1))
            v.reciprocal(tE[:, 512:1024], tE[:, 0:512]).then_inc(sem_of("f_gate"), 1)
            v.wait_ge(*step("f_gate", 2))
            v.wait_ge(*step("f_v", 1))
            v.tensor_tensor(tC[:, 0:512], bank(3), tE[:, 512:1024], ALU.mult).then_inc(sem_of("f_out"), 1)
            v.wait_ge(*step("f_out", 1))
            v.tensor_tensor(xN_flat, xN_flat, tC[:, 0:512], ALU.add).then_inc(sem("x2_new"), 1)

        def l0f_pe(pe):
            transpose4_pe(pe, xhN, 0, (sem("ln_xh"), 2 * B + B), sem("ln_t"), by_block=True)
            pe.wait_ge(*step("f_mix", 2))
            for b in range(B):
                m = pe.matmul(bank(1, 128, 128 * b), x_r[:, b * S:(b + 1) * S], mat("L0f_rT"), start=True, stop=True)
            m.then_inc(sem_of("f_r"), 1)
            pe.wait_ge(*step("f_mix", 4))
            pe.matmul(bank(2), mat("L0f_kT"), x_k, start=True, stop=True).then_inc(sem_of("f_k"), 1)
            pe.wait_ge(*step("f_ksq", 1))
            for b in range(B):
                m = pe.matmul(bank(3, 128, 128 * b), tD[:, 512 + b * S:512 + (b + 1) * S], mat("L0f_vT"),
                              start=True, stop=True)
            m.then_inc(sem_of("f_v"), 1)

        def l0f_act(act):
            act.wait_ge(sem("ln_t"), 3)
            act.wait_ge(*step("f_zero", 1))
            act.activation(x_pad[:, :, 1:S + 1], b3(bank(0)), ACT.Copy).then_inc(sem("ln_T"), 1)
            act.wait_ge(*step("f_clamped", 1))
            act.activation(tE[:, 0:512], tE[:, 0:512], ACT.Exp, scale=-1.0).then_inc(sem_of("f_exp"), 1)
            act.wait_ge(*step("f_k", 1))
            act.activation(tD[:, 0:512], bank(2), ACT.Relu).then_inc(sem_of("f_relu"), 1)
            act.wait_ge(*step("f_relu", 1))
            act.activation(tD[:, 512:1024], tD[:, 0:512], ACT.Square).then_inc(sem_of("f_ksq"), 1)

        PV_COLS = HD + 1
        GROUPS = KT // 2
        STEPS = UNITS * GROUPS
        CHUNKS = HQ * KEYS // BANK
        AHEAD = CHUNKS + CHUNKS // 2
        at = 0
        k_slot, p_ring, v_slot, q_slot = [], [], [], []
        for i_ in range(UNITS):
            k_slot.append(arena[:, at:at + KEYS].bitcast(BF16).rearrange("p (g n) -> p g n", g=2))
            at += KEYS
        at = 10240
        for i_ in range(4):
            p_ring.append(arena[:, at:at + 1024])
            at += 1024
        for i_ in range(UNITS):
            v_slot.append(arena[:, at:at + KT * HQ * PV_COLS])
            at += KT * HQ * PV_COLS
        at = 33600
        for i_ in range(UNITS):
            q_slot.append(arena[:, at:at + 256].bitcast(BF16).rearrange("p (g a q) -> p g a q", g=2, a=2))
            at += 256
        q_f, q_rest = tA[:, 0:512], tA[:, 512:1024]
        q_part = tB[:, 0:768].bitcast(BF16).rearrange("p (j n) -> p j n", j=3)
        chunk_max = [tC[:, 16 * i_:16 * i_ + 16] for i_ in range(2)]
        neg_max = [tC[:, 32 + 4 * i_:36 + 4 * i_] for i_ in range(2)]
        m_rest = [tC[:, 40 + 4 * i_:44 + 4 * i_] for i_ in range(2)]
        m_part = [tC[:, 64 + 8 * i_:70 + 8 * i_].bitcast(BF16).rearrange("p (j h) -> p j h", j=3) for i_ in range(2)]
        m_cols = [tC[:, 96 + 32 * i_:114 + 32 * i_].bitcast(BF16).rearrange("p (h c) -> p h c", c=9) for i_ in range(2)]
        o_rcp = tC[:, 180:184]
        m_none = tC[:, 184:188]
        m_none3 = tC[:, 188:194].rearrange("p (g j) -> p g j", j=3)
        o_raw = tC[:, 256:384]
        zeros = tC[:, 384:512]
        o_all = tD[:, 0:512]
        o_T = tE[:, 0:512]
        ONES_PAIR = 1.0019378662109375
        START = {"o0_done": 2, "exp1": 2, "pv_chunk": 4, "pv_copied": 1, "o1_t": 1, "o1_norm": 1}

        def x1_init_pool(g, slots):
            for i_ in slots:
                g.memset(arena[:, i_ * KEYS:(i_ + 1) * KEYS], ONES_PAIR).then_inc(sem("k_ones"), 1)

        def x1_early_pool(g):
            for i_ in range(UNITS):
                g.memset(arena[:, 33600 + 256 * i_:33856 + 256 * i_], 0.0).then_inc(sem("q_zero"), 1)

        def x1_early_dve(v):
            v.wait_ge(sem("q_zero"), UNITS)
            for i_ in range(UNITS):
                v.memset(arena[MASK_ROW:MAX_ROW, 33600 + 256 * i_:33856 + 256 * i_], ONES_PAIR
                         ).then_inc(sem("q_ones"), 1)

        def x1_load_kv(sp, b, u):
            sp.dma_start(k_slot[u][0:MASK_ROW, :, :],
                         k_stack[bass.ds(b, 1), HQ * u:HQ * u + HQ, :, :]
                         .rearrange("o (g a) r n -> (o a r) g n", a=2)).then_inc(sem(f"unit_in{u}"), 16)
            for g_ in range(2):
                sp.dma_start(k_slot[u][MASK_ROW:MAX_ROW, g_, :],
                             mask_parts_d[:, bass.ds(b, 1), :].rearrange("j o n -> j (o n)")
                             ).then_inc(sem(f"unit_in{u}"), 16)
            sp.dma_start(v_slot[u], v_units[bass.ds(b, 1), u, :, :].rearrange("o k n -> (o k) n")
                         ).then_inc(sem(f"unit_in{u}"), 16)

        def x1_load_q(sp, b, u):
            for a_ in range(2):
                sp.dma_start(q_slot[u][ROWS * a_:ROWS * a_ + ROWS, :, a_, :],
                             q_stack[HQ * u + a_:HQ * u + a_ + 3:2, :, bass.ds(b * S, S)]
                             .rearrange("g r q -> r g q")).then_inc(sem(f"unit_in{u}"), 16)

        def x1_sync(sp):
            for s_ in range(2):
                sp.wait_ge(sem(f"k_out{s_}"), B // 2 * 16 * len(K_STORES) + 1)
                sp.wait_ge(sem(f"v_out{s_}"), B // 2 * 16 + 1)
            sp.wait_ge(sem("mask1_out"), 48)
            for u in range(UNITS):
                sp.wait_ge(sem("k_ones"), u + 1)
                x1_load_kv(sp, 0, u)
            sp.wait_ge(sem("q_ones"), UNITS)
            sp.wait_ge(sem("q_out"), 16 * len(Q_STORES))
            for u in range(UNITS):
                x1_load_q(sp, 0, u)
            with sp.Fori(1, B) as b:
                for u in range(UNITS):
                    sp.wait_ge(sem("pv_chunk"), (b * UNITS - UNITS + u + 1) * GROUPS + START["pv_chunk"])
                    x1_load_kv(sp, b, u)
                    x1_load_q(sp, b, u)

        def x1_q_store(act):
            act.wait_ge(sem("q1_part"), 3)
            for (j0, j1), (c0, c1) in Q_STORES:
                act.dma_start(q_stack.rearrange("h (d c) n -> (h d) c n", c=len(COMBOS))[:, c0:c1, :],
                              q_part[:, j0:j1, :]).then_inc(sem("q_out"), 16)

        def rows_bank(i_, m):
            return m % 4 if isinstance(m, int) and m < AHEAD - 4 else 4 + i_ % 2

        def rows_chunk(pe, u, i_, m):
            g_, a_, c = i_ // 8, i_ // 4 % 2, i_ % 4
            if isinstance(m, int) and m < AHEAD - 4:
                if m >= 4:
                    pe.wait_ge(sem("max_done"), m - 3)
            elif not (isinstance(m, int) and m < AHEAD - 2):
                pe.wait_ge(sem("max_done"), m - 1)
            pe.matmul(bank(rows_bank(i_, m)), q_slot[u][0:MAX_ROW, g_, a_, :], k_slot[u][0:MAX_ROW, g_, c * BANK:(c + 1) * BANK],
                      start=True, stop=True).then_inc(sem("rows_done"), 1)

        def max_rows_pe(pe, u, n):
            pe.wait_ge(sem("m_cols"), 2 * n + 2)
            out_bf = bank(7).bitcast(BF16)
            for h_ in range(HQ):
                t = pe.transpose(out_bf[MASK_ROW:PAIR_ROWS, 128 * h_:128 * h_ + 128], m_cols[u % 2][:, h_, :],
                                 ident_bf[:, :])
            t.then_inc(sem("m_t"), 1)

        def cols_chunk(pe, u, k2, n, N):
            if k2 == 0:
                pe.wait_ge(sem("m_rows"), n + 1)
            pe.wait_ge(sem("exp1"), N - 1 + START["exp1"])
            for kk in range(2):
                kt = 2 * k2 + kk
                for g_ in range(2):
                    m = pe.matmul(ps[:, (N_slot(k2) * 2 + kk) * BANK + 256 * g_:(N_slot(k2) * 2 + kk) * BANK + 256 * g_ + 256],
                                  k_slot[u][0:PAIR_ROWS, g_, kt * 128:kt * 128 + 128],
                                  q_slot[u][0:PAIR_ROWS, g_, :, :].rearrange("p a q -> p (a q)"),
                                  start=True, stop=True)
            m.then_inc(sem("cols_done"), 1)

        def N_slot(k2):
            return k2 % 2

        def values_chunk(pe, u, k2, n, N):
            if k2 == 0:
                pe.wait_ge(sem("pv_copied"), n + START["pv_copied"])
            pe.wait_ge(sem("exp1"), N + 1 + START["exp1"])
            for kk in range(2):
                kt = 2 * k2 + kk
                for h_ in range(HQ):
                    m = pe.matmul(ps[32 * h_:32 * h_ + PV_COLS, 6 * BANK:6 * BANK + 128],
                                  v_slot[u][:, kt * HQ * PV_COLS + h_ * PV_COLS:kt * HQ * PV_COLS + (h_ + 1) * PV_COLS],
                                  p_ring[k2 % 4][:, kk * BANK + 128 * h_:kk * BANK + 128 * h_ + 128],
                                  start=kt == 0, stop=kt == KT - 1)
            m.then_inc(sem("pv_chunk"), 1)

        def out_turn_pe(pe, n):
            pe.wait_ge(sem("pv_copied"), n + 1 + START["pv_copied"])
            pe.wait_ge(sem("o1_norm"), n + START["o1_norm"])
            pe.transpose(bank(7, 128, 256), o_raw, ident).then_inc(sem("o1_t"), 1)

        def x1_pe_batch(pe, b, last):
            for g in range(STEPS):
                u, k2 = g // GROUPS, g % GROUPS
                n, N = b * UNITS + u, b * STEPS + g
                cols_chunk(pe, u, k2, n, N)
                if g > 0:
                    pu, pk = (g - 1) // GROUPS, (g - 1) % GROUPS
                    values_chunk(pe, pu, pk, b * UNITS + pu, N - 1)
                for c in (AHEAD + 2 * g, AHEAD + 2 * g + 1):
                    if last and c >= UNITS * CHUNKS:
                        continue
                    ahead = c // CHUNKS
                    if c % CHUNKS == 0:
                        pe.wait_ge(sem(f"unit_in{ahead % UNITS}"), (b + ahead // UNITS) * 96 + 96)
                    rows_chunk(pe, ahead % UNITS, c % CHUNKS, b * (UNITS * CHUNKS) + c)
                if k2 == 2 and u > 0:
                    pe.wait_ge(sem("m_rows"), n + 1)
                    out_turn_pe(pe, n - 1)
                if k2 == 5 and not (last and u == UNITS - 1):
                    pe.wait_ge(sem("o1_norm"), n - 1 + START["o1_norm"] if u == 0 else n + START["o1_norm"])
                    max_rows_pe(pe, (u + 1) % UNITS, n + 1)
            values_chunk(pe, UNITS - 1, GROUPS - 1, b * UNITS + UNITS - 1, b * STEPS + STEPS - 1)
            pe.wait_ge(sem("m_rows"), b * UNITS + UNITS + (0 if last else 1))
            out_turn_pe(pe, b * UNITS + UNITS - 1)

        def x1_pe(pe):
            transpose4_pe(pe, xhN, 0, (sem("ln_xh"), 3 * B + B), sem("ln_t"), by_block=True)
            pe.wait_ge(sem("ln_T"), 4)
            pe.matmul(bank(1), mat("L1x_q"), xhT[:, :], start=True, stop=True).then_inc(sem("q1"), 1)
            pe.wait_ge(sem("x1_zeros"), 1)
            pe.matmul(bank(6, 128), zeros, zeros, start=True, stop=True)
            for c in range(AHEAD):
                if c % CHUNKS == 0:
                    pe.wait_ge(sem(f"unit_in{c // CHUNKS}"), 96)
                rows_chunk(pe, c // CHUNKS, c % CHUNKS, c)
                if c == CHUNKS + 4:
                    max_rows_pe(pe, 0, 0)
            pe.wait_ge(sem("max_done"), AHEAD - 4)
            with pe.Fori(0, B - 1) as b:
                x1_pe_batch(pe, b, False)
            x1_pe_batch(pe, B - 1, True)
            transpose4_pe(pe, b3(o_all), 0, (sem("o1_norm"), B * UNITS + 1), sem("o1_all_t"))
            pe.wait_ge(sem("o1_T"), 1)
            for b in range(B):
                m = pe.matmul(bank(1, 128, 128 * b), o_T[:, 128 * b:128 * b + 128], mat("L1x_o"), start=True, stop=True)
            m.then_inc(sem("y1"), 1)

        def copy_out_act(act, n):
            act.wait_ge(sem("o1_t"), n + START["o1_t"])
            act.wait_ge(sem("pv_chunk"), n * GROUPS + GROUPS + START["pv_chunk"])
            act.activation(o_raw, bank(6, 128), ACT.Copy).then_inc(sem("pv_copied"), 1)

        def x1_act_batch(act, b):
            for g in range(STEPS):
                u, k2 = g // GROUPS, g % GROUPS
                N = b * STEPS + g
                act.wait_ge(sem("cols_done"), N + 1)
                act.wait_ge(sem("pv_chunk"), N - 3 + START["pv_chunk"])
                act.activation(p_ring[k2 % 4], ps[:, 2 * BANK * (k2 % 2):2 * BANK * (k2 % 2) + 2 * BANK], ACT.Exp
                               ).then_inc(sem("exp1"), 1)
                if k2 == 0 and u > 0:
                    copy_out_act(act, b * UNITS + u - 1)
            copy_out_act(act, b * UNITS + UNITS - 1)

        def x1_act(act):
            act.wait_ge(sem("ln_t"), 4)
            act.activation(xhT[:, :], bank(0), ACT.Copy).then_inc(sem("ln_T"), 1)
            x1_q_store(act)
            with act.Fori(0, B - 1) as b:
                x1_act_batch(act, b)
            x1_act_batch(act, B - 1)
            act.wait_ge(sem("o1_all_t"), 1)
            act.activation(o_T, bank(0), ACT.Copy).then_inc(sem("o1_T"), 1)

        def max_chunk(v, u, i_, m):
            v.wait_ge(sem("rows_done"), m + 1)
            v.tensor_reduce(chunk_max[u % 2][:, i_:i_ + 1], bank(rows_bank(i_, m)), AX.X, ALU.max, negate=True
                            ).then_inc(sem("max_done"), 1)
            if i_ == 15:
                v.wait_ge(sem("max_done"), m + 1)
                v.tensor_reduce(neg_max[u % 2], chunk_max[u % 2].rearrange("p (h c) -> p h c", c=4), AX.X, ALU.min
                                ).then_inc(sem("neg_max"), 1)

        def max_rows_dve(v, u, n):
            v.wait_ge(sem("m_t"), n + 1)
            v.tensor_copy(q_slot[u][MASK_ROW:PAIR_ROWS, :, :, :].rearrange("p g a q -> p (g a q)"),
                          bank(7).bitcast(BF16)[MASK_ROW:PAIR_ROWS, 0:512]).then_inc(sem("m_rows"), 1)

        def norm_out_dve(v, b, u):
            n = b * UNITS + u
            t = bank(7, 128, 256).rearrange("p (h c) -> p h c", c=32)
            v.wait_ge(sem("o1_t"), n + 1 + START["o1_t"])
            v.reciprocal(o_rcp, t[:, :, HD]).then_inc(sem("o1_rcp"), 1)
            v.wait_ge(sem("o1_rcp"), n + 1)
            v.tensor_tensor(o_all[:, bass.ds(b * 128 + u * 32, 32)].rearrange("p (h d) -> p h d", d=HD),
                            t[:, :, 0:HD], bc_in(o_rcp, HD), ALU.mult).then_inc(sem("o1_norm"), 1)

        def x1_dve_batch(v, b, last):
            for g in range(STEPS):
                u, k2 = g // GROUPS, g % GROUPS
                n = b * UNITS + u
                for c in (AHEAD + 2 * g, AHEAD + 2 * g + 1):
                    if not (last and c >= UNITS * CHUNKS):
                        max_chunk(v, c // CHUNKS % UNITS, c % CHUNKS, b * (UNITS * CHUNKS) + c)
                if k2 == 3 and u > 0:
                    norm_out_dve(v, b, u - 1)
                if k2 == 6 and not (last and u == UNITS - 1):
                    max_rows_dve(v, (u + 1) % UNITS, n + 1)
            norm_out_dve(v, b, UNITS - 1)

        def x1_dve(v):
            ln_dve(v, 3, (sem("x2_new"), 1))
            v.wait_ge(sem("q1"), 1)
            v.tensor_scalar(q_f, bank(1), col("L1x_bq"), 1.0 / math.sqrt(HD), ALU.add, ALU.mult
                            ).then_inc(sem("q1_f"), 1)
            for j in range(3):
                v.wait_ge(sem("q1_f"), j + 1)
                v.tensor_copy(q_part[:, j, :], q_f).then_inc(sem("q1_part"), 1)
                if j < 2:
                    v.wait_ge(sem("q1_part"), j + 1)
                    v.tensor_tensor(q_f, q_f, q_part[:, j, :], ALU.subtract).then_inc(sem("q1_f"), 1)
            v.memset(zeros, 0.0).then_inc(sem("x1_zeros"), 1)
            v.wait_ge(sem("in_consts"), 16)
            v.tensor_copy(ident_bf[:, :], ident).then_inc(sem("ident_bf"), 1)
            v.tensor_tensor(xN[:, :, :], xN[:, :, :], bc_mid(row("L1x_bo"), B), ALU.add).then_inc(sem("x1_bo"), 1)
            for c in range(AHEAD):
                max_chunk(v, c // CHUNKS, c % CHUNKS, c)
                if c == CHUNKS + 6:
                    max_rows_dve(v, 0, 0)
            with v.Fori(0, B - 1) as b:
                x1_dve_batch(v, b, False)
            x1_dve_batch(v, B - 1, True)
            v.wait_ge(sem("y1"), 1)
            v.tensor_tensor(xN_flat, bank(1), xN_flat, ALU.add).then_inc(sem("x3_new"), 1)

        def x1_pool(g):
            g.wait_ge(sem("x2_new"), 1)
            for i_ in range(2):
                g.memset(tC[:, 96 + 32 * i_:114 + 32 * i_], 0.0).then_inc(sem("m_zero"), 1)
            g.memset(tC[:, 184:194], 0.0).then_inc(sem("m_zero"), 1)
            g.wait_ge(sem("m_zero"), 3)
            for i_ in range(2):
                g.memset(m_cols[i_][:, :, 0:3], 1.0).then_inc(sem("m_zero"), 1)
            g.wait_ge(sem("m_zero"), 5)
            with g.Fori(0, B * UNITS // 2) as it:
                for i_ in range(2):
                    n = it * 2 + i_
                    g.wait_ge(sem("neg_max"), n + 1)
                    g.tensor_tensor(m_part[i_][:, 0, :], neg_max[i_], m_none, ALU.add).then_inc(sem("m_split"), 1)
                    g.wait_ge(sem("m_split"), n * 4 + 1)
                    g.tensor_tensor(m_rest[i_], neg_max[i_], m_part[i_][:, 0, :], ALU.subtract).then_inc(sem("m_split"), 1)
                    g.wait_ge(sem("m_split"), n * 4 + 2)
                    g.tensor_tensor(m_part[i_][:, 1, :], m_rest[i_], m_none, ALU.add).then_inc(sem("m_split"), 1)
                    g.wait_ge(sem("m_split"), n * 4 + 3)
                    g.tensor_tensor(m_part[i_][:, 2, :], m_rest[i_], m_part[i_][:, 1, :], ALU.subtract
                                    ).then_inc(sem("m_split"), 1)
                    g.wait_ge(sem("m_split"), n * 4 + 4)
                    for a_ in range(2):
                        g.tensor_tensor(m_cols[i_][:, a_:a_ + 3:2, 3 + 3 * a_:6 + 3 * a_],
                                        m_part[i_][:, :, a_:a_ + 3:2].rearrange("p j g -> p g j"),
                                        m_none3, ALU.add).then_inc(sem("m_cols"), 1)

        (q2T, eq2T, k2T, ek2T, v2T, k_bd, ek_bd, s_sum, p2, p2T, e_dec, mix9, q_b2, eq_b2, m_b2, raw2, amp_w, o2_all,
         o2_T, ek_b2) = carve([512, 512, 512, 512, 512, 2048, 2048, 2048, 2048, 1024, 1024, B * H * 9, 128, 128, H * 9, 512,
                        1024, 512, 512, 128])
        z_all = amp_w[:, 0:128].rearrange("p (b c) -> p b c", c=32)
        e_amp, th, p_abs, s_arg, sin_p, cos_p, c_sin, c_cos = (
            amp_w[:, 128 + 64 * i_:192 + 64 * i_].rearrange("p (b h) -> p b h", h=H) for i_ in range(8))
        mix_v = mix9.rearrange("p (b h e) -> p b h e", b=B, h=H)
        o2_rcp = amp_w[:, 640:656]
        neg_max2 = amp_w[:, 656:672]
        o2_zero = tF[:, 0:512]
        SQ_HD = 1.0 / math.sqrt(HD)
        START.update({"c_scores": 1, "c_sum": 2, "c_exp": 4, "c_pt": 4, "c_ptc": 2, "c_pv": 2, "c_raw": 1, "c_ot": 1,
                      "c_norm": 1})

        def l1a_pe(pe):
            transpose4_pe(pe, xhN, 0, (sem("ln_xh"), 4 * B + B), sem("ln_t"), by_block=True)
            pe.wait_ge(sem("ln_T"), 5)
            for bk, n_ in ((1, "L1a_vT"), (4, "L1a_kT"), (2, "L1a_qT"), (5, "L1a_ekT"), (3, "L1a_eqT")):
                pe.matmul(bank(bk), mat(n_), xhT[:, :], start=True, stop=True).then_inc(sem_of("b_proj"), 1)
            for b in range(B):
                m = pe.matmul(bank(7, 32, 32 * b), xhT[:, b * S:(b + 1) * S], mat("amp_ph")[:, 0:32],
                              start=True, stop=True)
            m.then_inc(sem_of("b_amp"), 1)
            for b in range(B):
                m = pe.matmul(bank(6, 128, 128 * b), xhT[:, b * S:(b + 1) * S], mat("L1a_vT"), start=True, stop=True)
            m.then_inc(sem_of("b_vn"), 1)

            def scores(b, j):
                n = b * 4 + j
                if j == 0:
                    pe.wait_ge(sem("c_qb"), b * 2 + 2)
                pe.wait_ge(sem("c_ekbd"), n + 1)
                pe.wait_ge(sem("c_kbd"), n + 1)
                pe.wait_ge(sem("c_sum"), n - 1 + START["c_sum"])
                pe.matmul(bank(j % 2), eq_b2, ek_bd[:, j * BANK:(j + 1) * BANK], start=True, stop=True)
                pe.matmul(bank(2 + j % 2), q_b2, k_bd[:, j * BANK:(j + 1) * BANK], start=True, stop=True
                          ).then_inc(sem("c_scores"), 1)

            def turn(b, j):
                n = b * 4 + j
                pe.wait_ge(sem("c_exp"), n + 1 + START["c_exp"])
                pe.wait_ge(sem("c_ptc"), n - 1 + START["c_ptc"])
                for h_ in range(4):
                    t = pe.transpose(bank(4 + j % 2, 128, 128 * h_),
                                     p2[:, j * BANK + 128 * h_:j * BANK + 128 * h_ + 128], ident)
                t.then_inc(sem("c_pt"), 1)

            def values(b, j):
                n = b * 4 + j
                if j == 0:
                    pe.wait_ge(sem("c_mb"), b + 1)
                    pe.wait_ge(sem("c_raw"), b + START["c_raw"])
                pe.wait_ge(sem("c_ptc"), n + 1 + START["c_ptc"])
                for h_ in range(4):
                    m = pe.matmul(ps[32 * h_:32 * h_ + 9, 6 * BANK + 128 * j:6 * BANK + 128 * j + 128],
                                  m_b2[:, (4 * j + h_) * 9:(4 * j + h_) * 9 + 9],
                                  p2T[:, (j % 2) * BANK + 128 * h_:(j % 2) * BANK + 128 * h_ + 128],
                                  start=True, stop=True)
                m.then_inc(sem("c_pv"), 1)

            def turn_out(b):
                pe.wait_ge(sem("c_raw"), b + 1 + START["c_raw"])
                pe.wait_ge(sem("c_norm"), b + START["c_norm"])
                for j in range(4):
                    t = pe.transpose(bank(7, 128, 128 * j), raw2[:, 128 * j:128 * j + 128], ident)
                t.then_inc(sem("c_ot"), 1)

            def batch(b, first, last):
                for j in range(4):
                    turn(b, j)
                    if j < 2:
                        scores(b, j + 2)
                    elif not last:
                        scores(b + 1, j - 2)
                    if j > 0:
                        values(b, j - 1)
                    elif not first:
                        values(b - 1, 3)
                    if j == 2 and not first:
                        turn_out(b - 1)

            pe.wait_ge(*step("b_q", 2))
            scores(0, 0)
            scores(0, 1)
            pe.wait_ge(*step("b_vT", 1))
            pe.wait_ge(*step("b_k", 2))
            for i_, n_ in enumerate(("mix", "mix_rolled")):
                for b in range(B):
                    m = pe.matmul(bank(4 + i_, 128, 128 * b), v2T[:, b * S:(b + 1) * S], mat(n_),
                                  start=True, stop=True)
                m.then_inc(sem_of("b_sup"), 1)
            pe.wait_ge(*step("b_vb", 1))
            pe.wait_ge(*step("b_zero", 1))
            pe.matmul(bank(6), o2_zero[:, 0:128], o2_zero, start=True, stop=True)
            pe.wait_ge(*step("b_s2", 1))
            batch(0, True, False)
            with pe.Fori(1, B - 1) as b:
                batch(b, False, False)
            batch(B - 1, False, True)
            values(B - 1, 3)
            turn_out(B - 1)
            transpose4_pe(pe, b3(o2_all), 0, (sem("c_norm"), B + 1), sem_of("c_all_t"))
            pe.wait_ge(*step("c_oT", 1))
            for b in range(B):
                m = pe.matmul(bank(1, 128, 128 * b), o2_T[:, 128 * b:128 * b + 128], mat("L1a_oT"),
                              start=True, stop=True)
            m.then_inc(sem_of("c_out"), 1)

        def l1a_act(act):
            act.wait_ge(sem("ln_t"), 5)
            act.activation(xhT[:, :], bank(0), ACT.Copy).then_inc(sem("ln_T"), 1)
            act.wait_ge(*step("b_proj", 1))
            act.activation(v2T, bank(1), ACT.Identity, bias=col("L1a_bv")).then_inc(sem_of("b_vT"), 1)
            act.wait_ge(*step("b_proj", 2))
            act.activation(k2T, bank(4), ACT.Identity, bias=col("L1a_bk")).then_inc(sem_of("b_k"), 1)
            act.wait_ge(*step("b_proj", 4))
            act.activation(ek2T, bank(5), ACT.Identity, bias=col("L1a_bek")).then_inc(sem_of("b_k"), 1)
            def mixed_values(b):
                if isinstance(b, int) and b == 0:
                    act.wait_ge(*step("b_mixed", 1))
                act.wait_ge(sem("c_pv"), b * 4 + START["c_pv"])
                act.activation(m_b2, mix9[:, bass.ds(b * H * 9, H * 9)], ACT.Copy).then_inc(sem("c_mb"), 1)

            def exps(b, j):
                n = b * 4 + j
                act.wait_ge(sem("c_max"), n + 1)
                act.wait_ge(sem("c_pt"), n - 3 + START["c_pt"])
                for h_ in range(4):
                    at = slice(j * BANK + 128 * h_, j * BANK + 128 * h_ + 128)
                    e = act.activation(p2[:, at], s_sum[:, at], ACT.Exp, bias=neg_max2[:, 4 * j + h_:4 * j + h_ + 1])
                e.then_inc(sem("c_exp"), 1)

            def turned(b, j):
                n = b * 4 + j
                act.wait_ge(sem("c_pt"), n + 1 + START["c_pt"])
                act.wait_ge(sem("c_pv"), n - 1 + START["c_pv"])
                act.activation(p2T[:, (j % 2) * BANK:(j % 2) * BANK + BANK], bank(4 + j % 2), ACT.Copy
                               ).then_inc(sem("c_ptc"), 1)

            def raw_out(b):
                act.wait_ge(sem("c_pv"), b * 4 + 4 + START["c_pv"])
                act.wait_ge(sem("c_ot"), b + START["c_ot"])
                act.activation(raw2, bank(6), ACT.Copy).then_inc(sem("c_raw"), 1)

            def batch(b, first, last):
                for j in range(4):
                    exps(b, j)
                    if j == 1:
                        if not first:
                            raw_out(b - 1)
                        mixed_values(b)
                    if j > 0:
                        turned(b, j - 1)
                    elif not first:
                        turned(b - 1, 3)

            act.wait_ge(*step("b_z", 2))
            act.activation(e_amp, e_amp, ACT.Exp, scale=-1.0).then_inc(sem_of("b_eamp"), 1)
            act.activation(th, z_all[:, :, H:2 * H], ACT.Tanh).then_inc(sem_of("b_tanh"), 1)
            act.wait_ge(*step("b_tanh", 1))
            act.activation(p_abs, th, ACT.Abs, scale=math.pi).then_inc(sem_of("b_abs"), 1)
            act.wait_ge(*step("b_arg", 1))
            act.activation(sin_p, th, ACT.Sin, scale=math.pi).then_inc(sem_of("b_sin"), 1)
            act.activation(cos_p, s_arg, ACT.Sin).then_inc(sem_of("b_sin"), 1)
            batch(0, True, False)
            with act.Fori(1, B - 1) as b:
                batch(b, False, False)
            batch(B - 1, False, True)
            turned(B - 1, 3)
            raw_out(B - 1)
            act.wait_ge(*step("c_all_t", 1))
            act.activation(o2_T, bank(0), ACT.Copy).then_inc(sem_of("c_oT"), 1)

        def l1a_dve(v):
            ln_dve(v, 4, (sem("x3_new"), 1))
            def keys(b, j):
                if not isinstance(b, int) or b > 0:
                    v.wait_ge(sem("c_scores"), (b - 1) * 4 + j + 1 + START["c_scores"])
                v.tensor_tensor(b3(k_bd[:, j * BANK:(j + 1) * BANK]), bc_mid(k2T[:, bass.ds(b * 128, 128)], 4),
                                bc_in(const("head_mask")[:, 4 * j:4 * j + 4], 128), ALU.mult
                                ).then_inc(sem("c_kbd"), 1)

            def logits(b, j):
                n = b * 4 + j
                ss = s_sum[:, j * BANK:(j + 1) * BANK]
                dec = e_dec[:, (j % 2) * BANK:(j % 2) * BANK + BANK]
                v.wait_ge(sem("c_scores"), n + 1 + START["c_scores"])
                v.tensor_tensor(b3(dec), b3(bank(j % 2)), bc_mid(const("decay"), 4), ALU.mult
                                ).then_inc(sem("c_dec"), 1)
                v.wait_ge(sem("c_dec"), n + 1)
                v.wait_ge(sem("c_exp"), n - 3 + START["c_exp"])
                v.tensor_tensor(ss, bank(2 + j % 2), dec, ALU.add).then_inc(sem("c_sum"), 1)
                v.wait_ge(sem("c_sum"), n + 1 + START["c_sum"])
                v.tensor_reduce(neg_max2[:, 4 * j:4 * j + 4], b3(ss), AX.X, ALU.max, negate=True
                                ).then_inc(sem("c_max"), 1)

            v.memset(o2_zero, 0.0).then_inc(sem_of("b_zero"), 1)
            v.wait_ge(*step("b_proj", 3))
            v.tensor_scalar(q2T, bank(2), col("L1a_bq"), SQ_HD, ALU.add, ALU.mult).then_inc(sem_of("b_q"), 1)
            v.wait_ge(*step("b_proj", 5))
            v.tensor_scalar(eq2T, bank(3), col("L1a_beq"), SQ_HD, ALU.add, ALU.mult).then_inc(sem_of("b_q"), 1)
            v.wait_ge(*step("b_k", 2))
            keys(0, 0)
            keys(0, 1)
            v.wait_ge(*step("b_amp", 1))
            v.tensor_tensor(z_all, bank(7, 128).rearrange("p (b c) -> p b c", c=32),
                            bc_mid(row("amp_ph_b")[:, 0:32], B), ALU.add).then_inc(sem_of("b_z"), 1)
            v.wait_ge(*step("b_z", 1))
            v.tensor_scalar(e_amp, z_all[:, :, 0:H], -87.0, None, ALU.max).then_inc(sem_of("b_z"), 1)
            keys(0, 2)
            keys(0, 3)
            logits(0, 0)
            v.wait_ge(*step("b_abs", 1))
            v.tensor_scalar(s_arg, p_abs, -1.0, math.pi / 2, ALU.mult, ALU.add).then_inc(sem_of("b_arg"), 1)
            v.wait_ge(*step("b_eamp", 1))
            v.tensor_scalar(e_amp, e_amp, 1.0, None, ALU.add).then_inc(sem_of("b_amp1"), 1)
            v.wait_ge(*step("b_amp1", 1))
            v.reciprocal(e_amp, e_amp).then_inc(sem_of("b_amp1"), 1)
            v.wait_ge(*step("b_amp1", 2))
            v.tensor_scalar(e_amp, e_amp, 0.3, None, ALU.mult).then_inc(sem_of("b_amp1"), 1)
            v.wait_ge(*step("b_vn", 1))
            v.tensor_tensor(b3(tE[:, 0:512]), b3(bank(6)), bc_mid(row("L1a_bv"), B), ALU.add).then_inc(sem_of("b_vb"), 1)
            v.wait_ge(*step("b_sup", 2))
            v.tensor_tensor(b3(tC[:, 0:512]), b3(bank(4)), bc_mid(row("mix_b"), B), ALU.add).then_inc(sem_of("b_s1"), 1)
            v.tensor_tensor(b3(tD[:, 0:512]), b3(bank(5)), bc_mid(row("mix_b_rolled"), B), ALU.add
                            ).then_inc(sem_of("b_s2"), 1)
            v.wait_ge(*step("b_amp1", 3))
            v.wait_ge(*step("b_sin", 2))
            v.tensor_tensor(c_cos, e_amp, cos_p, ALU.mult).then_inc(sem_of("b_coef"), 1)
            v.tensor_tensor(c_sin, e_amp, sin_p, ALU.mult).then_inc(sem_of("b_coef"), 1)
            v.wait_ge(*step("b_s2", 1))
            v.wait_ge(*step("b_coef", 2))

            logits(0, 1)

            def by_head(ap):
                return ap.rearrange("p (g d) -> p g d", d=HD)

            v.tensor_tensor(by_head(tC[:, 0:512]), by_head(tC[:, 0:512]),
                            bc_in(c_cos.rearrange("p b h -> p (b h)"), HD), ALU.mult).then_inc(sem_of("b_t1"), 1)
            v.tensor_tensor(by_head(tD[:, 0:512]), by_head(tD[:, 0:512]),
                            bc_in(c_sin.rearrange("p b h -> p (b h)"), HD), ALU.mult).then_inc(sem_of("b_t2"), 1)
            v.wait_ge(*step("b_t1", 1))
            v.tensor_tensor(tE[:, 0:512], tE[:, 0:512], tC[:, 0:512], ALU.add).then_inc(sem_of("b_t3"), 1)
            v.wait_ge(*step("b_t2", 1))
            v.wait_ge(*step("b_t3", 1))
            v.wait_ge(sem("b_mix_one"), 1)
            v.tensor_tensor(mix9.rearrange("p (g e) -> p g e", e=9)[:, :, 0:HD], by_head(tE[:, 0:512]),
                            by_head(tD[:, 0:512]), ALU.add).then_inc(sem_of("b_mixed"), 1)
            def normed_out(b):
                v.wait_ge(sem("c_ot"), b + 1 + START["c_ot"])
                t = bank(7).rearrange("p (h c) -> p h c", c=32)
                v.reciprocal(o2_rcp, t[:, :, HD]).then_inc(sem("c_rcp"), 1)
                v.wait_ge(sem("c_rcp"), b + 1)
                v.tensor_tensor(o2_all[:, bass.ds(b * 128, 128)].rearrange("p (h d) -> p h d", d=HD), t[:, :, 0:HD],
                                bc_in(o2_rcp, HD), ALU.mult).then_inc(sem("c_norm"), 1)

            def batch(b, first, last):
                for j in range(4):
                    if not (first and j < 2):
                        logits(b, j)
                    if not last:
                        keys(b + 1, j)
                    if j == 3 and not first:
                        normed_out(b - 1)

            batch(0, True, False)
            with v.Fori(1, B - 1) as b:
                batch(b, False, False)
            batch(B - 1, False, True)
            normed_out(B - 1)
            v.tensor_tensor(xhN[:, :, :], xhN[:, :, :], bc_mid(row("L1a_bo"), B), ALU.add).then_inc(sem_of("c_bo"), 1)
            v.wait_ge(*step("c_bo", 1))
            v.wait_ge(*step("c_out", 1))
            v.tensor_tensor(tA[:, 0:512], bank(1), xhN[:, :, :].rearrange("p b d -> p (b d)"), ALU.add
                            ).then_inc(sem_of("c_res"), 1)
            ln_dve(v, 5, step("c_res", 1), src=b3(tA[:, 0:512]), dst=b3(tB[:, 0:512]))
            v.wait_ge(sem("ln_xh"), 5 * B + B)
            v.tensor_tensor(b3(tB[:, 0:512]), b3(tB[:, 0:512]), bc_mid(row("L1a_ln_g"), B), ALU.mult
                            ).then_inc(sem_of("c_gain"), 1)
            v.tensor_tensor(xN[:, :, :], xN[:, :, :], bc_mid(row("L1a_ln_b"), B), ALU.add).then_inc(sem_of("c_shiftb"), 1)
            v.wait_ge(*step("c_gain", 1))
            v.wait_ge(*step("c_shiftb", 1))
            v.tensor_tensor(xN_flat, xN_flat, tB[:, 0:512], ALU.add).then_inc(sem("x4_new"), 1)

        def l1a_pool(g):
            ln_pool(g, 4)
            g.memset(mix_v[:, :, :, HD], 1.0).then_inc(sem("b_mix_one"), 1)
            g.wait_ge(*step("b_k", 2))

            def batch_keys(b):
                if not isinstance(b, int):
                    g.wait_ge(sem("c_ekbd"), b * 4)
                g.tensor_copy(ek_b2, ek2T[:, bass.ds(b * 128, 128)]).then_inc(sem("c_ekb"), 1)

            def keys(b, j):
                g.wait_ge(sem("c_ekb"), b + 1)
                if not isinstance(b, int):
                    g.wait_ge(sem("c_scores"), (b - 1) * 4 + j + 1 + START["c_scores"])
                g.tensor_tensor(b3(ek_bd[:, j * BANK:(j + 1) * BANK]), bc_mid(ek_b2, 4),
                                bc_in(const("head_mask")[:, 4 * j:4 * j + 4], 128), ALU.mult
                                ).then_inc(sem("c_ekbd"), 1)

            def queries(b):
                if not isinstance(b, int):
                    g.wait_ge(sem("c_scores"), b * 4 + START["c_scores"])
                g.tensor_copy(eq_b2, eq2T[:, bass.ds(b * 128, 128)]).then_inc(sem("c_qb"), 1)
                g.tensor_copy(q_b2, q2T[:, bass.ds(b * 128, 128)]).then_inc(sem("c_qb"), 1)

            batch_keys(0)
            keys(0, 0)
            g.wait_ge(*step("b_q", 2))
            queries(0)
            for j in range(1, 4):
                keys(0, j)
            with g.Fori(1, B) as b:
                batch_keys(b)
                for j in range(3):
                    keys(b, j)
                queries(b)
                keys(b, 3)
            ln_pool(g, 5)

        w_slot = [arena[:, 34700 + 1024 * i_:35724 + 1024 * i_] for i_ in range(2)]
        (xn2N, xn2T, xe0, xe1, h0, h1, gate_T) = carve([512, 512, 512, 512, 2048, 2048, 512])
        x_e, h_e = [xe0, xe1], [h0, h1]
        aff = small[:, 104:136].rearrange("p (b e) -> p b e", e=NE)
        score = small[:, 136:168].rearrange("p (b e) -> p b e", e=NE)
        gate = small[:, 168:200].rearrange("p (b e) -> p b e", e=NE)
        top, s_top, alpha = small[:, 200:204], small[:, 204:208], small[:, 208:212]
        START.update({"e_relu": 4, "e_y": 2, "e_acc": 1, "e_h": 5, "e_x": 1})

        def l1f_load(sp, e, s):
            sp.wait_ge(sem("e_h"), (e - 1) * FT + START["e_h"])
            sp.dma_start(w_slot[s][:, 0:512], w1[bass.ds(e, 1), :, :].rearrange("o d f -> (o d) f")
                         ).then_inc(sem(f"in_w1_{s}"), 16)
            sp.wait_ge(sem("e_y"), e - 1 + START["e_y"])
            sp.dma_start(w_slot[s][:, 512:1024].rearrange("p (t d) -> p t d", d=D),
                         w2[bass.ds(e, 1), :, :].rearrange("o (t p) d -> p (o t) d", p=128)
                         ).then_inc(sem(f"in_w2_{s}"), 16)

        def l1f_sync(sp):
            with sp.Fori(0, NE // 2) as it:
                for s in range(2):
                    l1f_load(sp, it * 2 + s, s)

        def hidden_pe(pe, e, s, loads):
            pe.wait_ge(sem(f"in_w1_{s}"), 16 * loads)
            pe.wait_ge(sem("e_x"), e + 1 + START["e_x"])
            for t in range(FT):
                pe.wait_ge(sem("e_relu"), e * FT + t - 3 + START["e_relu"])
                pe.matmul(bank(t), w_slot[s][:, 128 * t:128 * t + 128], x_e[s], start=True, stop=True
                          ).then_inc(sem("e_h"), 1)

        def output_pe(pe, e, s, loads):
            pe.wait_ge(sem(f"in_w2_{s}"), 16 * loads)
            pe.wait_ge(sem("e_relu"), e * FT + FT + START["e_relu"])
            pe.wait_ge(sem("e_acc"), e * B + START["e_acc"])
            for b in range(B):
                for t in range(FT):
                    m = pe.matmul(bank(4 + s, 128, 128 * b), h_e[s][:, BANK * t + 128 * b:BANK * t + 128 * b + 128],
                                  w_slot[s][:, 512 + 128 * t:640 + 128 * t], start=t == 0, stop=t == FT - 1)
            m.then_inc(sem("e_y"), 1)

        def l1f_pe(pe):
            transpose4_pe(pe, xhN, 0, (sem("ln_xh"), 6 * B + B), sem("ln_t"), by_block=True)
            pe.wait_ge(sem("ln_T"), 6)
            pe.wait_ge(sem("in_experts"), 48)
            for b in range(B):
                m = pe.matmul(bank(1, NE, NE * b), xhT[:, b * S:(b + 1) * S], CT[:, :], start=True, stop=True)
            m.then_inc(sem_of("d_aff"), 1)
            transpose4_pe(pe, b3(xn2N), 2, (sem("ln_xh"), 7 * B + B), sem("ln_t"), by_block=True)
            hidden_pe(pe, 0, 0, 1)
            pe.wait_ge(*step("d_gate", 1))
            for b in range(B):
                t = pe.transpose(ps[0:NE, 6 * BANK + 128 * b:6 * BANK + 128 * b + 128], gate[:, b, :], ident)
            t.then_inc(sem_of("d_gate_t"), 1)
            pe.wait_ge(*step("d_gate_T", 1))
            for b in range(B):
                m = pe.matmul(bank(7, 128, 128 * b), gate_T[0:NE, 128 * b:128 * b + 128], B2[:, :], start=True, stop=True)
            m.then_inc(sem_of("d_b2"), 1)
            with pe.Fori(0, NE // 2 - 1) as it:
                e = it * 2
                hidden_pe(pe, e + 1, 1, it + 1)
                output_pe(pe, e, 0, it + 1)
                hidden_pe(pe, e + 2, 0, it + 2)
                output_pe(pe, e + 1, 1, it + 1)
            hidden_pe(pe, NE - 1, 1, NE // 2)
            output_pe(pe, NE - 2, 0, NE // 2)
            output_pe(pe, NE - 1, 1, NE // 2)

        def l1f_act(act):
            act.wait_ge(sem("ln_t"), 6)
            act.activation(xhT[:, :], bank(0), ACT.Copy).then_inc(sem("ln_T"), 1)
            act.wait_ge(sem("ln_t"), 7)
            act.activation(xn2T, bank(2), ACT.Copy).then_inc(sem("ln_T"), 1)
            act.wait_ge(*step("d_clamp", 1))
            act.activation(alpha, alpha, ACT.Exp, scale=-1.0).then_inc(sem_of("d_exp"), 1)
            with act.Fori(0, NE // 2) as it:
                for s in range(2):
                    e = it * 2 + s
                    act.wait_ge(sem("e_y"), e - 1 + START["e_y"])
                    for t in range(FT):
                        act.wait_ge(sem("e_h"), e * FT + t + 1 + START["e_h"])
                        act.activation(h_e[s][:, BANK * t:BANK * t + BANK], bank(t), ACT.Relu,
                                       bias=EC[:, bass.ds(2 * NE + e * FT + t, 1)]).then_inc(sem("e_relu"), 1)

        def l1f_dve(v):
            ln_dve(v, 6, (sem("x4_new"), 1))
            v.wait_ge(sem("ln_xh"), 6 * B + B)
            v.tensor_tensor(xN[:, :, :], xN[:, :, :], xhN[:, :, :], ALU.add).then_inc(sem_of("d_res"), 1)
            ln_dve(v, 7, step("d_res", 1), src=xhN[:, :, :], dst=b3(xn2N))
            v.wait_ge(*step("d_aff", 1))
            v.tensor_copy(aff, bank(1, NE * B).rearrange("p (b e) -> p b e", e=NE)).then_inc(sem_of("d_top"), 1)
            v.wait_ge(*step("d_top", 1))
            v.tensor_reduce(top, aff, AX.X, ALU.max).then_inc(sem_of("d_top"), 1)
            v.wait_ge(*step("d_top", 2))
            v.tensor_scalar(alpha, top, -87.0, None, ALU.max).then_inc(sem_of("d_clamp"), 1)
            v.tensor_tensor(score, aff, bc_in(top, NE), ALU.is_equal).then_inc(sem_of("d_sel"), 1)
            v.wait_ge(*step("d_sel", 1))
            v.tensor_tensor(score, score, bc_mid(const("first_weight")[:, 0:NE], B), ALU.mult).then_inc(sem_of("d_sel"), 1)
            v.wait_ge(*step("d_sel", 2))
            v.tensor_reduce(s_top, score, AX.X, ALU.max).then_inc(sem_of("d_sel"), 1)
            v.wait_ge(*step("d_sel", 3))
            v.tensor_tensor(gate, score, bc_in(s_top, NE), ALU.is_equal).then_inc(sem_of("d_sel"), 1)
            v.wait_ge(*step("d_exp", 1))
            v.tensor_scalar(alpha, alpha, 1.0, None, ALU.add).then_inc(sem_of("d_al"), 1)
            v.wait_ge(*step("d_al", 1))
            v.reciprocal(alpha, alpha).then_inc(sem_of("d_al"), 1)
            v.wait_ge(*step("d_al", 2))
            v.wait_ge(*step("d_sel", 4))
            v.tensor_tensor(gate, gate, bc_in(alpha, NE), ALU.mult).then_inc(sem_of("d_gate"), 1)

            def expert_in(e, s):
                v.wait_ge(sem("e_h"), (e - 1) * FT + START["e_h"])
                v.tensor_scalar(x_e[s], xn2T, EC[:, bass.ds(e, 1)], EC[:, bass.ds(NE + e, 1)], ALU.mult, ALU.add
                                ).then_inc(sem("e_x"), 1)

            def expert_out(e, s):
                v.wait_ge(sem("e_y"), e + 1 + START["e_y"])
                for b in range(B):
                    v.wait_ge(sem("e_acc"), e * B + b + 1 + START["e_acc"])
                    v.scalar_tensor_tensor(out=xN[:, b, :], in0=bank(4 + s, 128, 128 * b),
                                           scalar=small[:, bass.ds(168 + b * NE + e, 1)], in1=xN[:, b, :],
                                           op0=ALU.mult, op1=ALU.add).then_inc(sem("e_acc"), 1)

            v.wait_ge(sem("ln_T"), 7)
            for s in range(2):
                expert_in(s, s)
            v.wait_ge(*step("d_gate_t", 1))
            v.tensor_copy(gate_T[0:NE, :], ps[0:NE, 6 * BANK:7 * BANK]).then_inc(sem_of("d_gate_T"), 1)
            v.wait_ge(*step("d_b2", 1))
            v.wait_ge(*step("d_res", 1))
            v.tensor_tensor(xN_flat, xN_flat, bank(7), ALU.add).then_inc(sem("e_acc"), B)
            with v.Fori(0, NE // 2 - 1) as it:
                for s in range(2):
                    expert_in(it * 2 + 2 + s, s)
                    expert_out(it * 2 + s, s)
            for s in range(2):
                expert_out(NE - 2 + s, s)

        def l1f_pool(g):
            ln_pool(g, 6)
            ln_pool(g, 7)

        block = stack.enter_context(nc.Block())

        @block.sync
        def _(sp):
            l0x_sync(sp)
            x1_sync(sp)
            l1f_sync(sp)
            sp.wait_ge(sem("e_acc"), (NE + 1) * B + START["e_acc"])
            sp.wait_ge(sem("in_experts"), 48)
            sp.dma_start(out.rearrange("b s d -> s b d"), xN[:, :, :]).then_inc(sem("out"), 16)
            sp.wait_ge(sem("out"), 16)

        @block.tensor
        def _(pe):
            l0x_pe(pe)
            l0a_pe(pe)
            l0f_pe(pe)
            x1_pe(pe)
            l1a_pe(pe)
            l1f_pe(pe)

        @block.scalar
        def _(act):
            l0x_act(act)
            l0a_act(act)
            l0f_act(act)
            x1_act(act)
            l1a_act(act)
            l1f_act(act)

        @block.vector
        def _(v):
            l0x_dve(v)
            l0a_dve(v)
            l0f_dve(v)
            x1_dve(v)
            l1a_dve(v)
            l1f_dve(v)

        @block.gpsimd
        def _(g):
            l0x_pool(g)
            l0f_pool(g)
            ln_pool(g, 1)
            x1_init_pool(g, (0, 1))
            ln_pool(g, 2)
            x1_init_pool(g, (2, 3))
            ln_pool(g, 3)
            x1_pool(g)
            l1a_pool(g)
            l1f_pool(g)


def kernel(**inputs):
    import numpy as np
    import concourse.bacc as bacc
    from concourse.bass_utils import run_bass_kernel_spmd

    a = {n: np.asarray(v) for n, v in inputs.items()}

    def stacked(parts, axis):
        return np.ascontiguousarray(np.stack(parts, axis=axis))

    mix = np.zeros((H, HD, H, HD), np.float32)
    for h in range(H):
        mix[h, :, h, :] = a["L1_attn_mix_w"][h].T
    mats = {
        "L0x_q": a["L0_xattn_kernel_q"], "L0x_kT": a["L0_xattn_kernel_k"].T, "L0x_v": a["L0_xattn_kernel_v"],
        "L0a_q": a["L0_attn_w_q"], "L0a_k": a["L0_attn_w_k"], "L0a_v": a["L0_attn_w_v"], "L0a_o": a["L0_attn_w_o"],
        "L0f_rT": a["L0_ffn_W_r"].T, "L0f_kT": a["L0_ffn_W_k"].T, "L0f_vT": a["L0_ffn_W_v"].T,
        "L1x_q": a["L1_xattn_Wq"], "L1x_k": a["L1_xattn_Wk"], "L1x_v": a["L1_xattn_Wv"], "L1x_o": a["L1_xattn_Wo"],
        "L1a_qT": a["L1_attn_Wq"].T, "L1a_kT": a["L1_attn_Wk"].T, "L1a_vT": a["L1_attn_Wv"].T,
        "L1a_oT": a["L1_attn_Wo"].T, "L1a_eqT": a["L1_attn_Weq"].T, "L1a_ekT": a["L1_attn_Wek"].T,
        "mix": mix.reshape(D, D), "mix_rolled": np.roll(mix, 1, axis=3).reshape(D, D),
        "amp_ph": np.concatenate([a["L1_attn_amp_w"], a["L1_attn_ph_w"], np.zeros((96, D), np.float32)]).T,
    }
    cols = {
        "L0x_bq": a["L0_xattn_bias_q"], "L0x_bk": a["L0_xattn_bias_k"], "gain": np.broadcast_to(a["L0_attn_gain"], (D,)),
        "mu_r": a["L0_ffn_mu_r"], "mu_k": a["L0_ffn_mu_k"], "L1x_bq": a["L1_xattn_bq"], "L1x_bk": a["L1_xattn_bk"],
        "L1a_bq": a["L1_attn_bq"], "L1a_bk": a["L1_attn_bk"], "L1a_bv": a["L1_attn_bv"],
        "L1a_beq": a["L1_attn_beq"], "L1a_bek": a["L1_attn_bek"],
    }
    rows = {
        "L0x_bv": a["L0_xattn_bias_v"], "L1x_bv": a["L1_xattn_bv"], "L1x_bo": a["L1_xattn_bo"],
        "L1a_bv": a["L1_attn_bv"], "L1a_bo": a["L1_attn_bo"], "L1a_ln_g": a["L1_attn_ln_g"],
        "L1a_ln_b": a["L1_attn_ln_b"], "mix_b": a["L1_attn_mix_b"].reshape(D),
        "mix_b_rolled": np.roll(a["L1_attn_mix_b"], 1, axis=1).reshape(D),
        "amp_ph_b": np.concatenate([a["L1_attn_amp_b"], a["L1_attn_ph_b"], np.zeros(96, np.float32)]),
    }
    expert_cols = np.concatenate([a["L1_ffn_ln_g"].T, a["L1_ffn_ln_b"].T,
                                  a["L1_ffn_b1"].reshape(NE * FT, 128).T], axis=1)
    i = np.arange(128)
    first = np.zeros((128, 128))
    first[:, 0:NE] = NE - np.arange(NE)
    consts = {
        "identity": np.eye(128),
        "off_block": np.where(i[:, None] // HD == i[None, :] // HD, 0.0, -1.0e30),
        "head_mask": i[:, None] // HD == i[None, :],
        "decay": 0.5 * np.exp(-0.1 * np.abs(i[:, None] - i[None, :])),
        "first_weight": first,
    }
    arrays = {
        "x": a["x"], "ctx": a["ctx_1024"], "ctx_t": a["ctx_1024"].transpose(0, 2, 1),
        "mask0": a["mask_1xSxS2_ff0"].reshape(S, KEYS), "mask1": a["mask_Bx1x1xS2_fk0"].reshape(128, 64),
        "mats": stacked([mats[n] for n in MATS], 1), "cols": stacked([cols[n] for n in COLS], 1),
        "expert_cols": expert_cols, "rows": stacked([rows[n] for n in ROWV], 0),
        "centroids_t": a["L1_ffn_centroids"].T, "b2": a["L1_ffn_b2"], "w1": a["L1_ffn_w1"], "w2": a["L1_ffn_w2"],
        "consts": stacked([consts[n] for n in CONSTS], 1).astype(np.float32),
    }
    nc = bacc.Bacc("TRN2", target_bir_lowering=False, num_devices=1)
    given, args = {}, []
    for name, v in arrays.items():
        v = np.ascontiguousarray(v)
        given["in_" + name] = v
        args.append(nc.dram_tensor("in_" + name, v.shape, mybir.dt.from_np(v.dtype), kind="ExternalInput").ap())
    args.append(nc.dram_tensor("out_0", (B, S, D), F32, kind="ExternalOutput").ap())
    build(nc, *args)
    r = run_bass_kernel_spmd(nc, [given], core_ids=[0])
    return r.results[0]["out_0"]
```

```python
from contextlib import ExitStack
import math

import concourse.bass as bass
from concourse import mybir

F32 = mybir.dt.float32
BF16 = mybir.dt.bfloat16
ALU = mybir.AluOpType
ACT = mybir.ActivationFunctionType
AX = mybir.AxisListType

B, S, D = 4, 128, 128
KEYS = 2048
KT = KEYS // 128
H, HD = 16, 8
BANK = 512
NE, FF = 8, 512
FT = FF // 128
HQ = 4
UNITS = H // HQ
COMBOS = [(0, 0), (1, 0), (2, 0), (0, 1), (1, 1), (0, 2)]
ROWS = len(COMBOS) * HD
Q_RUNS = [((0, 3), (0, 3)), ((0, 2), (3, 5)), ((0, 1), (5, 6))]
K_RUNS = [(0, (0, 3)), (1, (3, 5)), (2, (5, 6))]
UNIT_DMAS = 2 * len(K_RUNS) + 5
MASK_ROW = 2 * ROWS
MAX_ROW = MASK_ROW + 3
PAIR_ROWS = MAX_ROW + 6
MATS = ["L0x_q", "L0x_kT", "L0x_v", "L1x_k", "L1x_v",
        "L0a_q", "L0a_k", "L0a_v", "L0a_o", "L0f_rT", "L0f_kT", "L0f_vT", "L1x_q", "L1x_o",
        "L1a_qT", "L1a_kT", "L1a_vT", "L1a_oT", "L1a_eqT", "L1a_ekT", "mix", "mix_rolled", "amp_ph"]
COLS = ["L0x_bq", "L0x_bk", "gain", "mu_r", "mu_k", "L1x_bq", "L1x_bk",
        "L1a_bq", "L1a_bk", "L1a_bv", "L1a_beq", "L1a_bek"]
ROWV = ["L0x_bv", "L1x_bv", "L1x_bo", "L1a_bv", "L1a_bo", "L1a_ln_g", "L1a_ln_b", "mix_b", "mix_b_rolled",
        "amp_ph_b"]
CONSTS = ["identity", "off_block", "head_mask", "decay", "first_weight"]


def build(nc, x, ctx, ctx_t, mask0, mask1, mats, cols, expert_cols, rows, centroids_t, b2, w1, w2,
          consts, out):
    with ExitStack() as stack:
        def sb(name, shape, dt=F32):
            return stack.enter_context(nc.sbuf_tensor(name, shape, dt))

        made = {}

        def sem(name):
            if name not in made:
                made[name] = stack.enter_context(nc.semaphore(name))
            return made[name]

        LINES = {
            "attn0_dve": [("a_wsq", 4), ("a_rw", 2), ("a_wn", 4), ("a_res", 1), ("a_headsq", 1), ("a_headw", 1),
                          ("a_headr", 1), ("a_qkn", 1), ("a_masked", 1), ("a_max", 1), ("a_shifted", 1), ("a_sum", 1),
                          ("a_rsum", 1), ("a_probs", 1)],
            "attn0_pe": [("a_wnt", 1), ("a_qk", 1), ("a_v", 1), ("a_scores", 1), ("a_mo", 1), ("a_out", 1)],
            "attn0_act": [("a_wnT", 1), ("a_sq", 1), ("a_headn", 1), ("a_vT", 1), ("a_exp", 1), ("a_mo_sb", 1)],
            "attn0_pool": [("a_half", 1), ("a_wroot", 1), ("a_w", 1)],
            "ffn0_dve": [("f_mix", 4), ("f_out", 1)],
            "ffn0_pe": [("f_r", 1), ("f_k", 1), ("f_v", 1)],
            "ffn0_act": [("f_gate", 1), ("f_relu", 1), ("f_ksq", 1)],
            "ffn0_pool": [("f_zero", 1), ("f_om", 1)],
            "attn1_dve": [("b_zero", 1), ("b_q", 2), ("b_z", 2), ("b_arg", 1), ("b_amp1", 3), ("b_vb", 1), ("b_s1", 1),
                          ("b_s2", 1), ("b_coef", 2), ("b_t1", 1), ("b_t3", 1), ("b_mixed", 1),
                          ("c_bo", 1), ("c_res", 1), ("c_shiftb", 1), ("c_gain", 1)],
            "attn1_pool": [("b_t2", 1)],
            "attn1_pe": [("b_proj", 5), ("b_amp", 1), ("b_vn", 1), ("b_sup", 2), ("c_all_t", 1), ("c_out", 1)],
            "attn1_act": [("b_vT", 1), ("b_k", 2), ("b_eamp", 1), ("b_tanh", 1), ("b_abs", 1), ("b_sin", 2),
                          ("c_oT", 1)],
            "ffn1_dve": [("d_res", 1), ("d_top", 2), ("d_clamp", 1), ("d_sel", 4), ("d_al", 2), ("d_gate", 1),
                         ("d_gate_T", 1)],
            "ffn1_pe": [("d_aff", 1), ("d_gate_t", 1), ("d_b2", 1)],
            "ffn1_act": [("d_exp", 1)],
        }
        LINE_OF = {name: line for line, steps in LINES.items() for name, _ in steps}

        def sem_of(name):
            return sem(LINE_OF[name])

        def step(name, count):
            steps = [n for n, _ in LINES[LINE_OF[name]]]
            return sem_of(name), sum(c for _, c in LINES[LINE_OF[name]][:steps.index(name)]) + count

        k_parts_d = nc.dram_tensor("k_parts_d", (B, 3, D, KEYS), BF16, kind="Internal").ap()
        q_stack = nc.dram_tensor("q_stack", (B, len(COMBOS), D, S), BF16, kind="Internal").ap()
        mask_parts_d = nc.dram_tensor("mask_parts_d", (3, B, KEYS), BF16, kind="Internal").ap()
        v_units = nc.dram_tensor("v_units", (B, UNITS, 128, KT * HQ * (HD + 1)), F32, kind="Internal").ap()

        W = sb("W", [128, len(MATS), 128])
        C = sb("C", [128, len(COLS)])
        EC = sb("EC", [128, NE * (2 + FT)])
        R = sb("R", [128, len(ROWV), 128])
        K = sb("K", [128, len(CONSTS), 128])
        CT = sb("CT", [128, NE])
        B2 = sb("B2", [NE, D])
        ident_bf = sb("ident_bf", [128, 128], BF16)

        def mat(n):
            return W[:, MATS.index(n), :]

        def col(n):
            i = COLS.index(n)
            return C[:, i:i + 1]

        def row(n):
            return R[:, ROWV.index(n), :]

        def const(n):
            return K[:, CONSTS.index(n), :]

        ident = const("identity")

        xN = sb("xN", [128, B, D])
        xhN = sb("xhN", [128, B, D])
        xhT = sb("xhT", [128, B * S])
        stats = sb("stats", [128, B, 6])
        mv = sb("mv", [128, B, 2])
        var_eps = sb("var_eps", [128, B])
        rstd = sb("rstd", [128, B])
        neg_half = sb("neg_half", [128, B])
        tA = sb("tA", [128, 1024])
        tB = sb("tB", [128, 1024])
        tC = sb("tC", [128, 1024])
        tD = sb("tD", [128, 1024])
        tE = sb("tE", [128, 1024])
        tF = sb("tF", [128, 1024])
        small = sb("small", [128, 256])
        ARENA = 38400
        arena = sb("arena", [128, ARENA])

        def carve(sizes):
            at, got = 0, []
            for words in sizes:
                got.append(arena[:, at:at + words])
                at += words
            assert at <= ARENA
            return got

        ps = stack.enter_context(nc.psum_tensor("ps", [128, 8 * BANK], F32))

        def bank(i, n=BANK, off=0):
            return ps[:, i * BANK + off:i * BANK + off + n]

        def b3(ap, inner=128):
            return ap.rearrange("p (b d) -> p b d", d=inner)

        def bc_mid(ap, n):
            return ap.rearrange("p (o m) -> p o m", o=1).broadcast_to([128, n, ap.shape[1]])

        def bc_in(ap, n):
            return ap.rearrange("p (m o) -> p m o", o=1).broadcast_to([128, ap.shape[1], n])

        def ln_dve(v, i, ready, src=None, dst=None, meanwhile=None):
            src = b3(xN_flat) if src is None else src
            dst = xhN if dst is None else dst
            for b in range(B):
                if b == 0:
                    v.wait_ge(*ready)
                v.bn_stats(stats[:, b, :], src[:, b, :]).then_inc(sem("ln_stats"), 1)
            for b in range(B):
                v.wait_ge(sem("ln_stats"), i * B + b + 1)
                v.bn_aggr(mv[:, b, :], stats[:, b, :]).then_inc(sem("ln_mv"), 1)
            v.wait_ge(sem("ln_mv"), i * B + B)
            v.tensor_scalar(var_eps[:, :], mv[:, :, 1], 1e-5, None, ALU.add).then_inc(sem("ln_ve"), 1)
            if meanwhile:
                meanwhile()
            v.wait_ge(sem("ln_rstd"), i + 1)
            for b in range(B):
                v.tensor_scalar(dst[:, b, :], src[:, b, :], mv[:, b, 0:1], rstd[:, b:b + 1],
                                ALU.subtract, ALU.mult).then_inc(sem("ln_xh"), 1)

        def ln_pool(g, i):
            g.wait_ge(sem("ln_ve"), i + 1)
            g.tensor_tensor(rstd[:, :], var_eps[:, :], neg_half[:, :], ALU.pow).then_inc(sem("ln_rstd"), 1)

        def transpose4_pe(pe, src, bk, ready, done, by_block=False):
            if not by_block:
                pe.wait_ge(*ready)
            for b in range(B):
                if by_block:
                    pe.wait_ge(ready[0], ready[1] - B + b + 1)
                t = pe.transpose(bank(bk, 128, 128 * b), src[:, b, :], ident)
            t.then_inc(done, 1)

        START_AT_ONE = ["s_masked", "pt_copied", "k_rest_done", "v_added", "x0_new", "scores0",
                        "k_out0", "k_out1", "v_out0", "v_out1", "p_t", "exp0", "nbias0", "k3_done"]

        xN_flat = xN[:, :, :].rearrange("p b d -> p (b d)")
        SQ_D = 1.0 / math.sqrt(D)

        (ctxN0, ctxN1, ctxT0, ctxT1, mask_sb, s_mask, p_nat, p_t, kp0, kp1, vb0, vb1, kr0, kr1, x_bv,
         mask1_f, mask1_r, mask1_p) = carve([
             2048, 2048, 2048, 2048, 2048, 2048, 2048, 2048, 3072, 3072, KT * H * 9, KT * H * 9, 512, 512, 512,
             64, 64, 96])
        ctxN = [b3(ctxN0), b3(ctxN1)]
        ctxT = [ctxT0, ctxT1]
        k_parts = [kp.bitcast(BF16).rearrange("p (j n) -> p j n", j=3) for kp in (kp0, kp1)]
        vbuf = [vb.rearrange("p (u t g e) -> p u t g e", u=UNITS, t=KT, g=HQ) for vb in (vb0, vb1)]
        k_rest = [kr0, kr1]
        mparts = mask1_p.bitcast(BF16).rearrange("p (j n) -> p j n", j=3)
        qT, qk_T = tA[:, 0:512], tB[:, 0:512]
        qk_b = [tC[:, 0:128], tC[:, 128:256]]
        oT0 = [tD[:, 0:128], tD[:, 128:256]]
        c_q, mx, mc, nbias, rsum, rinv, cb = (small[:, 8 * i:8 * i + 8] for i in range(7))

        def l0x_sync(sp):
            for name in START_AT_ONE:
                sp.sem_inc(sem(name), 1)
            for name, value in START.items():
                sp.sem_inc(sem(name), value)
            sp.dma_start(xN[:, :, :], x.rearrange("b s d -> s b d")).then_inc(sem("in_x"), 16)
            sp.dma_start(K[:, :, :], consts).then_inc(sem("in_consts"), 16)
            sp.dma_start(W[:, 0:5, :], mats[:, 0:5, :]).then_inc(sem("in_mats_first"), 16)
            sp.dma_start(C[:, :], cols).then_inc(sem("in_small"), 16)
            with sp.Fori(0, B // 2) as it:
                for s in range(2):
                    sp.wait_ge(sem("o0_done"), it * 2 + s - 1 + START["o0_done"])
                    sp.dma_start(ctxT[s], ctx_t[bass.ds(it * 2 + s, 1), :, :].rearrange("o d n -> (o d) n")
                                 ).then_inc(sem(f"in_ctx{s}"), 16)
                    if s == 0:
                        sp.wait_ge(sem("in_mask0"), 16)
                    for half in range(2):
                        t = slice(half * KT // 2, (half + 1) * KT // 2)
                        sp.dma_start(ctxN[s][:, t, :],
                                     ctx[bass.ds(it * 2 + s, 1), half * KEYS // 2:(half + 1) * KEYS // 2, :]
                                     .rearrange("o (t p) d -> p (o t) d", p=128)).then_inc(sem(f"in_ctxN{s}"), 16)

        def l0x_store_k(act, s, n):
            act.wait_ge(sem("k1_done"), n * 4 + 4)
            act.wait_ge(sem("k3_done"), n * 4 + 4 + 1)
            act.dma_start(k_parts_d[bass.ds(n, 1), :, :, :].rearrange("o j p n -> (o p) j n"),
                          k_parts[s]).then_inc(sem(f"k_out{s}"), 16)

        def l0x_store_v(act, s, n):
            act.wait_ge(sem("v_added"), n * 4 + 4 + 1)
            act.dma_start(v_units[bass.ds(n, 1), :, :, :].rearrange("o u k n -> k (o u) n"),
                          vbuf[s].rearrange("p u t g e -> p u (t g e)")).then_inc(sem(f"v_out{s}"), 16)

        T_BANK = (4, 6, 5, 4)

        def l0x_scores_pe(pe, s, n, it):
            pe.wait_ge(sem(f"in_ctx{s}"), it * 16 + 16)
            pe.wait_ge(sem("qk_b"), n + 1)
            pe.wait_ge(sem("s_masked"), n + 1)
            for c in range(4):
                m = pe.matmul(bank(c), qk_b[s], ctxT[s][:, c * BANK:(c + 1) * BANK], start=True, stop=True)
            m.then_inc(sem("scores0"), 1)

        def l0x_kv_pe(pe, s, n, c):
            if c == 0:
                pe.wait_ge(sem("pt_copied"), n * 4 + 1)
            if c >= 2:
                pe.wait_ge(sem("k_rest_done"), n * 4 + c)
            pe.matmul(bank(4 + 2 * (c % 2)), mat("L1x_k"), ctxT[s][:, c * BANK:(c + 1) * BANK],
                      start=True, stop=True).then_inc(sem("k_proj"), 1)
            if c >= 1:
                pe.wait_ge(sem("v_added"), n * 4 + c + 1)
            for t in range(4 * c, 4 * c + 4):
                m = pe.matmul(bank(5, 128, 128 * (t % 4)), ctxT[s][:, t * 128:(t + 1) * 128],
                              mat("L1x_v"), start=True, stop=True)
            m.then_inc(sem("v_proj"), 1)

        def l0x_probs_pe(pe, s, n, it):
            pe.wait_ge(sem("exp0"), n + 1 + 1)
            for gr in range(4):
                if gr == 0:
                    pe.wait_ge(sem("k_rest_done"), n * 4 + 4 + 1)
                if gr == 2:
                    pe.wait_ge(sem("v_added"), n * 4 + 4 + 1)
                if gr == 3:
                    pe.wait_ge(sem("pt_copied"), n * 4 + 1 + 1)
                for t in range(4 * gr, 4 * gr + 4):
                    m = pe.transpose(bank(T_BANK[gr], 128, 128 * (t % 4)), p_nat[:, t * 128:(t + 1) * 128], ident)
                m.then_inc(sem("p_t"), 1)
            pe.wait_ge(sem(f"in_ctxN{s}"), it * 32 + 32)
            pe.wait_ge(sem("x0_new"), n + 1)
            for gr in range(4):
                pe.wait_ge(sem("pt_copied"), n * 4 + gr + 1 + 1)
                for t in range(4 * gr, 4 * gr + 4):
                    m = pe.matmul(bank(7, 128), ctxN[s][:, t, :], p_t[:, t * 128:(t + 1) * 128],
                                  start=t == 0, stop=t == KT - 1)
            m.then_inc(sem("o0_done"), 1)

        def l0x_out_pe(pe, s, n):
            pe.wait_ge(sem("oT0_sb"), n + 1)
            pe.matmul(bank(7, 128, 128), oT0[s], mat("L0x_v"), start=True, stop=True).then_inc(sem("y0"), 1)

        def l0x_pe(pe):
            pe.wait_ge(sem("in_consts"), 16)
            transpose4_pe(pe, xhN, 0, (sem("ln_xh"), 0 * B + B), sem("ln_t"), by_block=True)
            pe.wait_ge(sem("in_mats_first"), 16)
            pe.wait_ge(sem("ln_T"), 1)
            pe.matmul(bank(1), mat("L0x_q"), xhT[:, :], start=True, stop=True).then_inc(sem("q0"), 1)
            pe.wait_ge(sem("q0_sb"), 1)
            pe.matmul(bank(2), mat("L0x_kT"), qT, start=True, stop=True).then_inc(sem("qk0"), 1)
            for b in range(B):
                m = pe.matmul(bank(3, 1, b), qT[:, b * S:(b + 1) * S], col("L0x_bk"), start=True, stop=True)
            m.then_inc(sem("c0"), 1)
            pe.wait_ge(sem("c0_sb"), 1)
            with pe.Fori(0, B // 2) as it:
                n = it * 2
                l0x_scores_pe(pe, 0, n, it)
                for c in range(4):
                    l0x_kv_pe(pe, 0, n, c)
                l0x_scores_pe(pe, 1, n + 1, it)
                l0x_probs_pe(pe, 0, n, it)
                for c in range(4):
                    l0x_kv_pe(pe, 1, n + 1, c)
                    if c == 0:
                        l0x_out_pe(pe, 0, n)
                l0x_probs_pe(pe, 1, n + 1, it)
                l0x_out_pe(pe, 1, n + 1)

        def l0x_act(act):
            act.wait_ge(sem("in_x"), 16)
            act.dma_start(R[:, :, :], rows.partition_broadcast(128)).then_inc(sem("in_rows"), 16)
            act.dma_start(mask1_f, mask1).then_inc(sem("in_mask1"), 16)
            act.dma_start(mask_sb, mask0).then_inc(sem("in_mask0"), 16)
            act.dma_start(W[:, 5:len(MATS), :], mats[:, 5:len(MATS), :]).then_inc(sem("in_mats"), 16)
            act.dma_start(EC[:, :], expert_cols).then_inc(sem("in_experts"), 16)
            act.dma_start(CT[:, :], centroids_t).then_inc(sem("in_experts"), 16)
            act.dma_start(B2[:, :], b2).then_inc(sem("in_experts"), 16)
            act.wait_ge(sem("ln_t"), 1)
            act.activation(xhT[:, :], bank(0), ACT.Copy).then_inc(sem("ln_T"), 1)
            act.wait_ge(sem("in_small"), 16)
            act.wait_ge(sem("q0"), 1)
            act.activation(qT, bank(1), ACT.Identity, bias=col("L0x_bq")).then_inc(sem("q0_sb"), 1)
            act.wait_ge(sem("qk0"), 1)
            act.activation(qk_T, bank(2), ACT.Copy, scale=SQ_D).then_inc(sem("qk0_sb"), 1)

            def exps(s, n):
                act.wait_ge(sem("nbias0"), n + 1 + 1)
                act.wait_ge(sem("p_t"), n * 4 + 1)
                act.activation(p_nat, s_mask, ACT.Exp, bias=nbias[:, s:s + 1],
                               accum_out=rsum[:, s:s + 1]).then_inc(sem("exp0"), 1)

            def second_parts(s, n, c):
                act.wait_ge(sem("k_rest_done"), n * 4 + c + 1 + 1)
                act.activation(k_parts[s][:, 1, c * BANK:(c + 1) * BANK], k_rest[c % 2], ACT.Copy
                               ).then_inc(sem("k2_done"), 1)

            with act.Fori(0, B // 2) as it:
                for s in range(2):
                    n = it * 2 + s
                    for c in range(4):
                        act.wait_ge(sem("k_proj"), n * 4 + c + 1)
                        if c == 0:
                            act.wait_ge(sem(f"k_out{s}"), it * 16 + 1)
                        act.activation(k_parts[s][:, 0, c * BANK:(c + 1) * BANK], bank(4 + 2 * (c % 2)),
                                       ACT.Identity, bias=col("L1x_bk")).then_inc(sem("k1_done"), 1)
                        if c > 0:
                            second_parts(s, n, c - 1)
                        if s == 1 and c == 0:
                            l0x_store_k(act, 0, n - 1)
                    second_parts(s, n, 3)
                    if s == 0:
                        exps(0, n)
                    if s == 1:
                        l0x_store_v(act, 0, n - 1)
                    act.wait_ge(sem("o0_done"), n + START["o0_done"])
                    for gr in range(4):
                        act.wait_ge(sem("p_t"), n * 4 + gr + 1 + 1)
                        act.activation(p_t[:, gr * BANK:(gr + 1) * BANK], bank(T_BANK[gr]), ACT.Copy
                                       ).then_inc(sem("pt_copied"), 1)
                    if s == 0:
                        exps(1, n + 1)
                    act.wait_ge(sem("o0_done"), n + 1 + START["o0_done"])
                    act.activation(oT0[s], bank(7, 128), ACT.Copy).then_inc(sem("oT0_sb"), 1)
                    if s == 1:
                        l0x_store_k(act, 1, n)
                        l0x_store_v(act, 1, n)

        def l0x_dve(v):
            ln_dve(v, 0, (sem("in_x"), 16))
            for s in range(2):
                v.memset(vbuf[s][:, :, :, :, HD], 1.0).then_inc(sem("v_ones"), 1)
            v.wait_ge(sem("in_rows"), 16)
            v.tensor_tensor(b3(x_bv), xN[:, :, :], bc_mid(row("L0x_bv"), B), ALU.add).then_inc(sem("x_bv"), 1)
            x1_early_dve(v)
            v.wait_ge(sem("qk0_sb"), 1)

            def finish(s, n):
                v.wait_ge(sem("exp0"), n + 1 + 1)
                v.reciprocal(rinv[:, s:s + 1], rsum[:, s:s + 1]).then_inc(sem("rinv0"), 1)
                v.wait_ge(sem("rinv0"), n + 1)
                v.wait_ge(sem("y0"), n + 1)
                v.scalar_tensor_tensor(out=xN_flat[:, bass.ds(n * 128, 128)], in0=bank(7, 128, 128),
                                       scalar=rinv[:, s:s + 1], in1=x_bv[:, bass.ds(n * 128, 128)],
                                       op0=ALU.mult, op1=ALU.add).then_inc(sem("x0_new"), 1)

            v.memset(tB[:, 512:768], 0.0).then_inc(sem("qk_end"), 1)
            for s in range(2):
                v.tensor_copy(qk_b[s], qk_T[:, s * 128:s * 128 + 128]).then_inc(sem("qk_b"), 1)
            v.wait_ge(sem("c0"), 1)
            v.tensor_scalar(c_q[:, 0:B], bank(3, B), SQ_D, None, ALU.mult).then_inc(sem("c0_sb"), 1)
            v.wait_ge(sem("c0_sb"), 1)
            v.wait_ge(sem("in_mask0"), 16)
            v.wait_ge(sem("in_small"), 16)
            v.wait_ge(sem("x_bv"), 1)
            l0a_prepare_dve(v)
            l0a_weights_dve(v)
            v.wait_ge(sem("qk_end"), 1)
            with v.Fori(0, B // 2) as it:
                for s in range(2):
                    n = it * 2 + s
                    v.wait_ge(sem("scores0"), n + 1 + 1)
                    v.wait_ge(sem("exp0"), n + 1)
                    v.wait_ge(sem("nbias0"), n + 1)
                    v.tensor_copy(cb[:, s:s + 1], c_q[:, bass.ds(n, 1)]).then_inc(sem("c_b"), 1)
                    v.tensor_tensor_reduce(s_mask, ps[:, 0:KEYS], mask_sb, 1.0, -3.0e38, ALU.add, ALU.max,
                                           mx[:, s:s + 1]).then_inc(sem("s_masked"), 1)
                    v.wait_ge(sem("s_masked"), n + 1 + 1)
                    v.wait_ge(sem("c_b"), n + 1)
                    v.tensor_tensor(mc[:, s:s + 1], mx[:, s:s + 1], cb[:, s:s + 1], ALU.add
                                    ).then_inc(sem("mc0"), 1)
                    v.wait_ge(sem("mc0"), n + 1)
                    v.tensor_tensor(nbias[:, s:s + 1], cb[:, s:s + 1], mc[:, s:s + 1], ALU.subtract
                                    ).then_inc(sem("nbias0"), 1)
                    for c in range(4):
                        v.wait_ge(sem("v_proj"), n * 4 + c + 1)
                        if c == 0:
                            v.wait_ge(sem(f"v_out{s}"), it * 16 + 1)
                        v.tensor_tensor(vbuf[s][:, :, 4 * c:4 * c + 4, :, 0:HD],
                                        bank(5).rearrange("p (t u g d) -> p u t g d", t=4, u=UNITS, g=HQ),
                                        row("L1x_bv").rearrange("p (u o g d) -> p u o g d", u=UNITS, o=1, g=HQ)
                                        .broadcast_to([128, UNITS, 4, HQ, HD]),
                                        ALU.add).then_inc(sem("v_added"), 1)
                        v.wait_ge(sem("k1_done"), n * 4 + c + 1)
                        v.wait_ge(sem("k3_done"), it * 8 + (s * 4 + c - 1 if s * 4 + c > 1 else 0) + 1)
                        v.scalar_tensor_tensor(out=k_rest[c % 2], in0=bank(4 + 2 * (c % 2)), scalar=col("L1x_bk"),
                                               in1=k_parts[s][:, 0, c * BANK:(c + 1) * BANK],
                                               op0=ALU.add, op1=ALU.subtract).then_inc(sem("k_rest_done"), 1)
                        if s == 1 and c == 0:
                            finish(0, n - 1)
                for s in range(2):
                    v.wait_ge(sem("scores0"), it * 2 + 2 + 1)
                    v.tensor_copy(qk_b[s], tB[:, bass.ds(it * 256 + 256 + s * 128, 128)]).then_inc(sem("qk_b"), 1)
                finish(1, it * 2 + 1)

        def l0x_pool(g):
            g.memset(neg_half[:, :], -0.5).then_inc(sem("pool_const"), 1)
            g.wait_ge(sem("pool_const"), 1)
            ln_pool(g, 0)
            x1_early_pool(g)
            g.wait_ge(sem("in_mask1"), 16)
            g.tensor_scalar(mask1_r, mask1_f, -1.0e9, None, ALU.mult).then_inc(sem("mask1_c"), 1)
            for j in range(3):
                g.wait_ge(sem("mask1_c"), 2 * j + 1)
                g.tensor_copy(mparts[:, j, :], mask1_r).then_inc(sem("mask1_c"), 1)
                if j < 2:
                    g.wait_ge(sem("mask1_c"), 2 * j + 2)
                    g.tensor_tensor(mask1_r, mask1_r, mparts[:, j, :], ALU.subtract).then_inc(sem("mask1_c"), 1)
            g.wait_ge(sem("mask1_c"), 6)
            for j in range(3):
                g.dma_start(mask_parts_d[j].rearrange("b (p n) -> (b p) n", n=64), mparts[:, j, :]
                            ).then_inc(sem("mask1_out"), 16)
            g.wait_ge(sem("v_ones"), 2)
            l0a_prepare_pool(g)
            with g.Fori(0, B // 2) as it:
                for s in range(2):
                    n = it * 2 + s
                    for c in range(4):
                        at = slice(c * BANK, (c + 1) * BANK)
                        g.wait_ge(sem("k2_done"), n * 4 + c + 1)
                        g.tensor_tensor(k_parts[s][:, 2, at], k_rest[c % 2], k_parts[s][:, 1, at], ALU.subtract
                                        ).then_inc(sem("k3_done"), 1)

        w_norm, r_scale, om = small[:, 64:68], small[:, 72:76], small[:, 80:82]
        half = small[:, 84:88]
        a_mx, a_sum, a_r = small[:, 88:92], small[:, 92:96], small[:, 96:100]
        wn, wnT, vT_a = tE[:, 0:512], tF[:, 0:512], tE[:, 512:1024]
        head_sq, head_n, head_w, head_r = (tB[:, 128 * i_:128 * i_ + 128] for i_ in range(4))
        RES = 0.5 / math.sqrt(0.5)
        EPS_W = 1e-4

        def l0a_prepare_dve(v):
            v.wait_ge(sem("in_mats"), 16)
            for i_, n_ in enumerate(["L0a_q", "L0a_k", "L0a_v", "L0a_o"]):
                v.tensor_tensor_reduce(tF[:, 512 + 128 * i_:640 + 128 * i_], mat(n_), mat(n_), 1.0, 0.0,
                                       ALU.mult, ALU.add, w_norm[:, i_:i_ + 1]).then_inc(sem_of("a_wsq"), 1)

        def l0a_prepare_pool(g):
            g.memset(half, 0.5).then_inc(sem_of("a_half"), 1)
            g.wait_ge(*step("a_half", 1))
            g.wait_ge(*step("a_wsq", 4))
            g.tensor_tensor(w_norm, w_norm, half, ALU.pow).then_inc(sem_of("a_wroot"), 1)
            g.wait_ge(*step("a_wroot", 1))
            g.tensor_scalar(w_norm, w_norm, SQ_D, EPS_W, ALU.mult, ALU.add).then_inc(sem_of("a_w"), 1)

        def l0a_weights_dve(v):
            v.wait_ge(sem("in_small"), 16)
            v.wait_ge(*step("a_w", 1))
            v.reciprocal(r_scale, w_norm).then_inc(sem_of("a_rw"), 1)
            v.wait_ge(*step("a_rw", 1))
            v.tensor_scalar(r_scale, r_scale, col("gain"), SQ_D, ALU.mult, ALU.mult).then_inc(sem_of("a_rw"), 1)
            v.wait_ge(*step("a_rw", 2))
            for i_, n_ in enumerate(["L0a_q", "L0a_k", "L0a_v", "L0a_o"]):
                v.tensor_scalar(wn[:, 128 * i_:128 * i_ + 128], mat(n_), r_scale[:, i_:i_ + 1], None, ALU.mult
                                ).then_inc(sem_of("a_wn"), 1)

        def l0a_dve(v):
            ln_dve(v, 1, (sem("x0_new"), B + 1))
            v.wait_ge(sem("ln_xh"), 1 * B + B)
            v.scalar_tensor_tensor(out=xN_flat, in0=xhN[:, :, :].rearrange("p b d -> p (b d)"), scalar=RES,
                                   in1=xN_flat, op0=ALU.mult, op1=ALU.add).then_inc(sem_of("a_res"), 1)
            v.wait_ge(*step("a_sq", 1))
            v.tensor_reduce(head_sq, tA[:, :].rearrange("p (g d) -> p g d", d=HD), AX.X, ALU.add
                            ).then_inc(sem_of("a_headsq"), 1)
            v.wait_ge(*step("a_headn", 1))
            v.tensor_scalar(head_w, head_n, EPS_W, None, ALU.add).then_inc(sem_of("a_headw"), 1)
            v.wait_ge(*step("a_headw", 1))
            v.reciprocal(head_r, head_w).then_inc(sem_of("a_headr"), 1)
            v.wait_ge(*step("a_headr", 1))
            v.tensor_tensor(tC[:, :].rearrange("p (g d) -> p g d", d=HD),
                            ps[:, 2 * BANK:4 * BANK].rearrange("p (g d) -> p g d", d=HD), bc_in(head_r, HD),
                            ALU.mult).then_inc(sem_of("a_qkn"), 1)
            v.wait_ge(*step("a_scores", 1))
            v.tensor_tensor(b3(tD[:, 0:512]), b3(bank(5)), bc_mid(const("off_block"), B), ALU.add
                            ).then_inc(sem_of("a_masked"), 1)
            v.wait_ge(*step("a_masked", 1))
            v.tensor_reduce(a_mx, b3(tD[:, 0:512]), AX.X, ALU.max).then_inc(sem_of("a_max"), 1)
            v.wait_ge(*step("a_max", 1))
            v.tensor_tensor(b3(tD[:, 0:512]), b3(tD[:, 0:512]), bc_in(a_mx, 128), ALU.subtract
                            ).then_inc(sem_of("a_shifted"), 1)
            v.wait_ge(*step("a_exp", 1))
            v.tensor_reduce(a_sum, b3(tD[:, 512:1024]), AX.X, ALU.add).then_inc(sem_of("a_sum"), 1)
            v.wait_ge(*step("a_sum", 1))
            v.reciprocal(a_r, a_sum).then_inc(sem_of("a_rsum"), 1)
            v.wait_ge(*step("a_rsum", 1))
            v.tensor_tensor(b3(tD[:, 0:512]), b3(tD[:, 512:1024]), bc_in(a_r, 128), ALU.mult
                            ).then_inc(sem_of("a_probs"), 1)
            v.wait_ge(*step("a_out", 1))
            v.wait_ge(*step("a_res", 1))
            v.scalar_tensor_tensor(out=xN_flat, in0=bank(7), scalar=RES, in1=xN_flat, op0=ALU.mult, op1=ALU.add
                                   ).then_inc(sem("x1_new"), 1)

        def l0a_pe(pe):
            pe.wait_ge(*step("a_wn", 4))
            transpose4_pe(pe, b3(wn), 0, step("a_wn", 4), sem_of("a_wnt"))
            transpose4_pe(pe, xhN, 1, (sem("ln_xh"), 1 * B + B), sem("ln_t"), by_block=True)
            pe.wait_ge(*step("a_wnT", 1))
            pe.wait_ge(sem("ln_T"), 2)
            for b in range(B):
                m = pe.matmul(bank(2 + b // 2, 256, 256 * (b % 2)), xhT[:, b * S:(b + 1) * S], wnT[:, 0:256],
                              start=True, stop=True)
            m.then_inc(sem_of("a_qk"), 1)
            pe.matmul(bank(4), wnT[:, 256:384], xhT[:, :], start=True, stop=True).then_inc(sem_of("a_v"), 1)
            pe.wait_ge(*step("a_qkn", 1))
            for b in range(B):
                m = pe.matmul(bank(5, 128, 128 * b), tC[:, 256 * b:256 * b + 128], tC[:, 256 * b + 128:256 * b + 256],
                              start=True, stop=True)
            m.then_inc(sem_of("a_scores"), 1)
            pe.wait_ge(*step("a_probs", 1))
            for b in range(B):
                m = pe.matmul(bank(6, 128, 128 * b), tD[:, 128 * b:128 * b + 128], wnT[:, 384:512],
                              start=True, stop=True)
            m.then_inc(sem_of("a_mo"), 1)
            pe.wait_ge(*step("a_vT", 1))
            pe.wait_ge(*step("a_mo_sb", 1))
            for b in range(B):
                m = pe.matmul(bank(7, 128, 128 * b), vT_a[:, b * S:(b + 1) * S], tA[:, 128 * b:128 * b + 128],
                              start=True, stop=True)
            m.then_inc(sem_of("a_out"), 1)

        def l0a_act(act):
            act.wait_ge(*step("a_wnt", 1))
            act.activation(wnT, bank(0), ACT.Copy).then_inc(sem_of("a_wnT"), 1)
            act.wait_ge(sem("ln_t"), 2)
            act.activation(xhT[:, :], bank(1), ACT.Copy).then_inc(sem("ln_T"), 1)
            act.wait_ge(*step("a_qk", 1))
            act.activation(tA[:, :], ps[:, 2 * BANK:4 * BANK], ACT.Square).then_inc(sem_of("a_sq"), 1)
            act.wait_ge(*step("a_headsq", 1))
            act.activation(head_n, head_sq, ACT.Sqrt, scale=1.0 / HD).then_inc(sem_of("a_headn"), 1)
            act.wait_ge(*step("a_v", 1))
            act.activation(vT_a, bank(4), ACT.Copy).then_inc(sem_of("a_vT"), 1)
            act.wait_ge(*step("a_shifted", 1))
            act.activation(tD[:, 512:1024], tD[:, 0:512], ACT.Exp, scale=1.0 / math.sqrt(S)
                           ).then_inc(sem_of("a_exp"), 1)
            act.wait_ge(*step("a_mo", 1))
            act.activation(tA[:, 0:512], bank(6), ACT.Copy).then_inc(sem_of("a_mo_sb"), 1)

        x_pad = mask_sb[:, 0:B * (S + 1)].rearrange("p (b s) -> p b s", s=S + 1)
        x_r, x_k = tB[:, 0:512], tB[:, 512:1024]

        def l0f_pool(g):
            g.wait_ge(sem("x0_new"), B + 1)
            g.memset(x_pad[:, :, 0:1], 0.0).then_inc(sem_of("f_zero"), 1)
            g.tensor_scalar(om, C[:, 3:5], -1.0, 1.0, ALU.mult, ALU.add).then_inc(sem_of("f_om"), 1)

        def l0f_dve(v):
            ln_dve(v, 2, (sem("x1_new"), 1))
            v.wait_ge(*step("f_om", 1))
            v.wait_ge(*step("f_zero", 1))
            v.wait_ge(sem("ln_T"), 3)
            for i_, dst in enumerate((x_r, x_k)):
                before = b3(tC[:, 512 * i_:512 * i_ + 512])
                v.tensor_scalar(before, x_pad[:, :, 0:S], om[:, i_:i_ + 1], None, ALU.mult
                                ).then_inc(sem_of("f_mix"), 1)
                v.wait_ge(*step("f_mix", 2 * i_ + 1))
                v.scalar_tensor_tensor(out=b3(dst), in0=x_pad[:, :, 1:S + 1], scalar=C[:, 3 + i_:4 + i_], in1=before,
                                       op0=ALU.mult, op1=ALU.add).then_inc(sem_of("f_mix"), 1)
            v.wait_ge(*step("f_gate", 1))
            v.wait_ge(*step("f_v", 1))
            v.tensor_tensor(tC[:, 0:512], bank(3), tE[:, 0:512], ALU.mult).then_inc(sem_of("f_out"), 1)
            v.wait_ge(*step("f_out", 1))
            v.tensor_tensor(xN_flat, xN_flat, tC[:, 0:512], ALU.add).then_inc(sem("x2_new"), 1)

        def l0f_pe(pe):
            transpose4_pe(pe, xhN, 0, (sem("ln_xh"), 2 * B + B), sem("ln_t"), by_block=True)
            pe.wait_ge(*step("f_mix", 2))
            for b in range(B):
                m = pe.matmul(bank(1, 128, 128 * b), x_r[:, b * S:(b + 1) * S], mat("L0f_rT"), start=True, stop=True)
            m.then_inc(sem_of("f_r"), 1)
            pe.wait_ge(*step("f_mix", 4))
            pe.matmul(bank(2), mat("L0f_kT"), x_k, start=True, stop=True).then_inc(sem_of("f_k"), 1)
            pe.wait_ge(*step("f_ksq", 1))
            for b in range(B):
                m = pe.matmul(bank(3, 128, 128 * b), tD[:, 512 + b * S:512 + (b + 1) * S], mat("L0f_vT"),
                              start=True, stop=True)
            m.then_inc(sem_of("f_v"), 1)

        def l0f_act(act):
            act.wait_ge(sem("ln_t"), 3)
            act.wait_ge(*step("f_zero", 1))
            act.activation(x_pad[:, :, 1:S + 1], b3(bank(0)), ACT.Copy).then_inc(sem("ln_T"), 1)
            act.wait_ge(*step("f_r", 1))
            act.activation(tE[:, 0:512], bank(1), ACT.Sigmoid).then_inc(sem_of("f_gate"), 1)
            act.wait_ge(*step("f_k", 1))
            act.activation(tD[:, 0:512], bank(2), ACT.Relu).then_inc(sem_of("f_relu"), 1)
            act.wait_ge(*step("f_relu", 1))
            act.activation(tD[:, 512:1024], tD[:, 0:512], ACT.Square).then_inc(sem_of("f_ksq"), 1)

        PV_COLS = HD + 1
        GROUPS = KT // 2
        STEPS = UNITS * GROUPS
        CHUNKS = HQ * KEYS // BANK
        AHEAD = CHUNKS + CHUNKS // 2
        P_AT, Q_AT = UNITS * KEYS + KEYS, 33600
        V_AT, V_WORDS, Q_WORDS = P_AT + 4 * 2 * BANK, KT * HQ * PV_COLS, 2 * S
        k_slot = [arena[:, u * KEYS:(u + 1) * KEYS].bitcast(BF16).rearrange("p (g n) -> p g n", g=2)
                  for u in range(UNITS)]
        p_ring = [arena[:, P_AT + 2 * BANK * i_:P_AT + 2 * BANK * (i_ + 1)] for i_ in range(4)]
        v_slot = [arena[:, V_AT + V_WORDS * u:V_AT + V_WORDS * (u + 1)] for u in range(UNITS)]
        q_words = [arena[:, Q_AT + Q_WORDS * u:Q_AT + Q_WORDS * (u + 1)] for u in range(UNITS)]
        q_slot = [q.bitcast(BF16).rearrange("p (a g q) -> p a g q", g=2, a=2) for q in q_words]
        q_f = tA[:, 0:512]
        q_part = tB[:, 0:768].bitcast(BF16).rearrange("p (j n) -> p j n", j=3)
        chunk_max = [tC[:, 16 * i_:16 * i_ + 16] for i_ in range(2)]
        neg_max = [tC[:, 32 + 4 * i_:36 + 4 * i_] for i_ in range(2)]
        m_rest = [tC[:, 40 + 4 * i_:44 + 4 * i_] for i_ in range(2)]
        m_part = [tC[:, 64 + 8 * i_:70 + 8 * i_].bitcast(BF16).rearrange("p (j h) -> p j h", j=3) for i_ in range(2)]
        m_cols = [tC[:, 96 + 32 * i_:114 + 32 * i_].bitcast(BF16).rearrange("p (h c) -> p h c", c=9) for i_ in range(2)]
        o_rcp = tC[:, 180:184]
        m_none = tC[:, 184:188]
        m_none3 = tC[:, 188:194].rearrange("p (g j) -> p g j", j=3)
        o_raw = tC[:, 256:384]
        zeros = tC[:, 384:512]
        o_all = tD[:, 0:512]
        o_T = tE[:, 0:512]
        ONES_PAIR = 1.0019378662109375
        START = {"o0_done": 2, "exp1": 2, "pv_chunk": 4, "pv_copied": 1, "o1_t": 1, "o1_norm": 1}

        def x1_init_pool(g, slots):
            for i_ in slots:
                g.memset(arena[:, i_ * KEYS:(i_ + 1) * KEYS], ONES_PAIR).then_inc(sem("k_ones"), 1)

        def x1_early_pool(g):
            for i_ in range(UNITS):
                g.memset(q_words[i_], 0.0).then_inc(sem("q_zero"), 1)

        def x1_early_dve(v):
            v.wait_ge(sem("q_zero"), UNITS)
            for i_ in range(UNITS):
                v.memset(q_words[i_][MASK_ROW:MAX_ROW, :], ONES_PAIR).then_inc(sem("q_ones"), 1)

        def x1_load_kv(sp, b, u):
            for a_ in range(2):
                at = 4 * HD * u + 2 * HD * a_
                for j, (c0, c1) in K_RUNS:
                    sp.dma_start(k_slot[u][ROWS * a_ + c0 * HD:ROWS * a_ + c1 * HD, :, :].rearrange("r g n -> r (g n)"),
                                 k_parts_d[bass.ds(b, 1), j, at:at + 2 * HD, :]
                                 .rearrange("o (d g) n -> o d (g n)", g=2).broadcast_to([c1 - c0, HD, 2 * KEYS])
                                 ).then_inc(sem(f"unit_in{u}"), 16)
            for g_ in range(2):
                sp.dma_start(k_slot[u][MASK_ROW:MAX_ROW, g_, :],
                             mask_parts_d[:, bass.ds(b, 1), :].rearrange("j o n -> j (o n)")
                             ).then_inc(sem(f"unit_in{u}"), 16)
            sp.dma_start(v_slot[u], v_units[bass.ds(b, 1), u, :, :].rearrange("o k n -> (o k) n")
                         ).then_inc(sem(f"unit_in{u}"), 16)

        def x1_load_q(sp, b, u):
            for a_ in range(2):
                at = 4 * HD * u + 2 * HD * a_
                sp.dma_start(q_slot[u][ROWS * a_:ROWS * a_ + ROWS, a_, :, :].rearrange("r g q -> r (g q)"),
                             q_stack[bass.ds(b, 1), :, at:at + 2 * HD, :].rearrange("o c (d g) q -> (o c) d (g q)", g=2)
                             ).then_inc(sem(f"unit_in{u}"), 16)

        def x1_sync(sp):
            for s_ in range(2):
                sp.wait_ge(sem(f"k_out{s_}"), B // 2 * 16 + 1)
                sp.wait_ge(sem(f"v_out{s_}"), B // 2 * 16 + 1)
            sp.wait_ge(sem("mask1_out"), 48)
            for u in range(2):
                sp.wait_ge(sem("k_ones"), u + 1)
                x1_load_kv(sp, 0, u)
            sp.wait_ge(sem("q_ones"), UNITS)
            sp.wait_ge(sem("q_out_first"), 16 * len(Q_RUNS))
            for u in range(UNITS):
                x1_load_q(sp, 0, u)
                if u >= 2:
                    sp.wait_ge(sem("k_ones"), u + 1)
                    x1_load_kv(sp, 0, u)
            sp.wait_ge(sem("q_out"), (B - 1) * 16 * len(Q_RUNS))
            with sp.Fori(1, B) as b:
                for u in range(UNITS):
                    sp.wait_ge(sem("pv_chunk"), (b * UNITS - UNITS + u + 1) * GROUPS + START["pv_chunk"])
                    x1_load_kv(sp, b, u)
                    x1_load_q(sp, b, u)

        def x1_q_store(act):
            for b in range(B):
                if b < 2:
                    act.wait_ge(sem("q1_part"), 3 * b + 3)
                for (j0, j1), (c0, c1) in Q_RUNS:
                    act.dma_start(q_stack[b, c0:c1, :, :].rearrange("c p q -> p c q"),
                                  q_part[:, j0:j1, b * S:(b + 1) * S]
                                  ).then_inc(sem("q_out" if b else "q_out_first"), 16)

        def rows_bank(i_, m):
            return m % 4 if isinstance(m, int) and m < AHEAD - 4 else 4 + i_ % 2

        def rows_chunk(pe, u, i_, m):
            g_, a_, c = i_ // 8, i_ // 4 % 2, i_ % 4
            if isinstance(m, int) and m < AHEAD - 4:
                if m >= 4:
                    pe.wait_ge(sem("max_done"), m - 3)
            elif not (isinstance(m, int) and m < AHEAD - 2):
                pe.wait_ge(sem("max_done"), m - 1)
            pe.matmul(bank(rows_bank(i_, m)), q_slot[u][0:MAX_ROW, a_, g_, :],
                      k_slot[u][0:MAX_ROW, g_, c * BANK:(c + 1) * BANK],
                      start=True, stop=True).then_inc(sem("rows_done"), 1)

        def max_rows_pe(pe, u, n):
            pe.wait_ge(sem("m_cols"), 2 * n + 2)
            out_bf = bank(7).bitcast(BF16)
            for h_ in range(HQ):
                t = pe.transpose(out_bf[MASK_ROW:PAIR_ROWS, 128 * h_:128 * h_ + 128], m_cols[u % 2][:, h_, :],
                                 ident_bf[:, :])
            t.then_inc(sem("m_t"), 1)

        def cols_chunk(pe, u, k2, n, N):
            if k2 == 0:
                pe.wait_ge(sem("m_rows"), n + 1)
            pe.wait_ge(sem("exp1"), N - 1 + START["exp1"])
            for kk in range(2):
                kt = 2 * k2 + kk
                for g_ in range(2):
                    m = pe.matmul(bank((k2 % 2) * 2 + kk, 256, 256 * g_),
                                  k_slot[u][0:PAIR_ROWS, g_, kt * 128:kt * 128 + 128],
                                  q_slot[u][0:PAIR_ROWS, :, g_, :],
                                  start=True, stop=True)
            m.then_inc(sem("cols_done"), 1)

        def values_chunk(pe, u, k2, n, N):
            if k2 == 0:
                pe.wait_ge(sem("pv_copied"), n + START["pv_copied"])
            pe.wait_ge(sem("exp1"), N + 1 + START["exp1"])
            for kk in range(2):
                kt = 2 * k2 + kk
                for h_ in range(HQ):
                    m = pe.matmul(ps[32 * h_:32 * h_ + PV_COLS, 6 * BANK:6 * BANK + 128],
                                  v_slot[u][:, kt * HQ * PV_COLS + h_ * PV_COLS:kt * HQ * PV_COLS + (h_ + 1) * PV_COLS],
                                  p_ring[k2 % 4][:, kk * BANK + 128 * h_:kk * BANK + 128 * h_ + 128],
                                  start=kt == 0, stop=kt == KT - 1)
            m.then_inc(sem("pv_chunk"), 1)

        def out_turn_pe(pe, n):
            pe.wait_ge(sem("pv_copied"), n + 1 + START["pv_copied"])
            pe.wait_ge(sem("o1_norm"), n + START["o1_norm"])
            pe.transpose(bank(7, 128, 256), o_raw, ident).then_inc(sem("o1_t"), 1)

        def x1_pe_batch(pe, b, first, last):
            for g in range(STEPS):
                u, k2 = g // GROUPS, g % GROUPS
                n, N = b * UNITS + u, b * STEPS + g
                cols_chunk(pe, u, k2, n, N)
                if k2 > 0:
                    values_chunk(pe, u, k2 - 1, n, N - 1)
                elif u > 0 or not first:
                    values_chunk(pe, (u - 1) % UNITS, GROUPS - 1, n - 1, N - 1)
                for c in (AHEAD + 2 * g, AHEAD + 2 * g + 1):
                    if last and c >= UNITS * CHUNKS:
                        continue
                    ahead = c // CHUNKS
                    if c % CHUNKS == 0:
                        pe.wait_ge(sem(f"unit_in{ahead % UNITS}"), (b + ahead // UNITS + 1) * (16 * UNIT_DMAS))
                    rows_chunk(pe, ahead % UNITS, c % CHUNKS, b * (UNITS * CHUNKS) + c)
                if k2 == 2 and (u > 0 or not first):
                    pe.wait_ge(sem("m_rows"), n + 1)
                    out_turn_pe(pe, n - 1)
                if k2 == 5 and not (last and u == UNITS - 1):
                    pe.wait_ge(sem("o1_norm"), n + START["o1_norm"])
                    max_rows_pe(pe, (u + 1) % UNITS, n + 1)
            if last:
                values_chunk(pe, UNITS - 1, GROUPS - 1, B * UNITS - 1, B * STEPS - 1)
                pe.wait_ge(sem("m_rows"), B * UNITS)
                out_turn_pe(pe, B * UNITS - 1)

        def x1_pe(pe):
            transpose4_pe(pe, xhN, 0, (sem("ln_xh"), 3 * B + B), sem("ln_t"), by_block=True)
            pe.wait_ge(sem("ln_T"), 4)
            pe.matmul(bank(1), mat("L1x_q"), xhT[:, :], start=True, stop=True).then_inc(sem("q1"), 1)
            pe.wait_ge(sem("x1_zeros"), 1)
            pe.matmul(bank(6, 128), zeros, zeros, start=True, stop=True)
            for c in range(AHEAD):
                if c % CHUNKS == 0:
                    pe.wait_ge(sem(f"unit_in{c // CHUNKS}"), 16 * UNIT_DMAS)
                rows_chunk(pe, c // CHUNKS, c % CHUNKS, c)
                if c == CHUNKS + 4:
                    max_rows_pe(pe, 0, 0)
            pe.wait_ge(sem("max_done"), AHEAD - 4)
            x1_pe_batch(pe, 0, True, False)
            with pe.Fori(1, B - 1) as b:
                x1_pe_batch(pe, b, False, False)
            x1_pe_batch(pe, B - 1, False, True)
            transpose4_pe(pe, b3(o_all), 0, (sem("o1_norm"), B * UNITS + 1), sem("o1_all_t"))
            pe.wait_ge(sem("o1_T"), 1)
            for b in range(B):
                m = pe.matmul(bank(1, 128, 128 * b), o_T[:, 128 * b:128 * b + 128], mat("L1x_o"), start=True, stop=True)
            m.then_inc(sem("y1"), 1)

        def copy_out_act(act, n):
            act.wait_ge(sem("o1_t"), n + START["o1_t"])
            act.wait_ge(sem("pv_chunk"), n * GROUPS + GROUPS + START["pv_chunk"])
            act.activation(o_raw, bank(6, 128), ACT.Copy).then_inc(sem("pv_copied"), 1)

        def x1_act_batch(act, b, first):
            for g in range(STEPS):
                u, k2 = g // GROUPS, g % GROUPS
                N = b * STEPS + g
                act.wait_ge(sem("cols_done"), N + 1)
                act.wait_ge(sem("pv_chunk"), N - 3 + START["pv_chunk"])
                act.activation(p_ring[k2 % 4], ps[:, 2 * BANK * (k2 % 2):2 * BANK * (k2 % 2) + 2 * BANK], ACT.Exp
                               ).then_inc(sem("exp1"), 1)
                if k2 == 0 and (u > 0 or not first):
                    copy_out_act(act, b * UNITS + u - 1)

        def x1_act(act):
            act.wait_ge(sem("ln_t"), 4)
            act.activation(xhT[:, :], bank(0), ACT.Copy).then_inc(sem("ln_T"), 1)
            x1_q_store(act)
            x1_act_batch(act, 0, True)
            with act.Fori(1, B) as b:
                x1_act_batch(act, b, False)
            copy_out_act(act, B * UNITS - 1)
            act.wait_ge(sem("o1_all_t"), 1)
            act.activation(o_T, bank(0), ACT.Copy).then_inc(sem("o1_T"), 1)

        def max_chunk(v, u, i_, m):
            v.wait_ge(sem("rows_done"), m + 1)
            v.tensor_reduce(chunk_max[u % 2][:, i_:i_ + 1], bank(rows_bank(i_, m)), AX.X, ALU.max, negate=True
                            ).then_inc(sem("max_done"), 1)
            if i_ == 15:
                v.wait_ge(sem("max_done"), m + 1)
                v.tensor_reduce(neg_max[u % 2], chunk_max[u % 2].rearrange("p (h c) -> p h c", c=4), AX.X, ALU.min
                                ).then_inc(sem("neg_max"), 1)

        def max_rows_dve(v, u, n):
            v.wait_ge(sem("m_t"), n + 1)
            v.tensor_copy(q_slot[u][MASK_ROW:PAIR_ROWS, :, :, :].rearrange("p a g q -> p g a q"),
                          bank(7).bitcast(BF16)[MASK_ROW:PAIR_ROWS, 0:512]
                          .rearrange("p (g a q) -> p g a q", g=2, a=2)).then_inc(sem("m_rows"), 1)

        def norm_out_dve(v, n):
            t = bank(7, 128, 256).rearrange("p (h c) -> p h c", c=32)
            v.wait_ge(sem("o1_t"), n + 1 + START["o1_t"])
            v.reciprocal(o_rcp, t[:, :, HD]).then_inc(sem("o1_rcp"), 1)
            v.wait_ge(sem("o1_rcp"), n + 1)
            v.tensor_tensor(o_all[:, bass.ds(n * 32, 32)].rearrange("p (h d) -> p h d", d=HD),
                            t[:, :, 0:HD], bc_in(o_rcp, HD), ALU.mult).then_inc(sem("o1_norm"), 1)

        def x1_dve_batch(v, b, first, last):
            for g in range(STEPS):
                u, k2 = g // GROUPS, g % GROUPS
                n = b * UNITS + u
                for c in (AHEAD + 2 * g, AHEAD + 2 * g + 1):
                    if not (last and c >= UNITS * CHUNKS):
                        max_chunk(v, c // CHUNKS % UNITS, c % CHUNKS, b * (UNITS * CHUNKS) + c)
                if k2 == 4 and (u > 0 or not first):
                    norm_out_dve(v, n - 1)
                if k2 == 6 and not (last and u == UNITS - 1):
                    max_rows_dve(v, (u + 1) % UNITS, n + 1)
            if last:
                norm_out_dve(v, B * UNITS - 1)

        def x1_dve(v):
            ln_dve(v, 3, (sem("x2_new"), 1))
            v.wait_ge(sem("q1"), 1)
            for k, at in enumerate((slice(0, S), slice(S, B * S))):
                v.tensor_scalar(q_f[:, at], bank(1)[:, at], col("L1x_bq"), 1.0 / math.sqrt(HD), ALU.add, ALU.mult
                                ).then_inc(sem("q1_f"), 1)
                for j in range(3):
                    v.wait_ge(sem("q1_f"), 3 * k + j + 1)
                    v.tensor_copy(q_part[:, j, at], q_f[:, at]).then_inc(sem("q1_part"), 1)
                    if j < 2:
                        v.wait_ge(sem("q1_part"), 3 * k + j + 1)
                        v.tensor_tensor(q_f[:, at], q_f[:, at], q_part[:, j, at], ALU.subtract).then_inc(sem("q1_f"), 1)
            v.memset(zeros, 0.0).then_inc(sem("x1_zeros"), 1)
            v.wait_ge(sem("in_consts"), 16)
            v.tensor_copy(ident_bf[:, :], ident).then_inc(sem("ident_bf"), 1)
            v.tensor_tensor(xN[:, :, :], xN[:, :, :], bc_mid(row("L1x_bo"), B), ALU.add).then_inc(sem("x1_bo"), 1)
            for c in range(AHEAD):
                max_chunk(v, c // CHUNKS, c % CHUNKS, c)
                if c == CHUNKS + 6:
                    max_rows_dve(v, 0, 0)
            x1_dve_batch(v, 0, True, False)
            with v.Fori(1, B - 1) as b:
                x1_dve_batch(v, b, False, False)
            x1_dve_batch(v, B - 1, False, True)
            v.wait_ge(sem("y1"), 1)
            v.tensor_tensor(xN_flat, bank(1), xN_flat, ALU.add).then_inc(sem("x3_new"), 1)

        def x1_pool(g):
            g.wait_ge(sem("x2_new"), 1)
            for i_ in range(2):
                g.memset(tC[:, 96 + 32 * i_:114 + 32 * i_], 0.0).then_inc(sem("m_zero"), 1)
            g.memset(tC[:, 184:194], 0.0).then_inc(sem("m_zero"), 1)
            g.wait_ge(sem("m_zero"), 3)
            for i_ in range(2):
                g.memset(m_cols[i_][:, :, 0:3], 1.0).then_inc(sem("m_zero"), 1)
            g.wait_ge(sem("m_zero"), 5)
            with g.Fori(0, B * UNITS // 2) as it:
                for i_ in range(2):
                    n = it * 2 + i_
                    g.wait_ge(sem("neg_max"), n + 1)
                    g.tensor_tensor(m_part[i_][:, 0, :], neg_max[i_], m_none, ALU.add).then_inc(sem("m_split"), 1)
                    g.wait_ge(sem("m_split"), n * 4 + 1)
                    g.tensor_tensor(m_rest[i_], neg_max[i_], m_part[i_][:, 0, :], ALU.subtract
                                    ).then_inc(sem("m_split"), 1)
                    g.wait_ge(sem("m_split"), n * 4 + 2)
                    g.tensor_tensor(m_part[i_][:, 1, :], m_rest[i_], m_none, ALU.add).then_inc(sem("m_split"), 1)
                    g.wait_ge(sem("m_split"), n * 4 + 3)
                    g.tensor_tensor(m_part[i_][:, 2, :], m_rest[i_], m_part[i_][:, 1, :], ALU.subtract
                                    ).then_inc(sem("m_split"), 1)
                    g.wait_ge(sem("m_split"), n * 4 + 4)
                    for a_ in range(2):
                        g.tensor_tensor(m_cols[i_][:, a_:a_ + 3:2, 3 + 3 * a_:6 + 3 * a_],
                                        m_part[i_][:, :, a_:a_ + 3:2].rearrange("p j g -> p g j"),
                                        m_none3, ALU.add).then_inc(sem("m_cols"), 1)

        (q2T, eq2T, k2T, ek2T, v2T, k_bd, ek_bd, s_sum, p2, p2T, e_dec, mix9, q_b2, eq_b2, m_b2, raw2, amp_w, o2_all,
         o2_T, ek_b2) = carve([
             512, 512, 512, 512, 512, 2048, 2048, 2048, 2048, 1024, 1024, B * H * 9, 128, 128, H * 9, 512, 1024, 512,
             512, 128])
        z_all = amp_w[:, 0:128].rearrange("p (b c) -> p b c", c=32)
        e_amp, th, p_abs, s_arg, sin_p, cos_p, c_sin, c_cos = (
            amp_w[:, 128 + 64 * i_:192 + 64 * i_].rearrange("p (b h) -> p b h", h=H) for i_ in range(8))
        mix_v = mix9.rearrange("p (b h e) -> p b h e", b=B, h=H)
        o2_rcp = amp_w[:, 640:656]
        neg_max2 = amp_w[:, 656:672]
        o2_zero = tF[:, 0:512]
        SQ_HD = 1.0 / math.sqrt(HD)
        START.update({"c_scores": 1, "c_sum": 2, "c_exp": 4, "c_pt": 4, "c_ptc": 2, "c_pv": 2, "c_raw": 1, "c_ot": 1,
                      "c_norm": 1})

        def by_head(ap):
            return ap.rearrange("p (g d) -> p g d", d=HD)

        def l1a_pe(pe):
            transpose4_pe(pe, xhN, 0, (sem("ln_xh"), 4 * B + B), sem("ln_t"), by_block=True)
            pe.wait_ge(sem("ln_T"), 5)
            for bk, n_ in ((1, "L1a_vT"), (4, "L1a_kT"), (2, "L1a_qT"), (5, "L1a_ekT"), (3, "L1a_eqT")):
                pe.matmul(bank(bk), mat(n_), xhT[:, :], start=True, stop=True).then_inc(sem_of("b_proj"), 1)
            for b in range(B):
                m = pe.matmul(bank(7, 32, 32 * b), xhT[:, b * S:(b + 1) * S], mat("amp_ph")[:, 0:32],
                              start=True, stop=True)
            m.then_inc(sem_of("b_amp"), 1)
            for b in range(B):
                m = pe.matmul(bank(6, 128, 128 * b), xhT[:, b * S:(b + 1) * S], mat("L1a_vT"), start=True, stop=True)
            m.then_inc(sem_of("b_vn"), 1)

            def scores(b, j):
                n = b * 4 + j
                if j == 0:
                    pe.wait_ge(sem("c_qb"), b * 2 + 2)
                pe.wait_ge(sem("c_ekbd"), n + 1)
                pe.wait_ge(sem("c_kbd"), n + 1)
                pe.wait_ge(sem("c_sum"), n - 1 + START["c_sum"])
                pe.matmul(bank(j % 2), eq_b2, ek_bd[:, j * BANK:(j + 1) * BANK], start=True, stop=True)
                pe.matmul(bank(2 + j % 2), q_b2, k_bd[:, j * BANK:(j + 1) * BANK], start=True, stop=True
                          ).then_inc(sem("c_scores"), 1)

            def turn(b, j):
                n = b * 4 + j
                pe.wait_ge(sem("c_exp"), n + 1 + START["c_exp"])
                pe.wait_ge(sem("c_ptc"), n - 1 + START["c_ptc"])
                for h_ in range(4):
                    t = pe.transpose(bank(4 + j % 2, 128, 128 * h_),
                                     p2[:, j * BANK + 128 * h_:j * BANK + 128 * h_ + 128], ident)
                t.then_inc(sem("c_pt"), 1)

            def values(b, j):
                n = b * 4 + j
                if j == 0:
                    pe.wait_ge(sem("c_mb"), b + 1)
                    pe.wait_ge(sem("c_raw"), b + START["c_raw"])
                pe.wait_ge(sem("c_ptc"), n + 1 + START["c_ptc"])
                for h_ in range(4):
                    m = pe.matmul(ps[32 * h_:32 * h_ + 9, 6 * BANK + 128 * j:6 * BANK + 128 * j + 128],
                                  m_b2[:, (4 * j + h_) * 9:(4 * j + h_) * 9 + 9],
                                  p2T[:, (j % 2) * BANK + 128 * h_:(j % 2) * BANK + 128 * h_ + 128],
                                  start=True, stop=True)
                m.then_inc(sem("c_pv"), 1)

            def turn_out(b):
                pe.wait_ge(sem("c_raw"), b + 1 + START["c_raw"])
                pe.wait_ge(sem("c_norm"), b + START["c_norm"])
                for j in range(4):
                    t = pe.transpose(bank(7, 128, 128 * j), raw2[:, 128 * j:128 * j + 128], ident)
                t.then_inc(sem("c_ot"), 1)

            def batch(b, first, last):
                for j in range(4):
                    turn(b, j)
                    if j == 2 and not first:
                        turn_out(b - 1)
                    if j < 2:
                        scores(b, j + 2)
                    elif not last:
                        scores(b + 1, j - 2)
                    if j > 0:
                        values(b, j - 1)
                    elif not first:
                        values(b - 1, 3)

            pe.wait_ge(*step("b_q", 2))
            scores(0, 0)
            scores(0, 1)
            pe.wait_ge(*step("b_vT", 1))
            pe.wait_ge(*step("b_k", 2))
            for i_, n_ in enumerate(("mix", "mix_rolled")):
                for b in range(B):
                    m = pe.matmul(bank(4 + i_, 128, 128 * b), v2T[:, b * S:(b + 1) * S], mat(n_),
                                  start=True, stop=True)
                m.then_inc(sem_of("b_sup"), 1)
            pe.wait_ge(*step("b_vb", 1))
            pe.wait_ge(*step("b_zero", 1))
            pe.matmul(bank(6), o2_zero[:, 0:128], o2_zero, start=True, stop=True)
            pe.wait_ge(*step("b_s2", 1))
            batch(0, True, False)
            with pe.Fori(1, B - 1) as b:
                batch(b, False, False)
            batch(B - 1, False, True)
            values(B - 1, 3)
            turn_out(B - 1)
            transpose4_pe(pe, b3(o2_all), 0, (sem("c_norm"), B + 1), sem_of("c_all_t"))
            pe.wait_ge(*step("c_oT", 1))
            for b in range(B):
                m = pe.matmul(bank(1, 128, 128 * b), o2_T[:, 128 * b:128 * b + 128], mat("L1a_oT"),
                              start=True, stop=True)
            m.then_inc(sem_of("c_out"), 1)

        def l1a_act(act):
            act.wait_ge(sem("ln_t"), 5)
            act.activation(xhT[:, :], bank(0), ACT.Copy).then_inc(sem("ln_T"), 1)
            act.wait_ge(*step("b_proj", 1))
            act.activation(v2T, bank(1), ACT.Identity, bias=col("L1a_bv")).then_inc(sem_of("b_vT"), 1)
            act.wait_ge(*step("b_proj", 2))
            act.activation(k2T, bank(4), ACT.Identity, bias=col("L1a_bk")).then_inc(sem_of("b_k"), 1)
            act.wait_ge(*step("b_proj", 4))
            act.activation(ek2T, bank(5), ACT.Identity, bias=col("L1a_bek")).then_inc(sem_of("b_k"), 1)
            def mixed_values(b):
                if isinstance(b, int) and b == 0:
                    act.wait_ge(*step("b_mixed", 1))
                act.wait_ge(sem("c_pv"), b * 4 + START["c_pv"])
                act.activation(m_b2, mix9[:, bass.ds(b * H * 9, H * 9)], ACT.Copy).then_inc(sem("c_mb"), 1)

            def exps(b, j):
                n = b * 4 + j
                act.wait_ge(sem("c_max"), n + 1)
                act.wait_ge(sem("c_pt"), n - 3 + START["c_pt"])
                for h_ in range(4):
                    at = slice(j * BANK + 128 * h_, j * BANK + 128 * h_ + 128)
                    e = act.activation(p2[:, at], s_sum[:, at], ACT.Exp, bias=neg_max2[:, 4 * j + h_:4 * j + h_ + 1])
                e.then_inc(sem("c_exp"), 1)

            def turned(b, j):
                n = b * 4 + j
                act.wait_ge(sem("c_pt"), n + 1 + START["c_pt"])
                act.wait_ge(sem("c_pv"), n - 1 + START["c_pv"])
                act.activation(p2T[:, (j % 2) * BANK:(j % 2) * BANK + BANK], bank(4 + j % 2), ACT.Copy
                               ).then_inc(sem("c_ptc"), 1)

            def raw_out(b):
                act.wait_ge(sem("c_pv"), b * 4 + 4 + START["c_pv"])
                act.wait_ge(sem("c_ot"), b + START["c_ot"])
                act.activation(raw2, bank(6), ACT.Copy).then_inc(sem("c_raw"), 1)

            def batch(b, first, last):
                for j in range(4):
                    exps(b, j)
                    if j == 1:
                        if not first:
                            raw_out(b - 1)
                        mixed_values(b)
                    if j > 0:
                        turned(b, j - 1)
                    elif not first:
                        turned(b - 1, 3)

            act.wait_ge(*step("b_z", 2))
            act.activation(e_amp, e_amp, ACT.Exp, scale=-1.0).then_inc(sem_of("b_eamp"), 1)
            act.activation(th, z_all[:, :, H:2 * H], ACT.Tanh).then_inc(sem_of("b_tanh"), 1)
            act.wait_ge(*step("b_tanh", 1))
            act.activation(p_abs, th, ACT.Abs, scale=math.pi).then_inc(sem_of("b_abs"), 1)
            act.wait_ge(*step("b_arg", 1))
            act.activation(sin_p, th, ACT.Sin, scale=math.pi).then_inc(sem_of("b_sin"), 1)
            act.activation(cos_p, s_arg, ACT.Sin).then_inc(sem_of("b_sin"), 1)
            batch(0, True, False)
            with act.Fori(1, B - 1) as b:
                batch(b, False, False)
            batch(B - 1, False, True)
            turned(B - 1, 3)
            raw_out(B - 1)
            act.wait_ge(*step("c_all_t", 1))
            act.activation(o2_T, bank(0), ACT.Copy).then_inc(sem_of("c_oT"), 1)

        def l1a_dve(v):
            ln_dve(v, 4, (sem("x3_new"), 1))
            def keys(b, j):
                if not isinstance(b, int) or b > 0:
                    v.wait_ge(sem("c_scores"), (b - 1) * 4 + j + 1 + START["c_scores"])
                v.tensor_tensor(b3(k_bd[:, j * BANK:(j + 1) * BANK]), bc_mid(k2T[:, bass.ds(b * 128, 128)], 4),
                                bc_in(const("head_mask")[:, 4 * j:4 * j + 4], 128), ALU.mult
                                ).then_inc(sem("c_kbd"), 1)

            def logits(b, j):
                n = b * 4 + j
                ss = s_sum[:, j * BANK:(j + 1) * BANK]
                dec = e_dec[:, (j % 2) * BANK:(j % 2) * BANK + BANK]
                v.wait_ge(sem("c_scores"), n + 1 + START["c_scores"])
                v.tensor_tensor(b3(dec), b3(bank(j % 2)), bc_mid(const("decay"), 4), ALU.mult
                                ).then_inc(sem("c_dec"), 1)
                v.wait_ge(sem("c_dec"), n + 1)
                v.wait_ge(sem("c_exp"), n - 3 + START["c_exp"])
                v.tensor_tensor(ss, bank(2 + j % 2), dec, ALU.add).then_inc(sem("c_sum"), 1)
                v.wait_ge(sem("c_sum"), n + 1 + START["c_sum"])
                v.tensor_reduce(neg_max2[:, 4 * j:4 * j + 4], b3(ss), AX.X, ALU.max, negate=True
                                ).then_inc(sem("c_max"), 1)

            v.memset(o2_zero, 0.0).then_inc(sem_of("b_zero"), 1)
            v.wait_ge(*step("b_proj", 3))
            v.tensor_scalar(q2T, bank(2), col("L1a_bq"), SQ_HD, ALU.add, ALU.mult).then_inc(sem_of("b_q"), 1)
            v.wait_ge(*step("b_proj", 5))
            v.tensor_scalar(eq2T, bank(3), col("L1a_beq"), SQ_HD, ALU.add, ALU.mult).then_inc(sem_of("b_q"), 1)
            v.wait_ge(*step("b_k", 2))
            keys(0, 0)
            keys(0, 1)
            v.wait_ge(*step("b_amp", 1))
            v.tensor_tensor(z_all, bank(7, 128).rearrange("p (b c) -> p b c", c=32),
                            bc_mid(row("amp_ph_b")[:, 0:32], B), ALU.add).then_inc(sem_of("b_z"), 1)
            v.wait_ge(*step("b_z", 1))
            v.tensor_scalar(e_amp, z_all[:, :, 0:H], -87.0, None, ALU.max).then_inc(sem_of("b_z"), 1)
            keys(0, 2)
            keys(0, 3)
            logits(0, 0)
            v.wait_ge(*step("b_abs", 1))
            v.tensor_scalar(s_arg, p_abs, -1.0, math.pi / 2, ALU.mult, ALU.add).then_inc(sem_of("b_arg"), 1)
            v.wait_ge(*step("b_eamp", 1))
            v.tensor_scalar(e_amp, e_amp, 1.0, None, ALU.add).then_inc(sem_of("b_amp1"), 1)
            v.wait_ge(*step("b_amp1", 1))
            v.reciprocal(e_amp, e_amp).then_inc(sem_of("b_amp1"), 1)
            v.wait_ge(*step("b_amp1", 2))
            v.tensor_scalar(e_amp, e_amp, 0.3, None, ALU.mult).then_inc(sem_of("b_amp1"), 1)
            v.wait_ge(*step("b_vn", 1))
            v.tensor_tensor(b3(tE[:, 0:512]), b3(bank(6)), bc_mid(row("L1a_bv"), B), ALU.add
                            ).then_inc(sem_of("b_vb"), 1)
            v.wait_ge(*step("b_sup", 2))
            v.tensor_tensor(b3(tC[:, 0:512]), b3(bank(4)), bc_mid(row("mix_b"), B), ALU.add).then_inc(sem_of("b_s1"), 1)
            v.tensor_tensor(b3(tD[:, 0:512]), b3(bank(5)), bc_mid(row("mix_b_rolled"), B), ALU.add
                            ).then_inc(sem_of("b_s2"), 1)
            v.wait_ge(*step("b_amp1", 3))
            v.wait_ge(*step("b_sin", 2))
            v.tensor_tensor(c_cos, e_amp, cos_p, ALU.mult).then_inc(sem_of("b_coef"), 1)
            v.tensor_tensor(c_sin, e_amp, sin_p, ALU.mult).then_inc(sem_of("b_coef"), 1)
            v.wait_ge(*step("b_s2", 1))
            v.wait_ge(*step("b_coef", 2))

            logits(0, 1)

            v.tensor_tensor(by_head(tC[:, 0:512]), by_head(tC[:, 0:512]),
                            bc_in(c_cos.rearrange("p b h -> p (b h)"), HD), ALU.mult).then_inc(sem_of("b_t1"), 1)
            v.wait_ge(*step("b_t1", 1))
            v.tensor_tensor(tE[:, 0:512], tE[:, 0:512], tC[:, 0:512], ALU.add).then_inc(sem_of("b_t3"), 1)
            v.wait_ge(*step("b_t2", 1))
            v.wait_ge(*step("b_t3", 1))
            v.wait_ge(sem("b_mix_one"), 1)
            v.tensor_tensor(mix9.rearrange("p (g e) -> p g e", e=9)[:, :, 0:HD], by_head(tE[:, 0:512]),
                            by_head(tD[:, 0:512]), ALU.add).then_inc(sem_of("b_mixed"), 1)
            def normed_out(b):
                v.wait_ge(sem("c_ot"), b + 1 + START["c_ot"])
                t = bank(7).rearrange("p (h c) -> p h c", c=32)
                v.reciprocal(o2_rcp, t[:, :, HD]).then_inc(sem("c_rcp"), 1)
                v.wait_ge(sem("c_rcp"), b + 1)
                v.tensor_tensor(o2_all[:, bass.ds(b * 128, 128)].rearrange("p (h d) -> p h d", d=HD), t[:, :, 0:HD],
                                bc_in(o2_rcp, HD), ALU.mult).then_inc(sem("c_norm"), 1)

            def batch(b, first, last):
                for j in range(4):
                    if not (first and j < 2):
                        logits(b, j)
                    if first and j == 2:
                        keys(1, 0)
                        keys(1, 1)
                    if not (last or first and j < 2):
                        keys(b + 1, j)
                    if j == 3 and not first:
                        normed_out(b - 1)

            batch(0, True, False)
            with v.Fori(1, B - 1) as b:
                batch(b, False, False)
            batch(B - 1, False, True)
            normed_out(B - 1)
            v.tensor_tensor(xhN[:, :, :], xhN[:, :, :], bc_mid(row("L1a_bo"), B), ALU.add).then_inc(sem_of("c_bo"), 1)
            v.wait_ge(*step("c_bo", 1))
            v.wait_ge(*step("c_out", 1))
            v.tensor_tensor(tA[:, 0:512], bank(1), xhN[:, :, :].rearrange("p b d -> p (b d)"), ALU.add
                            ).then_inc(sem_of("c_res"), 1)

            def shift():
                v.tensor_tensor(xN[:, :, :], xN[:, :, :], bc_mid(row("L1a_ln_b"), B), ALU.add
                                ).then_inc(sem_of("c_shiftb"), 1)

            ln_dve(v, 5, step("c_res", 1), src=b3(tA[:, 0:512]), dst=b3(tB[:, 0:512]), meanwhile=shift)
            v.wait_ge(sem("ln_xh"), 5 * B + B)
            v.tensor_tensor(b3(tB[:, 0:512]), b3(tB[:, 0:512]), bc_mid(row("L1a_ln_g"), B), ALU.mult
                            ).then_inc(sem_of("c_gain"), 1)
            v.wait_ge(*step("c_gain", 1))
            v.wait_ge(*step("c_shiftb", 1))
            v.tensor_tensor(xN_flat, xN_flat, tB[:, 0:512], ALU.add).then_inc(sem("x4_new"), 1)

        def l1a_pool(g):
            ln_pool(g, 4)
            g.memset(mix_v[:, :, :, HD], 1.0).then_inc(sem("b_mix_one"), 1)
            g.wait_ge(*step("b_k", 2))

            def batch_keys(b):
                if not isinstance(b, int):
                    g.wait_ge(sem("c_ekbd"), b * 4)
                g.tensor_copy(ek_b2, ek2T[:, bass.ds(b * 128, 128)]).then_inc(sem("c_ekb"), 1)

            def keys(b, j):
                g.wait_ge(sem("c_ekb"), b + 1)
                if not isinstance(b, int):
                    g.wait_ge(sem("c_scores"), (b - 1) * 4 + j + 1 + START["c_scores"])
                g.tensor_tensor(b3(ek_bd[:, j * BANK:(j + 1) * BANK]), bc_mid(ek_b2, 4),
                                bc_in(const("head_mask")[:, 4 * j:4 * j + 4], 128), ALU.mult
                                ).then_inc(sem("c_ekbd"), 1)

            def queries(b):
                if not isinstance(b, int):
                    g.wait_ge(sem("c_scores"), b * 4 + START["c_scores"])
                g.tensor_copy(eq_b2, eq2T[:, bass.ds(b * 128, 128)]).then_inc(sem("c_qb"), 1)
                g.tensor_copy(q_b2, q2T[:, bass.ds(b * 128, 128)]).then_inc(sem("c_qb"), 1)

            batch_keys(0)
            keys(0, 0)
            g.wait_ge(*step("b_q", 2))
            queries(0)
            for j in range(1, 4):
                keys(0, j)
            g.wait_ge(*step("b_s2", 1))
            g.wait_ge(*step("b_coef", 2))
            g.tensor_tensor(by_head(tD[:, 0:512]), by_head(tD[:, 0:512]),
                            bc_in(c_sin.rearrange("p b h -> p (b h)"), HD), ALU.mult).then_inc(sem_of("b_t2"), 1)
            with g.Fori(1, B) as b:
                batch_keys(b)
                for j in range(3):
                    keys(b, j)
                queries(b)
                keys(b, 3)
            ln_pool(g, 5)

        W_AT = Q_AT + UNITS * Q_WORDS
        w_slot = [arena[:, W_AT + 2 * FF * i_:W_AT + 2 * FF * (i_ + 1)] for i_ in range(2)]
        (xn2N, xn2T, xe0, xe1, h0, h1, gate_T) = carve([512, 512, 512, 512, 2048, 2048, 512])
        x_e, h_e = [xe0, xe1], [h0, h1]
        aff = small[:, 104:136].rearrange("p (b e) -> p b e", e=NE)
        score = small[:, 136:168].rearrange("p (b e) -> p b e", e=NE)
        GATE_AT = 168
        gate = small[:, GATE_AT:GATE_AT + B * NE].rearrange("p (b e) -> p b e", e=NE)
        top, s_top, alpha = small[:, 200:204], small[:, 204:208], small[:, 208:212]
        START.update({"e_relu": 4, "e_y": 2, "e_acc": 1, "e_h": 5, "e_x": 1})

        def l1f_load(sp, e, s):
            sp.wait_ge(sem("e_h"), (e - 1) * FT + START["e_h"])
            sp.dma_start(w_slot[s][:, 0:512], w1[bass.ds(e, 1), :, :].rearrange("o d f -> (o d) f")
                         ).then_inc(sem(f"in_w1_{s}"), 16)
            sp.wait_ge(sem("e_y"), e - 1 + START["e_y"])
            sp.dma_start(w_slot[s][:, 512:1024].rearrange("p (t d) -> p t d", d=D),
                         w2[bass.ds(e, 1), :, :].rearrange("o (t p) d -> p (o t) d", p=128)
                         ).then_inc(sem(f"in_w2_{s}"), 16)

        def l1f_sync(sp):
            with sp.Fori(0, NE // 2) as it:
                for s in range(2):
                    l1f_load(sp, it * 2 + s, s)

        def hidden_pe(pe, e, s, loads):
            pe.wait_ge(sem(f"in_w1_{s}"), 16 * loads)
            pe.wait_ge(sem("e_x"), e + 1 + START["e_x"])
            for t in range(FT):
                pe.wait_ge(sem("e_relu"), e * FT + t - 3 + START["e_relu"])
                pe.matmul(bank(t), w_slot[s][:, 128 * t:128 * t + 128], x_e[s], start=True, stop=True
                          ).then_inc(sem("e_h"), 1)

        def output_pe(pe, e, s, loads):
            pe.wait_ge(sem(f"in_w2_{s}"), 16 * loads)
            pe.wait_ge(sem("e_relu"), e * FT + FT + START["e_relu"])
            pe.wait_ge(sem("e_acc"), e * B + START["e_acc"])
            for b in range(B):
                for t in range(FT):
                    m = pe.matmul(bank(4 + s, 128, 128 * b), h_e[s][:, BANK * t + 128 * b:BANK * t + 128 * b + 128],
                                  w_slot[s][:, 512 + 128 * t:640 + 128 * t], start=t == 0, stop=t == FT - 1)
            m.then_inc(sem("e_y"), 1)

        def l1f_pe(pe):
            transpose4_pe(pe, xhN, 0, (sem("ln_xh"), 6 * B + B), sem("ln_t"), by_block=True)
            pe.wait_ge(sem("ln_T"), 6)
            pe.wait_ge(sem("in_experts"), 48)
            for b in range(B):
                m = pe.matmul(bank(1, NE, NE * b), xhT[:, b * S:(b + 1) * S], CT[:, :], start=True, stop=True)
            m.then_inc(sem_of("d_aff"), 1)
            transpose4_pe(pe, b3(xn2N), 2, (sem("ln_xh"), 7 * B + B), sem("ln_t"), by_block=True)
            hidden_pe(pe, 0, 0, 1)
            pe.wait_ge(*step("d_gate", 1))
            for b in range(B):
                t = pe.transpose(ps[0:NE, 6 * BANK + 128 * b:6 * BANK + 128 * b + 128], gate[:, b, :], ident)
            t.then_inc(sem_of("d_gate_t"), 1)
            pe.wait_ge(*step("d_gate_T", 1))
            for b in range(B):
                m = pe.matmul(bank(7, 128, 128 * b), gate_T[0:NE, 128 * b:128 * b + 128], B2[:, :],
                              start=True, stop=True)
            m.then_inc(sem_of("d_b2"), 1)
            with pe.Fori(0, NE // 2 - 1) as it:
                e = it * 2
                hidden_pe(pe, e + 1, 1, it + 1)
                output_pe(pe, e, 0, it + 1)
                hidden_pe(pe, e + 2, 0, it + 2)
                output_pe(pe, e + 1, 1, it + 1)
            hidden_pe(pe, NE - 1, 1, NE // 2)
            output_pe(pe, NE - 2, 0, NE // 2)
            output_pe(pe, NE - 1, 1, NE // 2)

        def l1f_act(act):
            act.wait_ge(sem("ln_t"), 6)
            act.activation(xhT[:, :], bank(0), ACT.Copy).then_inc(sem("ln_T"), 1)
            act.wait_ge(sem("ln_t"), 7)
            act.activation(xn2T, bank(2), ACT.Copy).then_inc(sem("ln_T"), 1)
            act.wait_ge(*step("d_clamp", 1))
            act.activation(alpha, alpha, ACT.Exp, scale=-1.0).then_inc(sem_of("d_exp"), 1)
            with act.Fori(0, NE // 2) as it:
                for s in range(2):
                    e = it * 2 + s
                    act.wait_ge(sem("e_y"), e - 1 + START["e_y"])
                    for t in range(FT):
                        act.wait_ge(sem("e_h"), e * FT + t + 1 + START["e_h"])
                        act.activation(h_e[s][:, BANK * t:BANK * t + BANK], bank(t), ACT.Relu,
                                       bias=EC[:, bass.ds(2 * NE + e * FT + t, 1)]).then_inc(sem("e_relu"), 1)

        def l1f_dve(v):
            ln_dve(v, 6, (sem("x4_new"), 1))

            def residual():
                v.tensor_tensor(xN[:, :, :], xN[:, :, :], xhN[:, :, :], ALU.add).then_inc(sem_of("d_res"), 1)

            ln_dve(v, 7, (sem("ln_xh"), 6 * B + B), src=xhN[:, :, :], dst=b3(xn2N), meanwhile=residual)
            v.wait_ge(*step("d_aff", 1))
            v.tensor_copy(aff, bank(1, NE * B).rearrange("p (b e) -> p b e", e=NE)).then_inc(sem_of("d_top"), 1)
            v.wait_ge(*step("d_top", 1))
            v.tensor_reduce(top, aff, AX.X, ALU.max).then_inc(sem_of("d_top"), 1)
            v.wait_ge(*step("d_top", 2))
            v.tensor_scalar(alpha, top, -87.0, None, ALU.max).then_inc(sem_of("d_clamp"), 1)
            v.tensor_tensor(score, aff, bc_in(top, NE), ALU.is_equal).then_inc(sem_of("d_sel"), 1)
            v.wait_ge(*step("d_sel", 1))
            v.tensor_tensor(score, score, bc_mid(const("first_weight")[:, 0:NE], B), ALU.mult
                            ).then_inc(sem_of("d_sel"), 1)
            v.wait_ge(*step("d_sel", 2))
            v.tensor_reduce(s_top, score, AX.X, ALU.max).then_inc(sem_of("d_sel"), 1)
            v.wait_ge(*step("d_sel", 3))
            v.tensor_tensor(gate, score, bc_in(s_top, NE), ALU.is_equal).then_inc(sem_of("d_sel"), 1)
            v.wait_ge(*step("d_exp", 1))
            v.tensor_scalar(alpha, alpha, 1.0, None, ALU.add).then_inc(sem_of("d_al"), 1)
            v.wait_ge(*step("d_al", 1))
            v.reciprocal(alpha, alpha).then_inc(sem_of("d_al"), 1)
            v.wait_ge(*step("d_al", 2))
            v.wait_ge(*step("d_sel", 4))
            v.tensor_tensor(gate, gate, bc_in(alpha, NE), ALU.mult).then_inc(sem_of("d_gate"), 1)

            def expert_in(e, s):
                v.wait_ge(sem("e_h"), (e - 1) * FT + START["e_h"])
                v.tensor_scalar(x_e[s], xn2T, EC[:, bass.ds(e, 1)], EC[:, bass.ds(NE + e, 1)], ALU.mult, ALU.add
                                ).then_inc(sem("e_x"), 1)

            def expert_out(e, s):
                v.wait_ge(sem("e_y"), e + 1 + START["e_y"])
                for b in range(B):
                    v.wait_ge(sem("e_acc"), e * B + b + 1 + START["e_acc"])
                    v.scalar_tensor_tensor(out=xN[:, b, :], in0=bank(4 + s, 128, 128 * b),
                                           scalar=small[:, bass.ds(GATE_AT + b * NE + e, 1)], in1=xN[:, b, :],
                                           op0=ALU.mult, op1=ALU.add).then_inc(sem("e_acc"), 1)

            v.wait_ge(sem("ln_T"), 7)
            for s in range(2):
                expert_in(s, s)
            v.wait_ge(*step("d_gate_t", 1))
            v.tensor_copy(gate_T[0:NE, :], ps[0:NE, 6 * BANK:7 * BANK]).then_inc(sem_of("d_gate_T"), 1)
            v.wait_ge(*step("d_b2", 1))
            v.wait_ge(*step("d_res", 1))
            v.tensor_tensor(xN_flat, xN_flat, bank(7), ALU.add).then_inc(sem("e_acc"), B)
            with v.Fori(0, NE // 2 - 1) as it:
                for s in range(2):
                    expert_in(it * 2 + 2 + s, s)
                    expert_out(it * 2 + s, s)
            for s in range(2):
                expert_out(NE - 2 + s, s)

        def l1f_pool(g):
            ln_pool(g, 6)
            ln_pool(g, 7)

        block = stack.enter_context(nc.Block())

        @block.sync
        def _(sp):
            l0x_sync(sp)
            x1_sync(sp)
            l1f_sync(sp)
            sp.wait_ge(sem("e_acc"), (NE + 1) * B + START["e_acc"])
            sp.wait_ge(sem("in_experts"), 48)
            sp.dma_start(out.rearrange("b s d -> s b d"), xN[:, :, :]).then_inc(sem("out"), 16)
            sp.wait_ge(sem("out"), 16)

        @block.tensor
        def _(pe):
            l0x_pe(pe)
            l0a_pe(pe)
            l0f_pe(pe)
            x1_pe(pe)
            l1a_pe(pe)
            l1f_pe(pe)

        @block.scalar
        def _(act):
            l0x_act(act)
            l0a_act(act)
            l0f_act(act)
            x1_act(act)
            l1a_act(act)
            l1f_act(act)

        @block.vector
        def _(v):
            l0x_dve(v)
            l0a_dve(v)
            l0f_dve(v)
            x1_dve(v)
            l1a_dve(v)
            l1f_dve(v)

        @block.gpsimd
        def _(g):
            l0x_pool(g)
            l0f_pool(g)
            ln_pool(g, 1)
            x1_init_pool(g, (0, 1))
            ln_pool(g, 2)
            x1_init_pool(g, (2, 3))
            ln_pool(g, 3)
            x1_pool(g)
            l1a_pool(g)
            l1f_pool(g)


def kernel(**inputs):
    import numpy as np
    import concourse.bacc as bacc
    from concourse.bass_utils import run_bass_kernel_spmd

    a = {n: np.asarray(v) for n, v in inputs.items()}

    def stacked(parts, axis):
        return np.ascontiguousarray(np.stack(parts, axis=axis))

    mix = np.zeros((H, HD, H, HD), np.float32)
    for h in range(H):
        mix[h, :, h, :] = a["L1_attn_mix_w"][h].T
    order = [(HQ * u + 2 * g + h) * HD + d for u in range(UNITS) for h in range(2) for d in range(HD) for g in range(2)]
    mats = {
        "L0x_q": a["L0_xattn_kernel_q"], "L0x_kT": a["L0_xattn_kernel_k"].T, "L0x_v": a["L0_xattn_kernel_v"],
        "L0a_q": a["L0_attn_w_q"], "L0a_k": a["L0_attn_w_k"], "L0a_v": a["L0_attn_w_v"], "L0a_o": a["L0_attn_w_o"],
        "L0f_rT": a["L0_ffn_W_r"].T, "L0f_kT": a["L0_ffn_W_k"].T, "L0f_vT": a["L0_ffn_W_v"].T,
        "L1x_q": a["L1_xattn_Wq"][:, order], "L1x_k": a["L1_xattn_Wk"][:, order],
        "L1x_v": a["L1_xattn_Wv"], "L1x_o": a["L1_xattn_Wo"],
        "L1a_qT": a["L1_attn_Wq"].T, "L1a_kT": a["L1_attn_Wk"].T, "L1a_vT": a["L1_attn_Wv"].T,
        "L1a_oT": a["L1_attn_Wo"].T, "L1a_eqT": a["L1_attn_Weq"].T, "L1a_ekT": a["L1_attn_Wek"].T,
        "mix": mix.reshape(D, D), "mix_rolled": np.roll(mix, 1, axis=3).reshape(D, D),
        "amp_ph": np.concatenate([a["L1_attn_amp_w"], a["L1_attn_ph_w"], np.zeros((96, D), np.float32)]).T,
    }
    cols = {
        "L0x_bq": a["L0_xattn_bias_q"], "L0x_bk": a["L0_xattn_bias_k"],
        "gain": np.broadcast_to(a["L0_attn_gain"], (D,)),
        "mu_r": a["L0_ffn_mu_r"], "mu_k": a["L0_ffn_mu_k"],
        "L1x_bq": a["L1_xattn_bq"][order], "L1x_bk": a["L1_xattn_bk"][order],
        "L1a_bq": a["L1_attn_bq"], "L1a_bk": a["L1_attn_bk"], "L1a_bv": a["L1_attn_bv"],
        "L1a_beq": a["L1_attn_beq"], "L1a_bek": a["L1_attn_bek"],
    }
    rows = {
        "L0x_bv": a["L0_xattn_bias_v"], "L1x_bv": a["L1_xattn_bv"], "L1x_bo": a["L1_xattn_bo"],
        "L1a_bv": a["L1_attn_bv"], "L1a_bo": a["L1_attn_bo"], "L1a_ln_g": a["L1_attn_ln_g"],
        "L1a_ln_b": a["L1_attn_ln_b"], "mix_b": a["L1_attn_mix_b"].reshape(D),
        "mix_b_rolled": np.roll(a["L1_attn_mix_b"], 1, axis=1).reshape(D),
        "amp_ph_b": np.concatenate([a["L1_attn_amp_b"], a["L1_attn_ph_b"], np.zeros(96, np.float32)]),
    }
    expert_cols = np.concatenate([a["L1_ffn_ln_g"].T, a["L1_ffn_ln_b"].T,
                                  a["L1_ffn_b1"].reshape(NE * FT, 128).T], axis=1)
    i = np.arange(128)
    first = np.zeros((128, 128))
    first[:, 0:NE] = NE - np.arange(NE)
    consts = {
        "identity": np.eye(128),
        "off_block": np.where(i[:, None] // HD == i[None, :] // HD, 0.0, -1.0e30),
        "head_mask": i[:, None] // HD == i[None, :],
        "decay": 0.5 * np.exp(-0.1 * np.abs(i[:, None] - i[None, :])),
        "first_weight": first,
    }
    arrays = {
        "x": a["x"], "ctx": a["ctx_1024"], "ctx_t": a["ctx_1024"].transpose(0, 2, 1),
        "mask0": a["mask_1xSxS2_ff0"].reshape(S, KEYS), "mask1": a["mask_Bx1x1xS2_fk0"].reshape(128, 64),
        "mats": stacked([mats[n] for n in MATS], 1), "cols": stacked([cols[n] for n in COLS], 1),
        "expert_cols": expert_cols, "rows": stacked([rows[n] for n in ROWV], 0),
        "centroids_t": a["L1_ffn_centroids"].T, "b2": a["L1_ffn_b2"], "w1": a["L1_ffn_w1"], "w2": a["L1_ffn_w2"],
        "consts": stacked([consts[n] for n in CONSTS], 1).astype(np.float32),
    }
    nc = bacc.Bacc("TRN2", target_bir_lowering=False, num_devices=1)
    given, args = {}, []
    for name, v in arrays.items():
        v = np.ascontiguousarray(v)
        given["in_" + name] = v
        args.append(nc.dram_tensor("in_" + name, v.shape, mybir.dt.from_np(v.dtype), kind="ExternalInput").ap())
    args.append(nc.dram_tensor("out_0", (B, S, D), F32, kind="ExternalOutput").ap())
    build(nc, *args)
    r = run_bass_kernel_spmd(nc, [given], core_ids=[0])
    return r.results[0]["out_0"]
```
